# Optimizing a Trainium2 kernel written in Bass

```python
import numpy as np
import jax
import jax.numpy as jnp

def _softmax(x, axis=-1):
    return jax.nn.softmax(x, axis=axis)

def _gelu(x):
    return jax.nn.gelu(x, approximate=True)

def _silu(x):
    return jax.nn.silu(x)

def _sigmoid(x):
    return jax.nn.sigmoid(x)

def _layernorm(x, axis=-1, eps=1e-05):
    m = jnp.mean(x, axis=axis, keepdims=True)
    v = jnp.var(x, axis=axis, keepdims=True)
    return (x - m) / jnp.sqrt(v + eps)

def _scatter_add(tgt, idx, src, axis=0):
    return tgt.at[idx].add(src)

def _segment_sum(src, seg, n):
    return jax.ops.segment_sum(src, seg, n)
kernel_name = 'mk_hybrid_d1_jaxref_r8_8881cf'

def setup_inputs(seed: int=0):
    np.random.seed(seed)
    _w = jnp.asarray

    def _L0_attn_a_setup():
        import jax, jax.numpy as jnp
        import numpy as np
        B, N, DIM = (4, 128, 128)
        H, DH, ORDER = (16, 64, 3)
        MAXREL = 64
        INNER = H * DH
        VOCAB = 2 * MAXREL + 1
        SCALE = DH ** (-0.5)
        TOPK = int(0.25 * N)
        key = jax.random.key(seed)
        ks = jax.random.split(key, 8)
        s = 0.02
        return {'x': jax.random.normal(ks[0], (B, N, DIM), jnp.float32), 'Wqkv': jax.random.normal(ks[1], (3 * INNER, DIM), jnp.float32) * s, 'bqkv': jnp.zeros((3 * INNER,), jnp.float32), 'Wout': jax.random.normal(ks[2], (DIM, INNER), jnp.float32) * s, 'bout': jnp.zeros((DIM,), jnp.float32), 'rel_k_emb': jax.random.normal(ks[3], (VOCAB, DH), jnp.float32) * s, 'rel_v_emb': jax.random.normal(ks[4], (VOCAB, DH), jnp.float32) * s, 'alphas_raw': jax.random.normal(ks[5], (ORDER, H), jnp.float32) * 0.5}
    _L0_attn_a_in = _L0_attn_a_setup()

    def _L0_attn_b_setup():
        import jax, jax.numpy as jnp
        import numpy as np
        import math
        D_MODEL = 128
        EXPAND = 2
        D_INNER = EXPAND * D_MODEL
        HEADDIM = 16
        NHEADS = D_INNER // (HEADDIM * 2)
        D_STATE = 16
        NGROUPS = 1
        D_CONV = 4
        CHUNK = 32
        D_IN_PROJ = D_INNER + 2 * NGROUPS * D_STATE + NHEADS
        CONV_DIM = D_INNER // 2 + 2 * NGROUPS * D_STATE

        def _segsum(x):
            T = x.shape[-1]
            cs = jnp.cumsum(x, axis=-1)
            seg = cs[..., :, None] - cs[..., None, :]
            mask = jnp.tril(jnp.ones((T, T), dtype=bool))
            return jnp.where(mask, seg, -jnp.inf)

        def _ssd(X, Adt, B, C, chunk):
            b, l, h, p = X.shape
            c = l // chunk
            n = B.shape[-1]
            X = X.reshape(b, c, chunk, h, p)
            A = Adt.reshape(b, c, chunk, h).transpose(0, 3, 1, 2)
            B = B.reshape(b, c, chunk, n)
            C = C.reshape(b, c, chunk, n)
            A_cs = jnp.cumsum(A, axis=-1)
            Lmat = jnp.exp(_segsum(A))
            Y_diag = jnp.einsum('bcln,bcsn,bhcls,bcshp->bclhp', C, B, Lmat, X)
            decay_states = jnp.exp(A_cs[..., -1:] - A_cs)
            states = jnp.einsum('bcln,bhcl,bclhp->bchpn', B, decay_states, X)
            init = jnp.zeros_like(states[:, :1])
            states_cat = jnp.concatenate([init, states], axis=1)
            A_last = jnp.pad(A_cs[..., -1], ((0, 0), (0, 0), (1, 0)))
            decay_chunk = jnp.exp(_segsum(A_last))
            new_states = jnp.einsum('bhzc,bchpn->bzhpn', decay_chunk, states_cat)
            states_in = new_states[:, :-1]
            out_decay = jnp.exp(A_cs)
            Y_off = jnp.einsum('bcln,bchpn,bhcl->bclhp', C, states_in, out_decay)
            return (Y_diag + Y_off).reshape(b, l, h, p)

        def _forward(u, W_in, conv_w, conv_b, dt_bias, A_log, Dskip, ln_w, ln_b, W_out):
            b, l, _ = u.shape
            zxbcdt = jnp.einsum('bld,ed->ble', u, W_in)
            half = D_INNER // 2
            z = zxbcdt[..., :half]
            xBC = zxbcdt[..., half:half + CONV_DIM]
            dt = zxbcdt[..., half + CONV_DIM:]
            dt = jax.nn.softplus(dt + dt_bias)
            xBC_ncl = xBC.transpose(0, 2, 1)
            xBC_ncl = jax.lax.conv_general_dilated(xBC_ncl, conv_w, window_strides=(1,), padding=[(D_CONV - 1, 0)], feature_group_count=CONV_DIM, dimension_numbers=('NCH', 'OIH', 'NCH'))
            xBC = jax.nn.silu(xBC_ncl.transpose(0, 2, 1) + conv_b)
            x = xBC[..., :half]
            Bm = xBC[..., half:half + NGROUPS * D_STATE]
            Cm = xBC[..., half + NGROUPS * D_STATE:]
            A = -jnp.exp(A_log)
            xh = x.reshape(b, l, NHEADS, HEADDIM)
            y = _ssd(xh * dt[..., None], A * dt, Bm, Cm, CHUNK)
            y = y + xh * Dskip[None, None, :, None]
            y = y.reshape(b, l, half)
            y = jnp.concatenate([y, z], axis=-1)
            mu = jnp.mean(y, axis=-1, keepdims=True)
            var = jnp.mean((y - mu) ** 2, axis=-1, keepdims=True)
            y = (y - mu) / jnp.sqrt(var + 1e-05) * ln_w + ln_b
            return jnp.einsum('ble,de->bld', y, W_out)
        key = jax.random.key(seed)
        ks = jax.random.split(key, 10)
        u = jax.random.normal(ks[0], (2, 256, D_MODEL), dtype=jnp.float32)
        W_in = jax.random.normal(ks[1], (D_IN_PROJ, D_MODEL), dtype=jnp.float32) / math.sqrt(D_MODEL)
        conv_w = jax.random.normal(ks[2], (CONV_DIM, 1, D_CONV), dtype=jnp.float32) / math.sqrt(D_CONV)
        conv_b = jnp.zeros((CONV_DIM,), dtype=jnp.float32)
        dt = jnp.exp(jax.random.uniform(ks[3], (NHEADS,)) * (math.log(0.1) - math.log(0.001)) + math.log(0.001))
        dt = jnp.clip(dt, 0.0001, None)
        dt_bias = (dt + jnp.log(-jnp.expm1(-dt))).astype(jnp.float32)
        A_log = jnp.log(jax.random.uniform(ks[4], (NHEADS,), minval=1.0, maxval=16.0)).astype(jnp.float32)
        Dskip = jnp.ones((NHEADS,), dtype=jnp.float32)
        ln_w = jnp.ones((D_INNER,), dtype=jnp.float32)
        ln_b = jnp.zeros((D_INNER,), dtype=jnp.float32)
        W_out = jax.random.normal(ks[5], (D_MODEL, D_INNER), dtype=jnp.float32) / math.sqrt(D_INNER)
        return {'u': u, 'W_in': W_in, 'conv_w': conv_w, 'conv_b': conv_b, 'dt_bias': dt_bias, 'A_log': A_log, 'Dskip': Dskip, 'ln_w': ln_w, 'ln_b': ln_b, 'W_out': W_out}
    _L0_attn_b_in = _L0_attn_b_setup()

    def _L0_ffn_setup():
        import jax, jax.numpy as jnp
        import numpy as np
        H = 128
        E = 8
        B, S = (4, 256)
        key = jax.random.key(seed)
        k1, k2, k3, k4 = jax.random.split(key, 4)
        x = jax.random.normal(k1, (B, S, H), dtype=jnp.float32)
        wg = jax.random.normal(k2, (H, E), dtype=jnp.float32) * 0.02
        W = jax.random.normal(k3, (E, H, H), dtype=jnp.float32) * 0.02
        b = jax.random.normal(k4, (E, H), dtype=jnp.float32) * 0.02
        return {'x': x, 'wg': wg, 'W': W, 'b': b}
    _L0_ffn_in = _L0_ffn_setup()
    _d = {'L0_attn_a_x': _L0_attn_a_in['x'], 'L0_attn_a_Wqkv': _L0_attn_a_in['Wqkv'], 'L0_attn_a_bqkv': _L0_attn_a_in['bqkv'], 'L0_attn_a_Wout': _L0_attn_a_in['Wout'], 'L0_attn_a_bout': _L0_attn_a_in['bout'], 'L0_attn_a_rel_k_emb': _L0_attn_a_in['rel_k_emb'], 'L0_attn_a_rel_v_emb': _L0_attn_a_in['rel_v_emb'], 'L0_attn_a_alphas_raw': _L0_attn_a_in['alphas_raw'], 'L0_attn_b_W_in': _L0_attn_b_in['W_in'], 'L0_attn_b_conv_w': _L0_attn_b_in['conv_w'], 'L0_attn_b_conv_b': _L0_attn_b_in['conv_b'], 'L0_attn_b_dt_bias': _L0_attn_b_in['dt_bias'], 'L0_attn_b_A_log': _L0_attn_b_in['A_log'], 'L0_attn_b_Dskip': _L0_attn_b_in['Dskip'], 'L0_attn_b_ln_w': _L0_attn_b_in['ln_w'], 'L0_attn_b_ln_b': _L0_attn_b_in['ln_b'], 'L0_attn_b_W_out': _L0_attn_b_in['W_out'], 'L0_ffn_wg': _L0_ffn_in['wg'], 'L0_ffn_W': _L0_ffn_in['W'], 'L0_ffn_b': _L0_ffn_in['b']}
    _x0 = _d['L0_attn_a_x']
    _d['L0_attn_a_x'] = jax.random.normal(jax.random.fold_in(jax.random.key(seed), 1), (8, 512, 128), dtype=_x0.dtype)
    del _x0
    return _d

def reference(L0_attn_a_x, L0_attn_a_Wqkv, L0_attn_a_bqkv, L0_attn_a_Wout, L0_attn_a_bout, L0_attn_a_rel_k_emb, L0_attn_a_rel_v_emb, L0_attn_a_alphas_raw, L0_attn_b_W_in, L0_attn_b_conv_w, L0_attn_b_conv_b, L0_attn_b_dt_bias, L0_attn_b_A_log, L0_attn_b_Dskip, L0_attn_b_ln_w, L0_attn_b_ln_b, L0_attn_b_W_out, L0_ffn_wg, L0_ffn_W, L0_ffn_b):

    def _L0_attn_a_ref(x, Wqkv, bqkv, Wout, bout, rel_k_emb, rel_v_emb, alphas_raw):
        import jax, jax.numpy as jnp
        import numpy as np
        B, N, DIM = (4, 128, 128)
        H, DH, ORDER = (16, 64, 3)
        MAXREL = 64
        INNER = H * DH
        VOCAB = 2 * MAXREL + 1
        SCALE = DH ** (-0.5)
        TOPK = int(0.25 * N)
        b, n, _ = x.shape
        qkv = x @ Wqkv.T + bqkv
        q, k, v = jnp.split(qkv, 3, axis=-1)
        to_heads = lambda t: t.reshape(b, n, H, DH).transpose(0, 2, 1, 3)
        q, k, v = (to_heads(q), to_heads(k), to_heads(v))
        scores = jnp.einsum('bhid,bhjd->bhij', q, k) * SCALE
        coords = jnp.arange(n)
        dist = jnp.clip(coords[:, None] - coords[None, :], -MAXREL, MAXREL) + MAXREL
        rel_k = rel_k_emb[dist]
        scores = scores + jnp.einsum('bhid,ijd->bhij', q, rel_k)
        top_vals = jax.lax.top_k(scores, TOPK)[0]
        threshold = top_vals[..., -1:]
        scores = jnp.where(scores < threshold, -jnp.inf, scores)
        attn = jax.nn.softmax(scores, axis=-1)
        rel_v = rel_v_emb[dist]
        alphas = jax.nn.sigmoid(alphas_raw)
        res = jnp.zeros_like(v)
        v_curr = v
        for i in range(ORDER):
            a_v = jnp.einsum('bhij,bhjd->bhid', attn, v_curr)
            if i == 0:
                a_v = a_v + jnp.einsum('bhij,ijd->bhid', attn, rel_v)
            v_curr = a_v
            res = res + alphas[i][None, :, None, None] * v_curr
        out = res.transpose(0, 2, 1, 3).reshape(b, n, INNER)
        return out @ Wout.T + bout

    def _L0_attn_b_ref(u, W_in, conv_w, conv_b, dt_bias, A_log, Dskip, ln_w, ln_b, W_out):
        import jax, jax.numpy as jnp
        import numpy as np
        import math
        D_MODEL = 128
        EXPAND = 2
        D_INNER = EXPAND * D_MODEL
        HEADDIM = 16
        NHEADS = D_INNER // (HEADDIM * 2)
        D_STATE = 16
        NGROUPS = 1
        D_CONV = 4
        CHUNK = 32
        D_IN_PROJ = D_INNER + 2 * NGROUPS * D_STATE + NHEADS
        CONV_DIM = D_INNER // 2 + 2 * NGROUPS * D_STATE

        def _segsum(x):
            T = x.shape[-1]
            cs = jnp.cumsum(x, axis=-1)
            seg = cs[..., :, None] - cs[..., None, :]
            mask = jnp.tril(jnp.ones((T, T), dtype=bool))
            return jnp.where(mask, seg, -jnp.inf)

        def _ssd(X, Adt, B, C, chunk):
            b, l, h, p = X.shape
            c = l // chunk
            n = B.shape[-1]
            X = X.reshape(b, c, chunk, h, p)
            A = Adt.reshape(b, c, chunk, h).transpose(0, 3, 1, 2)
            B = B.reshape(b, c, chunk, n)
            C = C.reshape(b, c, chunk, n)
            A_cs = jnp.cumsum(A, axis=-1)
            Lmat = jnp.exp(_segsum(A))
            Y_diag = jnp.einsum('bcln,bcsn,bhcls,bcshp->bclhp', C, B, Lmat, X)
            decay_states = jnp.exp(A_cs[..., -1:] - A_cs)
            states = jnp.einsum('bcln,bhcl,bclhp->bchpn', B, decay_states, X)
            init = jnp.zeros_like(states[:, :1])
            states_cat = jnp.concatenate([init, states], axis=1)
            A_last = jnp.pad(A_cs[..., -1], ((0, 0), (0, 0), (1, 0)))
            decay_chunk = jnp.exp(_segsum(A_last))
            new_states = jnp.einsum('bhzc,bchpn->bzhpn', decay_chunk, states_cat)
            states_in = new_states[:, :-1]
            out_decay = jnp.exp(A_cs)
            Y_off = jnp.einsum('bcln,bchpn,bhcl->bclhp', C, states_in, out_decay)
            return (Y_diag + Y_off).reshape(b, l, h, p)

        def _forward(u, W_in, conv_w, conv_b, dt_bias, A_log, Dskip, ln_w, ln_b, W_out):
            b, l, _ = u.shape
            zxbcdt = jnp.einsum('bld,ed->ble', u, W_in)
            half = D_INNER // 2
            z = zxbcdt[..., :half]
            xBC = zxbcdt[..., half:half + CONV_DIM]
            dt = zxbcdt[..., half + CONV_DIM:]
            dt = jax.nn.softplus(dt + dt_bias)
            xBC_ncl = xBC.transpose(0, 2, 1)
            xBC_ncl = jax.lax.conv_general_dilated(xBC_ncl, conv_w, window_strides=(1,), padding=[(D_CONV - 1, 0)], feature_group_count=CONV_DIM, dimension_numbers=('NCH', 'OIH', 'NCH'))
            xBC = jax.nn.silu(xBC_ncl.transpose(0, 2, 1) + conv_b)
            x = xBC[..., :half]
            Bm = xBC[..., half:half + NGROUPS * D_STATE]
            Cm = xBC[..., half + NGROUPS * D_STATE:]
            A = -jnp.exp(A_log)
            xh = x.reshape(b, l, NHEADS, HEADDIM)
            y = _ssd(xh * dt[..., None], A * dt, Bm, Cm, CHUNK)
            y = y + xh * Dskip[None, None, :, None]
            y = y.reshape(b, l, half)
            y = jnp.concatenate([y, z], axis=-1)
            mu = jnp.mean(y, axis=-1, keepdims=True)
            var = jnp.mean((y - mu) ** 2, axis=-1, keepdims=True)
            y = (y - mu) / jnp.sqrt(var + 1e-05) * ln_w + ln_b
            return jnp.einsum('ble,de->bld', y, W_out)
        return _forward(u, W_in, conv_w, conv_b, dt_bias, A_log, Dskip, ln_w, ln_b, W_out)

    def _L0_ffn_ref(x, wg, W, b):
        import jax, jax.numpy as jnp
        import numpy as np
        H = 128
        E = 8
        B, S = (4, 256)
        Bb, Ss, Hh = x.shape
        Ee = wg.shape[1]
        T = Bb * Ss
        C = T // Ee
        xt = x.reshape(T, Hh)
        logits = xt @ wg
        probs = jax.nn.softmax(logits, axis=-1)
        idx = jnp.argmax(probs, axis=-1)
        mask = jax.nn.one_hot(idx, Ee, dtype=xt.dtype)
        locations = jnp.cumsum(mask, axis=0) - mask
        mask = mask * (locations < C).astype(xt.dtype)
        gate = jnp.sum(probs * mask, axis=-1)
        loc_s = jnp.sum(locations * mask, axis=-1).astype(jnp.int32)
        loc_oh = jax.nn.one_hot(loc_s, C, dtype=xt.dtype)
        dispatch = mask[:, :, None] * loc_oh[:, None, :]
        combine = gate[:, None, None] * dispatch
        exp_in = jnp.einsum('tec,th->ech', dispatch, xt)
        exp_out = jnp.einsum('ech,efh->ecf', exp_in, W) + b[:, None, :]
        out = jnp.einsum('tec,ecf->tf', combine, exp_out)
        return out.reshape(Bb, Ss, Hh)
    x = L0_attn_a_x
    x = x + _L0_attn_a_ref(_layernorm(x, axis=-1), L0_attn_a_Wqkv, L0_attn_a_bqkv, L0_attn_a_Wout, L0_attn_a_bout, L0_attn_a_rel_k_emb, L0_attn_a_rel_v_emb, L0_attn_a_alphas_raw)
    x = x + _L0_ffn_ref(_layernorm(x, axis=-1), L0_ffn_wg, L0_ffn_W, L0_ffn_b)
    x = x + _L0_attn_b_ref(_layernorm(x, axis=-1), L0_attn_b_W_in, L0_attn_b_conv_w, L0_attn_b_conv_b, L0_attn_b_dt_bias, L0_attn_b_A_log, L0_attn_b_Dskip, L0_attn_b_ln_w, L0_attn_b_ln_b, L0_attn_b_W_out)
    x = x + _L0_ffn_ref(_layernorm(x, axis=-1), L0_ffn_wg, L0_ffn_W, L0_ffn_b)
    return x

_drawn_inputs = setup_inputs


def setup_inputs(seed=0):
    import zlib

    import numpy as np

    out = dict(_drawn_inputs(seed))
    spreads = {'L0_attn_a_bqkv': (0.0, 0.1),
     'L0_attn_a_bout': (0.0, 0.1),
     'L0_attn_b_conv_b': (0.0, 0.1),
     'L0_attn_b_Dskip': (1.0, 0.2),
     'L0_attn_b_ln_w': (1.0, 0.2),
     'L0_attn_b_ln_b': (0.0, 0.1)}
    factors = {'L0_attn_a_rel_k_emb': 4.718,
     'L0_attn_a_rel_v_emb': 4.523,
     'L0_attn_a_alphas_raw': 2.951,
     'L0_ffn_b': 8.0}
    for name, (base, spread) in spreads.items():
        noise = np.random.default_rng([zlib.crc32(name.encode()), seed]).standard_normal(out[name].shape)
        drawn = base * np.exp(spread * noise) if base else spread * noise
        out[name] = jnp.asarray(drawn.astype(out[name].dtype))
    for name, factor in factors.items():
        out[name] = (out[name] * factor).astype(out[name].dtype)
    return out
```

```python
from contextlib import ExitStack

import concourse.bass as bass
import concourse.mybir as mybir
from concourse.alu_op_type import AluOpType as ALU

F32 = mybir.dt.float32
ACT = mybir.ActivationFunctionType
AX = mybir.AxisListType

P = 128
B, N, D = 8, 512, 128
NT = N // P
TILES = B * NT
EPS = 1e-5

H, DH, ORDER = 16, 64, 3
PAIRS = H // 2
ITS = B * PAIRS
MAXREL = 64
TOPK = N // 4 // 4
SCALE = DH ** -0.5
HALF = MAXREL
RECT = P + 2 * HALF
EXT = RECT + P - 1
PADDED = N + 2 * HALF
NEG = -3.0e38

J_WQ, J_WK, J_WV, J_BV, J_BQ, J_BK = 0, 128, 256, 384, 512, 513
J_COLS = 514
O_W, O_AL = 0, 128
O_COLS = O_AL + 2 * ORDER


class Namespace:
    pass


def rect_of(T):
    lo, hi = max(0, P * T - HALF), min(N, P * T + P + HALF)
    return lo, hi, lo - (P * T - HALF)


def bcast(ap, dims):
    return bass.AP(ap.tensor, ap.offset, [list(ap.ap[0])] + [list(d) for d in dims])



def two_at_a_time(eng, count, body, with_half=False):
    for k in range(2):
        body(k, k, True, *([0] if with_half else []))
    with eng.Fori(1, count // 2) as g:
        for k in range(2):
            body(g * 2 + k, k, False, *([g] if with_half else []))


GROUPS = TILES // 4


def norm_sems(sem, tag):
    s = Namespace()
    s.stats, s.chain, s.var, s.rstd = (sem(f"{tag}_{n}") for n in ("stats", "chain", "var", "rstd"))
    s.scaled, s.transposed, s.stored = (sem(f"{tag}_{n}") for n in ("scaled", "transposed", "stored"))
    return s


def norm_buffers(sb, tag):
    w = Namespace()
    w.stats = sb(f"{tag}_stats", [P, TILES * 6])
    w.mean2 = sb(f"{tag}_mean2", [P, TILES])
    w.diff = sb(f"{tag}_diff", [P, TILES])
    w.diff2 = sb(f"{tag}_diff2", [P, TILES])
    w.var2 = sb(f"{tag}_var2", [P, TILES])
    w.mean = sb(f"{tag}_mean", [P, TILES])
    w.var = sb(f"{tag}_var", [P, TILES])
    w.vareps = sb(f"{tag}_vareps", [P, TILES])
    w.rstd = sb(f"{tag}_rstd", [P, TILES])
    w.mhalf = sb(f"{tag}_mhalf", [P, TILES])
    w.xn = sb(f"{tag}_xn", [P, 2, 4 * D])
    return w


def norm_vector(nc, dve, s, w, X):
    nc.vector.memset(w.mhalf[:, :], -0.5)
    with dve.Fori(0, TILES) as t:
        nc.vector.bn_stats(w.stats[:, bass.ds(t * 6, 6)], X[:, bass.ds(t * D, D)]).then_inc(s.stats, 1)
    dve.wait_ge(s.stats, TILES)
    st = w.stats[:, :].rearrange("p (t s) -> p t s", s=6)
    nc.vector.tensor_tensor(w.mean2[:, :], st[:, :, 1], st[:, :, 4], ALU.add)
    nc.vector.tensor_tensor(w.diff[:, :], st[:, :, 1], st[:, :, 4], ALU.subtract)
    nc.vector.tensor_tensor(w.var2[:, :], st[:, :, 2], st[:, :, 5], ALU.add).then_inc(s.chain, 1)
    dve.wait_ge(s.chain, 1)
    nc.vector.tensor_tensor(w.diff2[:, :], w.diff[:, :], w.diff[:, :], ALU.mult)
    nc.vector.tensor_scalar(w.mean[:, :], w.mean2[:, :], 0.5, None, ALU.mult)
    nc.vector.tensor_scalar(w.var[:, :], w.var2[:, :], 1.0 / D, EPS, ALU.mult, ALU.add).then_inc(s.chain, 1)
    dve.wait_ge(s.chain, 2)
    nc.vector.scalar_tensor_tensor(out=w.vareps[:, :], in0=w.diff2[:, :], scalar=0.25, in1=w.var[:, :],
                                   op0=ALU.mult, op1=ALU.add).then_inc(s.var, 1)
    dve.wait_ge(s.rstd, 1)

    def scale(i, par, first):
        if not first:
            dve.wait_ge(s.transposed, i - 1)
        for k in range(4):
            last = nc.vector.tensor_scalar(w.xn[:, par, k * D:(k + 1) * D],
                                           X[:, bass.ds((i * 4 + k) * D, D)],
                                           w.mean[:, bass.ds(i * 4 + k, 1)], w.rstd[:, bass.ds(i * 4 + k, 1)],
                                           ALU.subtract, ALU.mult)
        last.then_inc(s.scaled, 1)

    two_at_a_time(dve, GROUPS, scale)


def norm_gpsimd(nc, pool, s, w):
    pool.wait_ge(s.var, 1)
    nc.gpsimd.tensor_tensor(w.rstd[:, :], w.vareps[:, :], w.mhalf[:, :], ALU.pow).then_inc(s.rstd, 1)


def norm_tensor(nc, pe, s, w, banks, ident):
    def transpose(i, par, first):
        pe.wait_ge(s.scaled, i + 1)
        if not first:
            pe.wait_ge(s.stored, i - 1)
        for k in range(4):
            last = nc.tensor.transpose(banks[par][:, k * P:(k + 1) * P], w.xn[:, par, k * D:(k + 1) * D],
                                       ident[:, :])
        last.then_inc(s.transposed, 1)

    two_at_a_time(pe, GROUPS, transpose)


def norm_scalar(nc, act, s, banks, XNT):
    def store(i, par, first):
        act.wait_ge(s.transposed, i + 1)
        nc.scalar.activation(XNT[:, bass.ds(i * 4 * P, 4 * P)], banks[par][:, :], ACT.Copy).then_inc(s.stored, 1)

    two_at_a_time(act, GROUPS, store)


def set_up(nc, sem, sb, ps, a, k, t):
    x_in, w_in, consts, turned, kept, chain = (sem(f"setup_{n}") for n in
                                               ("x_in", "w_in", "consts", "turned", "kept", "chain"))
    wqkv = sb("wqkv_rows", [P, 24, D])
    wout = sb("wout_rows", [P, H * DH])
    relk = sb("relk_rows", [P, 2 * DH])
    relk0 = sb("relk0_col", [P, 1])
    relv = sb("relv_rows", [P, DH])
    relv0 = sb("relv0_all", [P, DH])
    bqk = sb("bqk_rows", [16, P])
    bv = sb("bv_all", [P, H * DH])
    al = sb("alphas_all", [P, ORDER * H])
    al1 = sb("alphas_e", [P, ORDER * H])
    al2 = sb("alphas_d", [P, ORDER * H])
    relv_turned = sb("relv_turned", [P, DH])
    anti = sb("anti_identity", [P, P])
    zeros = k.zeros
    LOADS = 12

    with nc.Block() as block:
        @block.sync
        def _(sp):
            xv = a["x"].rearrange("b (t p) d -> p (b t) d", p=P)
            Xv = k.X[:, :].rearrange("p (t d) -> p t d", d=D)
            for q in range(4):
                sp.dma_start(Xv[:, q * 8:(q + 1) * 8, :], xv[:, q * 8:(q + 1) * 8, :]).then_inc(x_in, 16)
            sp.wait_ge(consts, 1)
            for q in range(2):
                rows = bass.AP(t.p_dram[q], P + RECT, [[2 * PITCH, P], [PITCH, 2], [1, P]])
                sp.dma_start(rows, zeros[:, 0:2 * P].rearrange("p (h c) -> p h c", h=2)).then_inc(x_in, 16)
                sp.dma_start(bass.AP(t.p_dram[q], 0, [[P, 1], [1, P]]), zeros[0:1, 0:P]).then_inc(x_in, 16)
            sp.wait_ge(x_in, 16 * 8)

        @block.gpsimd
        def _(pool):
            nc.gpsimd.memset(zeros[:, :], 0.0).then_inc(consts, 1)
            nc.gpsimd.memset(k.ident[:, :], 0.0)
            nc.gpsimd.memset(anti[:, :], 0.0).then_inc(consts, 1)
            pool.wait_ge(consts, 2)
            nc.gpsimd.affine_select(out=k.ident[:, :], in_=k.ident[:, :], compare_op=ALU.not_equal, fill=1.0,
                                    base=0, pattern=[[-1, P]], channel_multiplier=1)
            nc.gpsimd.affine_select(out=anti[:, :], in_=anti[:, :], compare_op=ALU.not_equal, fill=1.0,
                                    base=-(P - 1), pattern=[[1, P]], channel_multiplier=1).then_inc(consts, 1)

        @block.scalar
        def _(act):
            act.dma_start(wqkv[:, :, :], a["Wqkv"].rearrange("(c p) d -> p c d", p=P)).then_inc(w_in, 16)
            act.dma_start(wout[:, :], a["Wout"]).then_inc(w_in, 16)
            for s in range(2):
                act.dma_start(relk[:, s * DH:(s + 1) * DH], a["rel_k_emb"][1:2 * MAXREL + 1, :]).then_inc(w_in, 16)
                with nc.allow_non_contiguous_dma(reason="64 values, once"):
                    act.dma_start(relk0[s * DH:(s + 1) * DH, :],
                                  a["rel_k_emb"][0:1, :].rearrange("o d -> d o")).then_inc(w_in, 16)
            act.dma_start(relv[:, :], a["rel_v_emb"][1:2 * MAXREL + 1, :]).then_inc(w_in, 16)
            act.dma_start(relv0[:, :], a["rel_v_emb"][0:1, :].to_broadcast([P, DH])).then_inc(w_in, 16)
            act.dma_start(bqk[:, :], a["bqkv"][0:2 * H * DH].rearrange("(c p) -> c p", p=P)).then_inc(w_in, 16)
            act.dma_start(bv[:, :], a["bqkv"][2 * H * DH:].rearrange("(o n) -> o n", o=1)
                          .to_broadcast([P, H * DH])).then_inc(w_in, 16)
            act.dma_start(al[:, :], a["alphas_raw"].rearrange("(o k) h -> o (k h)", o=1)
                          .to_broadcast([P, ORDER * H])).then_inc(w_in, 16)
            act.dma_start(k.bout[:, :], a["bout"].rearrange("(o n) -> o n", o=1).to_broadcast([P, D])).then_inc(w_in, 16)
            act.wait_ge(w_in, 16 * LOADS)
            nc.scalar.activation(al1[:, :], al[:, :], ACT.Exp, scale=-1.0).then_inc(chain, 1)
            for g in range(8):
                act.wait_ge(turned, g + 1)
                which, half = divmod(g, 2)
                if which < 3:
                    to = t.TJ[:, 4 * half:4 * half + 4, which * P:(which + 1) * P]
                else:
                    to = t.TO[:, 4 * half:4 * half + 4, 0:P]
                nc.scalar.activation(to, ps[g % 4][:, :].rearrange("p (c n) -> p c n", c=4), ACT.Copy).then_inc(kept, 1)

        @block.tensor
        def _(pe):
            pe.wait_ge(consts, 3)
            pe.wait_ge(w_in, 16 * LOADS)
            for g in range(8):
                if g >= 4:
                    pe.wait_ge(kept, g - 3)
                for c in range(4):
                    src = wqkv[:, g * 4 + c, :] if g < 6 else wout[:, ((g - 6) * 4 + c) * P:((g - 6) * 4 + c + 1) * P]
                    last = nc.tensor.transpose(ps[g % 4][:, c * P:(c + 1) * P], src, k.ident[:, :])
                last.then_inc(turned, 1)
            nc.tensor.transpose(ps[4][:, 0:16], bqk[:, :], k.ident[0:16, 0:16])
            nc.tensor.transpose(ps[5][:, 0:P], relk[:, :], anti[:, :])
            nc.tensor.matmul(ps[6][:, 0:DH], anti[:, :], relv[:, :], start=True, stop=True).then_inc(turned, 1)

        @block.vector
        def _(dve):
            for T in range(NT):
                nc.vector.memset(t.prob[T][:, :, 0:HALF], 0.0)
                nc.vector.memset(t.prob[T][:, :, HALF + N:PADDED], 0.0)
            for par in range(2):
                nc.vector.memset(t.kz[par][0][DH:P, :], 0.0)
                nc.vector.memset(t.kz[par][1][0:DH, :], 0.0)
            nc.vector.memset(t.relk[0][DH:P, :], 0.0)
            nc.vector.memset(t.relk[1][0:DH, :], 0.0)
            dve.wait_ge(w_in, 16 * LOADS)
            dve.wait_ge(chain, 1)
            nc.vector.tensor_scalar(al2[:, :], al1[:, :], 1.0, None, ALU.add).then_inc(chain, 1)
            dve.wait_ge(chain, 2)
            nc.vector.reciprocal(al[:, :], al2[:, :]).then_inc(chain, 1)
            dve.wait_ge(chain, 3)
            nc.vector.tensor_copy(t.TO[:, :, O_AL:O_AL + 2 * ORDER].rearrange("p r (k s) -> p r k s", k=ORDER),
                                  al[:, :].rearrange("p (k r s) -> p r k s", k=ORDER, s=2))
            nc.vector.tensor_tensor(t.TJ[:, :, J_BV:J_BV + P].rearrange("p r (s d) -> p r s d", s=2),
                                    bv[:, :].rearrange("p (r s d) -> p r s d", s=2, d=DH),
                                    bcast(relv0[:, :], [[0, PAIRS], [0, 2], [1, DH]]), ALU.add)
            dve.wait_ge(turned, 9)
            nc.vector.tensor_copy(t.TJ[:, :, J_BQ:J_BQ + 1].rearrange("p r o -> p (r o)"), ps[4][:, 0:PAIRS])
            nc.vector.tensor_scalar(t.TJ[:, :, J_BK:J_BK + 1].rearrange("p r o -> p (r o)"), ps[4][:, PAIRS:2 * PAIRS],
                                    SCALE, None, ALU.mult)
            for s in range(2):
                r = slice(s * DH, (s + 1) * DH)
                nc.vector.tensor_copy(t.relk[s][r, 0:P - 1], bcast(ps[5][r, 0:1], [[0, P - 1]]))
                nc.vector.tensor_copy(t.relk[s][r, P - 1:2 * P - 1], ps[5][r, 0:P])
                nc.vector.tensor_copy(t.relk[s][r, 2 * P - 1:EXT], bcast(relk0[r, 0:1], [[0, EXT - 2 * P + 1]]))
            nc.vector.tensor_copy(relv_turned[:, :], ps[6][:, 0:DH]).then_inc(chain, 1)
            dve.wait_ge(chain, 4)
            nc.vector.tensor_tensor(t.relv[:, :], relv_turned[:, :], relv0[:, :], ALU.subtract)


PITCH = RECT + P


class Slots:

    def __init__(self, g, par, T):
        self.g, self.par, self.i, self.T = g, par, g * 2 + par, T

    def half(self, d):
        return self.g + (self.par + d) // 2

    def back(self, slots):
        q, T = divmod(self.T - slots, NT)
        it = self.i + q
        if isinstance(it, int) and not 0 <= it < ITS:
            return None
        return it, T, it * NT + T

    def iteration(self, d):
        it = self.i + d
        if isinstance(it, int) and not 0 <= it < ITS:
            return None
        return it


def early(value):
    return isinstance(value, int) and value <= 0


def known(eng, *values):
    for value in values:
        if not isinstance(value, int):
            eng.compute_val(value)
    return values


def run_iterations(eng, body):
    first, last = 4, ITS - 2
    for i in range(-1, first):
        for T in range(NT):
            body(Slots(i // 2, i % 2, T), i % 2)
    with eng.Fori(first // 2, last // 2) as g:
        for par in range(2):
            for T in range(NT):
                body(Slots(g, par, T), par)
    for i in range(last, ITS + 3):
        for T in range(NT):
            body(Slots(i // 2, i % 2, T), i % 2)


def attention(nc, sem, sb, ps, k, t):
    s = Namespace()
    s.q_made = sem("att_q_made")
    s.k_made = sem("att_k_made")
    s.v_made = sem("att_v_made")
    s.q_kept = sem("att_q_kept")
    s.k_kept = sem("att_k_kept")
    s.v_kept = sem("att_v_kept")
    s.v_ready = sem("att_v_ready")
    s.rel_made = sem("att_rel_made")
    s.rel_kept = sem("att_rel_kept")
    s.scores_made = sem("att_scores_made")
    s.scores_kept = sem("att_scores_kept")
    s.tops = sem("att_tops")
    s.maxes = sem("att_maxes")
    s.exps = sem("att_exps")
    s.probs = sem("att_probs")
    s.probs_turned = sem("att_probs_turned")
    s.probs_kept = sem("att_probs_kept")
    s.sums = sem("att_sums")
    s.band_closed = sem("att_band_closed")
    s.band_turned = sem("att_band_turned")
    s.band_kept = sem("att_band_kept")
    s.mixed = sem("att_mixed")
    s.mixed_kept = sem("att_mixed_kept")
    s.mixed_turned = sem("att_mixed_turned")
    s.raw_kept = sem("att_raw_kept")
    s.inverse = sem("att_inverse")
    s.values_next = sem("att_values_next")
    s.res_chain = sem("att_res_chain")
    s.res_turned = sem("att_res_turned")
    s.res_kept = sem("att_res_kept")
    s.out_made = sem("att_out_made")
    s.out_added = sem("att_out_added")
    s.next_tops = sem("att_next_tops")
    s.shortened = sem("att_shortened")
    s.bias_added = sem("att_bias_added")
    s.pj_in = [sem(f"att_pj_in{q}") for q in range(2)]
    s.po_in = [sem(f"att_po_in{q}") for q in range(2)]
    s.rel_stored = [sem(f"att_rel_stored{q}") for q in range(2)]
    s.rel_in = [sem(f"att_rel_in{q}") for q in range(2)]
    s.probs_stored = [sem(f"att_probs_stored{q}") for q in range(2)]
    s.band_in = [sem(f"att_band_in{q}") for q in range(2)]

    def two(name, shape):
        return [sb(f"{name}{q}", shape) for q in range(2)]

    pj = two("pair_j", [P, J_COLS])
    po = two("pair_o", [P, O_COLS])
    xt = two("xt", [P, N])
    qt = two("qt", [P, N])
    v = two("v", [P, NT, P])
    vraw = sb("vraw", [P, NT, P])
    rel = two("rel", [P, 2, EXT])
    relj = two("relj", [P, 2, RECT])
    sc = two("scores", [P, 2, N])
    work = sb("work", [P, 2, N])
    top = two("top", [P, 2, TOPK])
    nmax = two("nmax", [P, 2])
    ex = two("exps", [P, 2, N])
    rs = two("row_sums", [P, 2 * NT])
    inv = two("inverse", [P, 2 * NT])
    band = two("band", [P, 2, RECT])
    la = two("left_a", [P, 2])
    lb = two("left_b", [P, 2])
    pt = two("probs_t", [P, 2, NT, N])
    bt = two("band_t", [P, 2, N])
    mixed = sb("mixed", [P, N])
    raw = sb("raw", [P, NT, 2, DH])
    u = sb("u", [P, NT, 2, DH])
    tmp = sb("tmp", [P, NT, 2, DH])
    res = sb("res", [P, NT, 2, DH])
    rest = sb("rest", [P, N])
    SC, RL, PT, U, MISC = ps[0:2], ps[2:4], ps[4:6], ps[6], ps[7]

    with nc.Block() as block:
        @block.sync
        def _(sp):
            def body(z, par):
                T, q = z.T, z.T % 2
                if T == 0 and (it := z.iteration(1)) is not None:
                    at_pair, at_batch = known(sp, (it % PAIRS) * J_COLS, (it // PAIRS) * N)
                    c0 = known(sp, it - 1)[0]
                    if not early(c0):
                        sp.wait_ge(s.v_ready, c0)
                    sp.dma_start(pj[1 - par][:, :], t.TJf[:, bass.ds(at_pair, J_COLS)]).then_inc(s.pj_in[1 - par], 16)
                    sp.dma_start(xt[1 - par][:, :], t.XNT[:, bass.ds(at_batch, N)]).then_inc(s.pj_in[1 - par], 16)
                if T == 2 and (it := z.iteration(-1)) is not None:
                    at_out, = known(sp, (it % PAIRS) * O_COLS)
                    c0 = known(sp, it - 1)[0]
                    if not early(c0):
                        sp.wait_ge(s.out_made, c0)
                    sp.dma_start(po[1 - par][:, :], t.TOf[:, bass.ds(at_out, O_COLS)]).then_inc(s.po_in[1 - par], 16)
                d, a = z.back(3), z.back(0)
                if d:
                    it, Td, n = d
                    qd = Td % 2
                    c0, c1 = known(sp, 2 * n + 2, 16 * (it * 2 + Td // 2))
                    sp.wait_ge(s.probs, c0)
                    if not early(c1):
                        sp.wait_ge(s.band_in[qd], c1)
                    sp.dma_start(bass.AP(t.p_dram[qd], P, [[2 * PITCH, P], [PITCH, 2], [1, RECT]]),
                                 t.prob[Td][:, :, P * Td:P * Td + RECT]).then_inc(s.probs_stored[qd], 16)
                if a:
                    it, Ta, n = a
                    c0, c1 = known(sp, 2 * n + 2, 16 * (it * 2 + Ta // 2))
                    sp.wait_ge(s.rel_kept, c0)
                    if not early(c1):
                        sp.wait_ge(s.rel_in[q], c1)
                    sp.dma_start(bass.AP(t.r_dram[q], 0, [[2 * EXT, P], [EXT, 2], [1, EXT]]),
                                 rel[q][:, :, :]).then_inc(s.rel_stored[q], 16)
                if d:
                    it, Td, n = d
                    qd = Td % 2
                    c0, c1 = known(sp, 16 * (it * 2 + Td // 2 + 1), n - 1)
                    sp.wait_ge(s.probs_stored[qd], c0)
                    if not early(c1):
                        sp.wait_ge(s.band_turned, c1)
                    sp.dma_start(band[qd][:, :, :],
                                 bass.AP(t.p_dram[qd], 0, [[2 * PITCH + 1, P], [PITCH, 2], [1, RECT]]))\
                        .then_inc(s.band_in[qd], 16)
                if a:
                    it, Ta, n = a
                    c0, c1 = known(sp, 16 * (it * 2 + Ta // 2 + 1), 2 * n - 2)
                    sp.wait_ge(s.rel_stored[q], c0)
                    if not early(c1):
                        sp.wait_ge(s.scores_made, c1)
                    sp.dma_start(relj[q][:, :, :],
                                 bass.AP(t.r_dram[q], P - 1, [[2 * EXT - 1, P], [EXT, 2], [1, RECT]]))\
                        .then_inc(s.rel_in[q], 16)

            run_iterations(sp, body)
            for q in range(2):
                sp.wait_ge(s.rel_stored[q], 16 * ITS * 2)
                sp.wait_ge(s.probs_stored[q], 16 * ITS * 2)

        @block.tensor
        def _(pe):
            def body(z, par):
                T = z.T
                old, av, cur, nxt = z.iteration(-3), z.iteration(-2), z.iteration(0), z.iteration(1)
                b = z.back(1)
                if b:
                    it, Tb, n = b
                    q = Tb % 2
                    bpar = par if T >= 1 else 1 - par
                    lo, hi, at = rect_of(Tb)
                    pe.wait_ge(s.k_kept, it + 1)
                    for h in range(2):
                        if not early(2 * n + h - 1):
                            pe.wait_ge(s.scores_kept, 2 * n + h - 1)
                        nc.tensor.matmul(SC[h][:, :], qt[bpar][:, Tb * P:(Tb + 1) * P], t.kz[bpar][h][:, :],
                                         start=True, stop=False)
                        if h == 0:
                            pe.wait_ge(s.rel_in[q], 16 * (it * 2 + Tb // 2 + 1))
                        nc.tensor.matmul(SC[h][:, lo:hi], k.ident[:, :], relj[q][:, h, at:at + hi - lo],
                                         start=False, stop=True).then_inc(s.scores_made, 1)
                a = z.back(0)
                if a:
                    it, Ta, n = a
                    pe.wait_ge(s.q_kept, it + 1)
                    for h in range(2):
                        if not early(2 * n + h - 1):
                            pe.wait_ge(s.rel_kept, 2 * n + h - 1)
                        nc.tensor.matmul(RL[h][:, 0:EXT], qt[par][:, Ta * P:(Ta + 1) * P], t.relk[h][:, :],
                                         start=True, stop=True).then_inc(s.rel_made, 1)
                if old is not None and T == 0:
                    pe.wait_ge(s.res_chain, old * 5 + 5)
                    if cur is not None:
                        pe.wait_ge(s.k_kept, cur + 1)
                    for jt in range(NT):
                        last = nc.tensor.transpose(MISC[:, jt * P:(jt + 1) * P],
                                                   res[:, jt, :, :].rearrange("p h d -> p (h d)"), k.ident[:, :])
                    last.then_inc(s.res_turned, 1)
                if av is not None and T > 0:
                    pe.wait_ge(s.mixed_kept, av * ORDER + T)
                    if T == 1 and not early(av):
                        pe.wait_ge(s.out_added, av)
                    if T == 1 and cur is not None:
                        pe.wait_ge(s.k_kept, cur + 1)
                    if T == 2:
                        if cur is not None:
                            pe.wait_ge(s.v_kept, cur + 1)
                        else:
                            pe.wait_ge(s.raw_kept, av * ORDER + 1)
                    if T == 3:
                        if nxt is not None:
                            pe.wait_ge(s.q_kept, nxt + 1)
                        else:
                            pe.wait_ge(s.raw_kept, av * ORDER + 2)
                    for jt in range(NT):
                        last = nc.tensor.transpose(MISC[:, jt * P:(jt + 1) * P], mixed[:, jt * P:(jt + 1) * P],
                                                   k.ident[:, :])
                    last.then_inc(s.mixed_turned, 1)
                d = z.back(3)
                if d:
                    it, Td, n = d
                    for h in range(2):
                        pe.wait_ge(s.probs, 2 * n + h + 1)
                        if h == 0 and not early(n - 1):
                            pe.wait_ge(s.band_kept, n - 1)
                        if h == 1 and not early(2 * n):
                            pe.wait_ge(s.probs_kept, 2 * n)
                        for jt in range(NT):
                            last = nc.tensor.transpose(PT[h][:, jt * P:(jt + 1) * P],
                                                       t.prob[Td][:, h, HALF + jt * P:HALF + (jt + 1) * P],
                                                       k.ident[:, :])
                        last.then_inc(s.probs_turned, 1)
                if old is not None and T == 0:
                    pe.wait_ge(s.res_kept, old + 1)
                    pe.wait_ge(s.po_in[1 - par], 16 * (z.half(-3) + 1))
                    for jt in range(NT):
                        last = nc.tensor.matmul(MISC[:, jt * P:(jt + 1) * P], rest[:, jt * P:(jt + 1) * P],
                                                po[1 - par][:, O_W:O_W + P], start=True, stop=True)
                    last.then_inc(s.out_made, 1)
                if T == 1 and cur is not None:
                    pe.wait_ge(s.k_kept, cur + 1)
                    if av is not None:
                        pe.wait_ge(s.raw_kept, av * ORDER + 1)
                    for jt in range(NT):
                        last = nc.tensor.matmul(MISC[:, jt * P:(jt + 1) * P], xt[par][:, jt * P:(jt + 1) * P],
                                                pj[par][:, J_WV:J_WV + P], start=True, stop=True)
                    last.then_inc(s.v_made, 1)
                if T == 2 and nxt is not None:
                    pe.wait_ge(s.pj_in[1 - par], 32 * (z.half(1) + 1))
                    if av is not None:
                        pe.wait_ge(s.raw_kept, av * ORDER + 2)
                    elif cur is not None:
                        pe.wait_ge(s.v_kept, cur + 1)
                    nc.tensor.matmul(MISC[:, :], pj[1 - par][:, J_WQ:J_WQ + P], xt[1 - par][:, :],
                                     start=True, stop=True).then_inc(s.q_made, 1)
                if T == 3 and nxt is not None:
                    pe.wait_ge(s.q_kept, nxt + 1)
                    if av is not None:
                        pe.wait_ge(s.raw_kept, av * ORDER + 3)
                    nc.tensor.matmul(MISC[:, :], pj[1 - par][:, J_WK:J_WK + P], xt[1 - par][:, :],
                                     start=True, stop=True).then_inc(s.k_made, 1)
                e = z.back(4)
                if e:
                    it, Te, n = e
                    q = Te % 2
                    pe.wait_ge(s.band_closed, n + 1)
                    if d:
                        pe.wait_ge(s.probs_kept, 2 * (n + 1) + 1)
                    elif not early(n):
                        pe.wait_ge(s.band_kept, n)
                    for h in range(2):
                        last = nc.tensor.transpose(PT[0][:, h * P:(h + 1) * P], band[q][:, h, P:2 * P], k.ident[:, :])
                    last.then_inc(s.band_turned, 1)
                if av is not None and T < ORDER:
                    if T == 0:
                        pe.wait_ge(s.probs_kept, (av + 1) * 2 * NT)
                        pe.wait_ge(s.band_kept, (av + 1) * NT)
                        pe.wait_ge(s.v_ready, av + 1)
                    else:
                        pe.wait_ge(s.values_next, av * ORDER + T)
                    if not early(av * ORDER + T):
                        pe.wait_ge(s.mixed_kept, av * ORDER + T)
                    for jt in range(NT):
                        for h in range(2):
                            lhs = v[par][:, jt, h * DH:(h + 1) * DH] if T == 0 else u[:, jt, h, :]
                            last = nc.tensor.matmul(U[h * DH:(h + 1) * DH, :], lhs, pt[par][:, h, jt, :],
                                                    start=(jt == 0), stop=(jt == NT - 1 and T > 0))
                    if T == 0:
                        for h in range(2):
                            last = nc.tensor.matmul(U[h * DH:(h + 1) * DH, :], t.relv[:, :], bt[par][:, h, :],
                                                    start=False, stop=True)
                    last.then_inc(s.mixed, 1)

            run_iterations(pe, body)

        @block.scalar
        def _(act):
            def body(z, par):
                T, sp2 = z.T, z.T % 2
                old, av, cur, nxt = z.iteration(-3), z.iteration(-2), z.iteration(0), z.iteration(1)
                if av is not None and T > 0:
                    act.wait_ge(s.mixed, av * ORDER + T)
                    if not early(av * ORDER + T - 1):
                        act.wait_ge(s.mixed_turned, av * ORDER + T - 1)
                    nc.scalar.activation(mixed[:, :], U[:, :], ACT.Copy).then_inc(s.mixed_kept, 1)
                e = z.back(4)
                if e:
                    it, Te, n = e
                    q = Te % 2
                    act.wait_ge(s.band_in[q], 16 * (it * 2 + Te // 2 + 1))
                    for h in range(2):
                        last = nc.scalar.activation(band[q][:, h, 0:P + 1], band[q][:, h, 0:P + 1], ACT.Copy,
                                                    accum_out=la[q][:, h:h + 1])
                        if Te > 0:
                            far = t.prob[Te][:, h, HALF:P * Te]
                            last = nc.scalar.activation(far, far, ACT.Copy, accum_out=lb[q][:, h:h + 1])
                    last.then_inc(s.sums, 1)
                    act.wait_ge(s.sums, n + 1)
                    for h in range(2):
                        if Te > 0:
                            last = nc.scalar.activation(band[q][:, h, P:P + 1], la[q][:, h:h + 1], ACT.Identity,
                                                        bias=lb[q][:, h:h + 1])
                        else:
                            last = nc.scalar.activation(band[q][:, h, P:P + 1], la[q][:, h:h + 1], ACT.Copy)
                    last.then_inc(s.band_closed, 1)
                b = z.back(1)
                if b:
                    it, Tb, n = b
                    q = Tb % 2
                    lo, hi, _ = rect_of(Tb)
                    act.wait_ge(s.rel_kept, 2 * n + 2)
                    for h in range(2):
                        act.wait_ge(s.scores_made, 2 * n + h + 1)
                        if not early(2 * n - 3 + h):
                            act.wait_ge(s.probs, 2 * n - 3 + h)
                        last = nc.scalar.activation(sc[q][:, h, lo:hi], SC[h][:, lo:hi], ACT.Copy)
                        if lo > 0:
                            last = nc.scalar.activation(sc[q][:, h, 0:lo], SC[h][:, 0:lo], ACT.Identity,
                                                        bias=rel[q][:, h, 0:1])
                        if hi < N:
                            last = nc.scalar.activation(sc[q][:, h, hi:N], SC[h][:, hi:N], ACT.Identity,
                                                        bias=rel[q][:, h, EXT - 1:EXT])
                        last.then_inc(s.scores_kept, 1)
                a = z.back(0)
                if a:
                    it, Ta, n = a
                    if not early(it * 2 + Ta // 2):
                        act.wait_ge(s.rel_stored[sp2], 16 * (it * 2 + Ta // 2))
                    for h in range(2):
                        act.wait_ge(s.rel_made, 2 * n + h + 1)
                        nc.scalar.activation(rel[sp2][:, h, :], RL[h][:, 0:EXT], ACT.Copy).then_inc(s.rel_kept, 1)
                if old is not None and T == 0:
                    act.wait_ge(s.res_turned, old + 1)
                    if not early(old):
                        act.wait_ge(s.out_made, old)
                    nc.scalar.activation(rest[:, :], MISC[:, :], ACT.Copy).then_inc(s.res_kept, 1)
                if av is not None and T > 0:
                    act.wait_ge(s.mixed_turned, av * ORDER + T)
                    if not early(av * ORDER + T - 1):
                        act.wait_ge(s.values_next, av * ORDER + T - 1)
                    nc.scalar.activation(raw[:, :, :, :].rearrange("p j h d -> p (j h d)"), MISC[:, :],
                                         ACT.Copy).then_inc(s.raw_kept, 1)
                d = z.back(3)
                if d:
                    it, Td, n = d
                    dpar = 1 - par if T < 3 else par
                    if Td == 0 and not early((it - 1) * ORDER):
                        act.wait_ge(s.mixed, (it - 1) * ORDER)
                    for h in range(2):
                        act.wait_ge(s.probs_turned, 2 * n + h + 1)
                        nc.scalar.activation(pt[dpar][:, h, :, Td * P:(Td + 1) * P],
                                             PT[h][:, :].rearrange("p (j i) -> p j i", j=NT),
                                             ACT.Copy).then_inc(s.probs_kept, 1)
                c = z.back(2)
                if c:
                    it, Tc, n = c
                    q = Tc % 2
                    act.wait_ge(s.tops, 2 * n + 2)
                    nc.scalar.activation(nmax[q][:, :], top[q][:, :, 0], ACT.Copy, scale=-1.0).then_inc(s.maxes, 1)
                    act.wait_ge(s.maxes, n + 1)
                    for h in range(2):
                        if not early(2 * n - 3 + h):
                            act.wait_ge(s.probs, 2 * n - 3 + h)
                        nc.scalar.activation(ex[q][:, h, :], sc[q][:, h, :], ACT.Exp,
                                             bias=nmax[q][:, h:h + 1]).then_inc(s.exps, 1)
                if T == 1 and cur is not None:
                    act.wait_ge(s.v_made, cur + 1)
                    if not early(cur):
                        act.wait_ge(s.v_ready, cur)
                    nc.scalar.activation(vraw[:, :, :].rearrange("p j n -> p (j n)"), MISC[:, :],
                                         ACT.Copy).then_inc(s.v_kept, 1)
                if T == 2 and nxt is not None:
                    act.wait_ge(s.q_made, nxt + 1)
                    nc.scalar.activation(qt[1 - par][:, :], MISC[:, :], ACT.Identity,
                                         bias=pj[1 - par][:, J_BQ:J_BQ + 1]).then_inc(s.q_kept, 1)
                if T == 3 and nxt is not None:
                    act.wait_ge(s.k_made, nxt + 1)
                    for h in range(2):
                        r = slice(h * DH, (h + 1) * DH)
                        last = nc.scalar.activation(t.kz[1 - par][h][r, :], MISC[r, :], ACT.Identity, scale=SCALE,
                                                    bias=pj[1 - par][r, J_BK:J_BK + 1])
                    last.then_inc(s.k_kept, 1)
                if e:
                    it, Te, n = e
                    epar = 1 - par if T < 4 else par
                    if Te == 0 and not early((it - 1) * ORDER):
                        act.wait_ge(s.mixed, (it - 1) * ORDER)
                    act.wait_ge(s.band_turned, n + 1)
                    nc.scalar.activation(bt[epar][:, :, Te * P:(Te + 1) * P],
                                         PT[0][:, 0:2 * P].rearrange("p (h i) -> p h i", h=2),
                                         ACT.Copy).then_inc(s.band_kept, 1)

            run_iterations(act, body)

        @block.vector
        def _(dve):
            def met():
                dve.wait_ge(s.bias_added, B)

            def body(z, par):
                T = z.T
                old = z.iteration(-3)
                c = z.back(2)
                if c:
                    it, Tc, n = c
                    q = Tc % 2
                    cpar = par if T >= 2 else 1 - par
                    for r in range(4):
                        for h in range(2):
                            kept, shortened = known(dve, 2 * n + h + 1, 6 * n + (r - 1) * 2 + h + 1)
                            met()
                            if r == 0:
                                dve.wait_ge(s.scores_kept, kept)
                                nc.vector.max(top[q][:, h, 0:8], sc[q][:, h, :]).then_inc(s.tops, 1)
                            else:
                                dve.wait_ge(s.shortened, shortened)
                                nc.vector.max(top[q][:, h, 8 * r:8 * r + 8], work[:, h, :]).then_inc(s.next_tops, 1)
                        if r == 3:
                            continue
                        for h in range(2):
                            first_found, found = known(dve, 2 * n + h + 1, 6 * n + (r - 1) * 2 + h + 1)
                            met()
                            if r == 0:
                                dve.wait_ge(s.tops, first_found)
                            else:
                                dve.wait_ge(s.next_tops, found)
                            nc.vector.match_replace(out=work[:, h, :], in_to_replace=top[q][:, h, 8 * r:8 * r + 8],
                                                    in_values=sc[q][:, h, :] if r == 0 else work[:, h, :],
                                                    imm_value=NEG).then_inc(s.shortened, 1)
                    if Tc == 0 and not early((it - 1)):
                        dve.wait_ge(s.inverse, it - 1)
                    for h in range(2):
                        dve.wait_ge(s.next_tops, 6 * n + 4 + h + 1)
                        dve.wait_ge(s.exps, 2 * n + h + 1)
                        if not early(n - 3):
                            dve.wait_ge(s.band_closed, n - 3)
                        nc.vector.scalar_tensor_tensor(out=t.prob[Tc][:, h, HALF:HALF + N], in0=sc[q][:, h, :],
                                                       scalar=top[q][:, h, TOPK - 1:TOPK], in1=ex[q][:, h, :],
                                                       op0=ALU.is_ge, op1=ALU.mult,
                                                       accum_out=rs[cpar][:, 2 * Tc + h:2 * Tc + h + 1]
                                                       ).then_inc(s.probs, 1)
                if T == 1 and (it := z.iteration(-1)) is not None:
                    dve.wait_ge(s.probs, (it + 1) * 2 * NT)
                    if not early((it - 1) * ORDER):
                        dve.wait_ge(s.values_next, (it - 1) * ORDER)
                    nc.vector.reciprocal(inv[1 - par][:, :], rs[1 - par][:, :]).then_inc(s.inverse, 1)
                if old is not None and T == 0:
                    dve.wait_ge(s.out_made, old + 1)
                    if not early(old):
                        dve.wait_ge(s.out_added, old)
                    Xb = k.X[:, bass.ds((old // PAIRS) * N, N)]
                    nc.vector.tensor_tensor(Xb, MISC[:, :], Xb, ALU.add).then_inc(s.out_added, 1)

            with dve.Fori(0, B) as b:
                Xb = k.X[:, bass.ds(b * N, N)].rearrange("p (t d) -> p t d", d=D)
                nc.vector.tensor_tensor(Xb, Xb, bcast(k.bout[:, :], [[0, NT], [1, D]]), ALU.add)\
                    .then_inc(s.bias_added, 1)
            dve.wait_ge(s.bias_added, B)
            run_iterations(dve, body)

        @block.gpsimd
        def _(pool):
            def body(z, par):
                T = z.T
                av, cur = z.iteration(-2), z.iteration(0)
                if av is not None and T > 0:
                    pool.wait_ge(s.raw_kept, av * ORDER + T)
                    if T == 1:
                        pool.wait_ge(s.inverse, av + 1)
                        if not early(av):
                            pool.wait_ge(s.res_chain, av * 5)
                    else:
                        pool.wait_ge(s.res_chain, av * 5 + 2 * T - 3)
                    nc.gpsimd.tensor_tensor(u[:, :, :, :], raw[:, :, :, :],
                                            bcast(inv[par][:, :], [[2, NT], [1, 2], [0, DH]]),
                                            ALU.mult).then_inc(s.values_next, 1)
                    alpha = bcast(po[par][:, O_AL + 2 * T - 2:O_AL + 2 * T], [[0, NT], [1, 2], [0, DH]])
                    pool.wait_ge(s.values_next, av * ORDER + T)
                    if T == 1:
                        pool.wait_ge(s.po_in[par], 16 * (z.half(-2) + 1))
                        if not early(av):
                            pool.wait_ge(s.res_turned, av)
                        nc.gpsimd.tensor_tensor(res[:, :, :, :], u[:, :, :, :], alpha, ALU.mult).then_inc(s.res_chain, 1)
                    else:
                        nc.gpsimd.tensor_tensor(tmp[:, :, :, :], u[:, :, :, :], alpha, ALU.mult).then_inc(s.res_chain, 1)
                        pool.wait_ge(s.res_chain, av * 5 + 2 * T - 2)
                        nc.gpsimd.tensor_tensor(res[:, :, :, :], res[:, :, :, :], tmp[:, :, :, :],
                                                ALU.add).then_inc(s.res_chain, 1)
                if T == 1 and cur is not None:
                    pool.wait_ge(s.v_kept, cur + 1)
                    if not early((cur - 2) * ORDER + 1):
                        pool.wait_ge(s.mixed, (cur - 2) * ORDER + 1)
                    nc.gpsimd.tensor_tensor(v[par][:, :, :], vraw[:, :, :], bcast(pj[par][:, J_BV:J_BV + P], [[0, NT], [1, P]]),
                                            ALU.add).then_inc(s.v_ready, 1)

            run_iterations(pool, body)


E, CAP = 8, TILES * P // 8
HALF_IN = 128
MH, MP, MS = 8, 16, 16
CONV = 4
SECOND = 32


def set_up_rest(nc, sem, sb, ps, a, k, r):
    loaded, consts, turned, chain, kept = (sem(f"rest_{n}") for n in ("loaded", "consts", "turned", "chain", "kept"))
    few = nc.allow_non_contiguous_dma
    w_rows = sb("expert_rows", [P, E, D])
    in_rows = sb("w_in_rows", [P, 2, D])
    bc_rows = sb("w_bc_rows", [2 * SECOND, D])
    dt_rows = sb("w_dt_rows", [MH, D])
    wo_rows = sb("w_out_rows", [P, 2 * HALF_IN])
    alog = sb("a_log_all", [P, MH])
    alog_e = sb("a_log_exp", [P, MH])
    LOADS = 19

    with nc.Block() as block:
        @block.sync
        def _(sp):
            sp.wait_ge(consts, 1)
            w_in = a["b_W_in"]
            x0 = HALF_IN
            b0 = x0 + HALF_IN
            c0 = b0 + MS
            d0 = c0 + MS
            sp.dma_start(w_rows[:, :, :], a["f_W"].rearrange("e f h -> f e h")).then_inc(loaded, 16)
            sp.dma_start(in_rows[:, :, :], w_in[0:b0, :].rearrange("(c p) d -> p c d", p=P)).then_inc(loaded, 16)
            sp.dma_start(bc_rows[0:MS, :], w_in[b0:c0, :]).then_inc(loaded, 16)
            sp.dma_start(bc_rows[SECOND:SECOND + MS, :], w_in[c0:d0, :]).then_inc(loaded, 16)
            sp.dma_start(dt_rows[:, :], w_in[d0:d0 + MH, :]).then_inc(loaded, 16)
            sp.dma_start(wo_rows[:, :], a["b_W_out"]).then_inc(loaded, 16)
            sp.dma_start(r.wg[:, :], a["f_wg"]).then_inc(loaded, 16)
            sp.dma_start(r.eb[:, :], a["f_b"]).then_inc(loaded, 16)
            cw = a["b_conv_w"].rearrange("c o k -> c (o k)")
            cb = a["b_conv_b"].rearrange("(c o) -> c o", o=1)
            sp.dma_start(r.cwx[:, :], cw[0:P, :]).then_inc(loaded, 16)
            sp.dma_start(r.cwb[0:MS, :], cw[P:P + MS, :]).then_inc(loaded, 16)
            sp.dma_start(r.cwb[SECOND:SECOND + MS, :], cw[P + MS:P + 2 * MS, :]).then_inc(loaded, 16)
            sp.dma_start(r.cbx[:, :], cb[0:P, :]).then_inc(loaded, 16)
            sp.dma_start(r.cbb[0:MS, :], cb[P:P + MS, :]).then_inc(loaded, 16)
            sp.dma_start(r.cbb[SECOND:SECOND + MS, :], cb[P + MS:P + 2 * MS, :]).then_inc(loaded, 16)

            def everywhere(to, of):
                sp.dma_start(to, of.rearrange("(o n) -> o n", o=1).to_broadcast([P, MH])).then_inc(loaded, 16)

            everywhere(r.dtb[:, :], a["b_dt_bias"])
            everywhere(alog[:, :], a["b_A_log"])
            everywhere(r.dskip[:, :], a["b_Dskip"])
            with few(reason="256 values each, once"):
                sp.dma_start(r.lnw[:, :], a["b_ln_w"].rearrange("(c p) -> p c", p=P)).then_inc(loaded, 16)
                sp.dma_start(r.lnb[:, :], a["b_ln_b"].rearrange("(c p) -> p c", p=P)).then_inc(loaded, 16)
            sp.wait_ge(loaded, 16 * LOADS)

        @block.gpsimd
        def _(pool):
            pool.wait_ge(chain, 1)
            for m, base in ((r.before, 0), (r.upto, 1)):
                nc.gpsimd.affine_select(out=m[:, :], in_=m[:, :], compare_op=ALU.is_gt, fill=0.0,
                                        base=base, pattern=[[1, P]], channel_multiplier=-1)
            nc.gpsimd.affine_select(out=r.after[:, :], in_=r.after[:, :], compare_op=ALU.is_gt, fill=0.0,
                                    base=0, pattern=[[-1, P]], channel_multiplier=1)

        @block.vector
        def _(dve):
            nc.vector.memset(bc_rows[:, :], 0.0)
            nc.vector.memset(r.cwb[:, :], 0.0)
            nc.vector.memset(r.cbb[:, :], 0.0).then_inc(consts, 1)
            for m in (r.before, r.upto, r.after):
                nc.vector.memset(m[:, :], 1.0)
            nc.vector.memset(r.ones[:, :], 1.0)
            nc.vector.memset(r.rank[:, 0:1], float(E))
            for e in range(1, E):
                last = nc.vector.memset(r.rank[:, e:e + 1], float(E - e))
            last.then_inc(chain, 1)
            dve.wait_ge(loaded, 16 * LOADS)
            dve.wait_ge(turned, 1)
            nc.vector.tensor_copy(r.win[:, 0:2 * P], ps[2][:, 0:2 * P])
            nc.vector.tensor_copy(r.win[:, 2 * P:2 * P + 2 * SECOND], ps[3][:, 0:2 * SECOND])
            nc.vector.tensor_copy(r.wdt[:, :], ps[4][:, 0:MH])
            nc.vector.tensor_copy(r.wo[:, :, :].rearrange("p c d -> p (c d)"), ps[5][:, 0:2 * P])
            nc.vector.tensor_scalar(r.cbx2[:, :], r.cbx[:, :], 0.5, None, ALU.mult)
            nc.vector.tensor_scalar(r.cbb2[:, :], r.cbb[:, :], 0.5, None, ALU.mult)
            dve.wait_ge(kept, 1)
            nc.vector.tensor_scalar(r.A[:, :], alog_e[:, :], -1.0, None, ALU.mult).then_inc(chain, 1)
            dve.wait_ge(chain, 2)

        @block.tensor
        def _(pe):
            pe.wait_ge(loaded, 16 * LOADS)
            for e in range(E):
                nc.tensor.transpose(ps[e // 4][:, (e % 4) * P:(e % 4 + 1) * P], w_rows[:, e, :], k.ident[:, :])
            for c in range(2):
                nc.tensor.transpose(ps[2][:, c * P:(c + 1) * P], in_rows[:, c, :], k.ident[:, :])
                nc.tensor.transpose(ps[5][:, c * P:(c + 1) * P], wo_rows[:, c * P:(c + 1) * P], k.ident[:, :])
            nc.tensor.transpose(ps[3][:, 0:2 * SECOND], bc_rows[:, :], k.ident[0:2 * SECOND, 0:2 * SECOND])
            nc.tensor.transpose(ps[4][:, 0:MH], dt_rows[:, :], k.ident[0:MH, 0:MH]).then_inc(turned, 1)

        @block.scalar
        def _(act):
            act.wait_ge(loaded, 16 * LOADS)
            nc.scalar.activation(alog_e[:, :], alog[:, :], ACT.Exp).then_inc(kept, 1)
            act.wait_ge(turned, 1)
            for q in range(2):
                last = nc.scalar.activation(r.we[:, q * 512:(q + 1) * 512], ps[q][:, :], ACT.Copy)
            last.then_inc(kept, 1)


def eight_sems(sem, tag):
    s = Namespace()
    s.made, s.kept, s.turned, s.stored = (sem(f"{tag}_{n}") for n in ("made", "kept", "turned", "stored"))
    return s


def eight_tensor(nc, pe, s, W, XNT, rows, banks, ident):
    def body(i, par, first):
        if not first:
            pe.wait_ge(s.kept, i - 1)
        nc.tensor.matmul(banks[par][0:8, :], W, XNT[:, bass.ds(i * 512, 512)], start=True, stop=True).then_inc(s.made, 1)
        kept, stored = known(pe, i + 1, i - 1)
        pe.wait_ge(s.made, 1)
        pe.wait_ge(s.kept, kept)
        if not first:
            pe.wait_ge(s.stored, stored)
        for c in range(4):
            last = nc.tensor.transpose(banks[2 + par][:, c * 8:c * 8 + 8], rows[par][:, c * P:(c + 1) * P],
                                       ident[0:8, 0:8])
        last.then_inc(s.turned, 1)

    two_at_a_time(pe, GROUPS, body)


def eight_scalar(nc, act, s, rows, banks):
    def body(i, par, first):
        act.wait_ge(s.made, i + 1)
        if not first:
            act.wait_ge(s.turned, i - 1)
        nc.scalar.activation(rows[par][:, :], banks[par][0:8, :], ACT.Copy).then_inc(s.kept, 1)

    two_at_a_time(act, GROUPS, body)


def eight_vector(nc, dve, s, OUT, banks):
    def body(i, par, first):
        dve.wait_ge(s.turned, i + 1)
        nc.vector.tensor_copy(OUT[:, bass.ds(i * 32, 32)], banks[2 + par][:, 0:32]).then_inc(s.stored, 1)

    two_at_a_time(dve, GROUPS, body)


def experts(nc, sem, sb, ps, k, r, tag):
    def S(n):
        return sem(f"{tag}_{n}")

    g = eight_sems(sem, f"{tag}_logits")
    step, ex_done, counted, gates = S("step"), S("exp"), S("counted"), S("gates")
    xs_in = [S(f"xs_in{q}") for q in range(2)]
    staged, g_turned, g_kept, bias_made, bias_added = (S(n) for n in (
        "staged", "g_turned", "g_kept", "bias_made", "bias_added"))
    y_made, y_used = S("y_made"), S("y_used")
    rows = [sb(f"{tag}_rows{q}", [8, 512]) for q in range(2)]
    n8 = TILES * E
    b = Namespace()
    b.logit = sb(f"{tag}_logit", [P, n8])
    b.diff = sb(f"{tag}_diff", [P, n8])
    b.exp = sb(f"{tag}_exp", [P, n8])
    b.same = sb(f"{tag}_same", [P, n8])
    b.score = sb(f"{tag}_score", [P, n8])
    b.mask = sb(f"{tag}_mask", [P, n8])
    b.loc = sb(f"{tag}_loc", [P, n8])
    b.keep = sb(f"{tag}_keep", [P, n8])
    b.gate8 = sb(f"{tag}_gate8", [P, n8])
    b.prev = sb(f"{tag}_prev", [P, n8])
    b.sum_a = sb(f"{tag}_sum_a", [P, n8])
    b.sum_b = sb(f"{tag}_sum_b", [P, n8])
    b.top = sb(f"{tag}_top", [P, TILES])
    b.total = sb(f"{tag}_total", [P, TILES])
    b.prob = sb(f"{tag}_prob", [P, TILES])
    b.best = sb(f"{tag}_best", [P, TILES])
    xs = [sb(f"{tag}_xs{q}", [P, 512]) for q in range(2)]
    gs = [sb(f"{tag}_gs{q}", [P, 4 * E]) for q in range(2)]
    gt = [sb(f"{tag}_gt{q}", [E, 512]) for q in range(2)]

    def v3(x):
        return x[:, :].rearrange("p (t e) -> p t e", e=E)

    def over(x):
        return bcast(x[:, :], [[1, TILES], [0, E]])

    with nc.Block() as block:
        @block.tensor
        def _(pe):
            eight_tensor(nc, pe, g, r.wg[:, :], k.XNT, rows, ps, k.ident)
            pe.wait_ge(step, 1)
            nc.tensor.matmul(ps[4][:, 0:n8], r.before[:, :], b.mask[:, :], start=True, stop=True)
            nc.tensor.matmul(ps[5][:, 0:n8], r.ones[:, :], b.mask[:, :], start=True, stop=True).then_inc(counted, 1)

        @block.scalar
        def _(act):
            eight_scalar(nc, act, g, rows, ps)
            act.wait_ge(ex_done, 1)
            nc.scalar.activation(b.exp[:, :], b.diff[:, :], ACT.Exp).then_inc(ex_done, 1)

        @block.vector
        def _(dve):
            chain = [0]

            def link(ins):
                chain[0] += 1
                ins.then_inc(gates, 1)
                dve.wait_ge(gates, chain[0])

            eight_vector(nc, dve, g, b.logit, ps)
            dve.wait_ge(g.stored, GROUPS)
            link(nc.vector.tensor_reduce(out=b.top[:, :], in_=v3(b.logit), axis=AX.X, op=ALU.max))
            nc.vector.tensor_tensor(v3(b.diff), v3(b.logit), over(b.top), ALU.subtract).then_inc(ex_done, 1)
            link(nc.vector.tensor_tensor(v3(b.same), v3(b.logit), over(b.top), ALU.is_equal))
            link(nc.vector.tensor_tensor(v3(b.score), v3(b.same), bcast(r.rank[:, :], [[0, TILES], [1, E]]), ALU.mult))
            link(nc.vector.tensor_reduce(out=b.best[:, :], in_=v3(b.score), axis=AX.X, op=ALU.max))
            nc.vector.tensor_tensor(v3(b.mask), v3(b.score), over(b.best), ALU.is_equal).then_inc(step, 1)
            dve.wait_ge(ex_done, 2)
            link(nc.vector.tensor_reduce(out=b.total[:, :], in_=v3(b.exp), axis=AX.X, op=ALU.add))
            link(nc.vector.reciprocal(b.prob[:, :], b.total[:, :]))
            dve.wait_ge(counted, 1)
            nc.vector.memset(b.sum_a[:, 0:E], 0.0)
            link(nc.vector.tensor_copy(b.sum_a[:, E:n8], ps[5][:, 0:n8 - E]))
            src, dst, stride = b.sum_a, b.sum_b, E
            while stride < n8:
                nc.vector.tensor_copy(dst[:, 0:stride], src[:, 0:stride])
                link(nc.vector.tensor_tensor(dst[:, stride:n8], src[:, stride:n8], src[:, 0:n8 - stride], ALU.add))
                src, dst, stride = dst, src, stride * 2
            link(nc.vector.tensor_tensor(b.loc[:, :], ps[4][:, 0:n8], src[:, :], ALU.add))
            link(nc.vector.scalar_tensor_tensor(out=b.keep[:, :], in0=b.loc[:, :], scalar=float(CAP), in1=b.mask[:, :],
                                                op0=ALU.is_lt, op1=ALU.mult))
            link(nc.vector.tensor_tensor(v3(b.gate8), v3(b.keep), over(b.prob), ALU.mult))

    with nc.Block() as block:
        @block.sync
        def _(sp):
            def body(i, par, first):
                at, free = known(sp, i * 512, (i - 1) * 4)
                if not first:
                    sp.wait_ge(y_made, free)
                sp.dma_start(xs[par][:, :], k.XNT[:, bass.ds(at, 512)]).then_inc(xs_in[par], 16)

            two_at_a_time(sp, GROUPS, body)

        @block.tensor
        def _(pe):
            def body(i, par, first, half=0):
                pe.wait_ge(staged, i + 1)
                if not first:
                    pe.wait_ge(g_kept, i - 1)
                for c in range(4):
                    last = nc.tensor.transpose(ps[4 + par][0:E, c * P:(c + 1) * P], gs[par][:, c * E:(c + 1) * E],
                                               k.ident[:, :])
                last.then_inc(g_turned, 1)
                pe.wait_ge(xs_in[par], (half + 1) * 16)
                for c in range(4):
                    for q in range(2):
                        bank = ps[2 * (c % 2) + q]
                        if not (first and par == 0 and c < 2):
                            pe.wait_ge(y_used, (i * 4 + c - 1) * E)
                        last = nc.tensor.matmul(bank[:, :], xs[par][:, c * P:(c + 1) * P],
                                                r.we[:, q * 512:(q + 1) * 512], start=True, stop=True)
                    last.then_inc(y_made, 1)
                    if c == 0:
                        pe.wait_ge(g_kept, i + 1)
                        if not first:
                            pe.wait_ge(bias_added, i - 1)
                        for cc in range(4):
                            last = nc.tensor.matmul(ps[6 + par][:, cc * P:(cc + 1) * P], gt[par][:, cc * P:(cc + 1) * P],
                                                    r.eb[:, :], start=True, stop=True)
                        last.then_inc(bias_made, 1)

            two_at_a_time(pe, GROUPS, body, with_half=True)

        @block.scalar
        def _(act):
            def body(i, par, first):
                if not first:
                    act.wait_ge(g_turned, i - 1)
                nc.scalar.activation(gs[par][:, :], b.gate8[:, bass.ds(i * 4 * E, 4 * E)], ACT.Copy).then_inc(staged, 1)
                act.wait_ge(g_turned, i + 1)
                if not first:
                    act.wait_ge(bias_made, i - 1)
                nc.scalar.activation(gt[par][:, :], ps[4 + par][0:E, :], ACT.Copy).then_inc(g_kept, 1)

            two_at_a_time(act, GROUPS, body)

        @block.vector
        def _(dve):
            def body(i, par, first):
                X4 = k.X[:, bass.ds(i * 512, 512)]
                dve.wait_ge(bias_made, i + 1)
                nc.vector.tensor_tensor(X4, ps[6 + par][:, :], X4, ALU.add).then_inc(bias_added, 1)
                for c in range(4):
                    Xc = k.X[:, bass.ds(i * 512 + c * D, D)]
                    dve.wait_ge(y_made, i * 4 + c + 1)
                    for e in range(E):
                        if e == 0:
                            dve.wait_ge(bias_added, i + 1)
                        else:
                            dve.wait_ge(y_used, (i * 4 + c) * E + e)
                        nc.vector.scalar_tensor_tensor(
                            out=Xc, in0=ps[2 * (c % 2) + e // 4][:, (e % 4) * P:(e % 4 + 1) * P],
                            scalar=b.gate8[:, bass.ds((i * 4 + c) * E + e, 1)], in1=Xc,
                            op0=ALU.mult, op1=ALU.add).then_inc(y_used, 1)

            two_at_a_time(dve, GROUPS, body)


def mixer(nc, sem, sb, ps, k, r):
    def S(n):
        return sem(f"mixer_{n}")

    g = eight_sems(sem, "mixer_dt")
    step, e_done, sums, dt_chain = S("step"), S("exp"), S("sums"), S("dt_chain")
    rows = [sb(f"mixer_rows{q}", [8, 512]) for q in range(2)]
    n8 = TILES * MH
    b = Namespace()
    b.raw = sb("mixer_raw", [P, n8])
    b.v = sb("mixer_v", [P, n8])
    b.neg = sb("mixer_neg", [P, n8])
    b.e = sb("mixer_e", [P, n8])
    b.log = sb("mixer_log", [P, n8])
    b.dt = sb("mixer_dt", [P, n8])
    b.a = sb("mixer_a", [P, n8])
    b.to_end = sb("mixer_to_end", [P, n8])
    b.from_start = sb("mixer_from_start", [P, n8])
    b.whole = sb("mixer_whole", [P, n8])

    with nc.Block() as block:
        @block.tensor
        def _(pe):
            eight_tensor(nc, pe, g, r.wdt[:, :], k.XNT, rows, ps, k.ident)
            pe.wait_ge(step, 2)
            nc.tensor.matmul(ps[4][:, 0:n8], r.after[:, :], b.a[:, :], start=True, stop=True)
            nc.tensor.matmul(ps[5][:, 0:n8], r.upto[:, :], b.a[:, :], start=True, stop=True)
            nc.tensor.matmul(ps[6][:, 0:n8], r.ones[:, :], b.a[:, :], start=True, stop=True).then_inc(sums, 1)

        @block.scalar
        def _(act):
            eight_scalar(nc, act, g, rows, ps)
            act.wait_ge(step, 1)
            nc.scalar.activation(b.e[:, :], b.neg[:, :], ACT.Exp).then_inc(e_done, 1)
            act.wait_ge(e_done, 1)
            nc.scalar.activation(b.log[:, :], b.e[:, :], ACT.Ln, bias=1.0).then_inc(e_done, 1)
            act.wait_ge(sums, 1)
            for bank, to in ((ps[4], b.to_end), (ps[5], b.from_start), (ps[6], b.whole)):
                nc.scalar.activation(to[:, :], bank[:, 0:n8], ACT.Exp).then_inc(e_done, 1)

        @block.vector
        def _(dve):
            eight_vector(nc, dve, g, b.raw, ps)
            dve.wait_ge(g.stored, GROUPS)
            v3, raw3 = (x[:, :].rearrange("p (t e) -> p t e", e=MH) for x in (b.v, b.raw))
            nc.vector.tensor_tensor(v3, raw3, bcast(r.dtb[:, :], [[0, TILES], [1, MH]]), ALU.add).then_inc(dt_chain, 1)
            dve.wait_ge(dt_chain, 1)
            nc.vector.scalar_tensor_tensor(out=b.neg[:, :], in0=b.v[:, :], scalar=-1.0, in1=b.v[:, :],
                                           op0=ALU.mult, op1=ALU.min).then_inc(step, 1)
            dve.wait_ge(e_done, 2)
            nc.vector.scalar_tensor_tensor(out=b.dt[:, :], in0=b.v[:, :], scalar=0.0, in1=b.log[:, :],
                                           op0=ALU.max, op1=ALU.add).then_inc(dt_chain, 1)
            dve.wait_ge(dt_chain, 2)
            nc.vector.tensor_tensor(b.a[:, :].rearrange("p (t e) -> p t e", e=MH),
                                    b.dt[:, :].rearrange("p (t e) -> p t e", e=MH),
                                    bcast(r.A[:, :], [[0, TILES], [1, MH]]), ALU.mult).then_inc(step, 1)

    xs_in = [S(f"xs_in{q}") for q in range(2)]
    m = Namespace()
    m.projected = S("projected")
    m.conv_in = S("conv_in")
    m.conv_out = S("conv_out")
    m.squashed = S("squashed")
    m.silu = S("silu")
    m.turned = S("turned")
    m.turned_used = S("turned_used")
    m.spread = S("spread")
    m.diffs = S("diffs")
    m.exps = S("exps")
    m.weights = S("weights")
    m.y_made = S("y_made")
    m.padded = S("padded")
    m.y_used = S("y_used")
    m.stats = S("stats")
    m.var = S("var")
    m.rstd = S("rstd")
    m.scaled = S("scaled")
    m.yn_turned = S("yn_turned")
    m.yt_kept = S("yt_kept")
    m.out_made = S("out_made")
    m.out_added = S("out_added")
    m.link = S("link")
    xs = [sb(f"mixer_xs{q}", [P, N]) for q in range(2)]
    PAD = CONV - 1
    xp = sb("mixer_conv_x", [P, PAD + N])
    bp = sb("mixer_conv_bc", [2 * SECOND, PAD + N])
    cx = [sb(f"mixer_sum_x{q}", [P, N]) for q in range(2)]
    cb = [sb(f"mixer_sum_bc{q}", [2 * SECOND, N]) for q in range(2)]
    tx, hx = sb("mixer_tanh_x", [P, N]), sb("mixer_half_x", [P, N])
    tb, hb = sb("mixer_tanh_bc", [2 * SECOND, N]), sb("mixer_half_bc", [2 * SECOND, N])
    xc = sb("mixer_x", [P, N])
    bs, cs = sb("mixer_b", [MS, N]), sb("mixer_c", [MS, N])
    yz = sb("mixer_yz", [P, NT, 2 * HALF_IN])
    yn = sb("mixer_yn", [P, NT, 2 * HALF_IN])
    yt = sb("mixer_yt", [P, 2, P])
    al = [sb(f"mixer_a_spread{q}", [P, MH, P]) for q in range(2)]
    ex = [sb(f"mixer_decay{q}", [P, MH, P]) for q in range(2)]
    mm = [sb(f"mixer_weights{q}", [P, MH, P]) for q in range(2)]
    gm = [sb(f"mixer_cb{q}", [P, P]) for q in range(2)]
    dx = [sb(f"mixer_dtx{q}", [P, MH, MP]) for q in range(2)]
    xd = [sb(f"mixer_dtx_end{q}", [P, MH, MP]) for q in range(2)]
    bt = [sb(f"mixer_b_rows{q}", [P, MS]) for q in range(2)]
    st, st2 = sb("mixer_state", [MS, MH, MP]), sb("mixer_state_decayed", [MS, MH, MP])
    yo, y1 = sb("mixer_y_off", [P, MH, MP]), sb("mixer_y_sum", [P, MH, MP])
    stat = sb("mixer_stats", [P, NT, 6])
    w = Namespace()
    w.mean2 = sb("mixer_n_mean2", [P, NT])
    w.mean = sb("mixer_n_mean", [P, NT])
    w.diff = sb("mixer_n_diff", [P, NT])
    w.diff2 = sb("mixer_n_diff2", [P, NT])
    w.var2 = sb("mixer_n_var2", [P, NT])
    w.var = sb("mixer_n_var", [P, NT])
    w.vareps = sb("mixer_n_vareps", [P, NT])
    w.rstd = sb("mixer_n_rstd", [P, NT])
    w.mhalf = sb("mixer_n_mhalf", [P, NT])
    LINKS = 25
    T1, DF, Y, O = ps[3], ps[4:6], ps[6], ps[7]
    PX, PB, PZ = ps[0], ps[1], ps[2]

    def heads(x, i, c):
        return x[:, bass.ds((i * NT + c) * MH, MH)].unsqueeze(2).to_broadcast([P, MH, MP])

    with nc.Block() as block:
        @block.sync
        def _(sp):
            def body(i, par, first):
                at, used = known(sp, i * N, (i - 1) * 3)
                if not first:
                    sp.wait_ge(m.projected, used)
                sp.dma_start(xs[par][:, :], k.XNT[:, bass.ds(at, N)]).then_inc(xs_in[par], 16)

            two_at_a_time(sp, B, body)

        @block.tensor
        def _(pe):
            def first_half(i, c):
                t, q, cols = i * NT + c, c % 2, slice(c * P, (c + 1) * P)
                if c == 0:
                    pe.wait_ge(m.silu, i * 3 + 3)
                if not early(t):
                    pe.wait_ge(m.turned_used, t)
                nc.tensor.transpose(T1[:, 0:P], xc[:, cols], k.ident[:, :])
                nc.tensor.transpose(T1[:, P:P + MS], bs[:, cols], k.ident[0:MS, 0:MS])
                nc.tensor.matmul(T1[:, 2 * P:3 * P], bs[:, cols], cs[:, cols], start=True, stop=True).then_inc(m.turned, 1)
                pe.wait_ge(m.spread, t + 1)
                if not early(t):
                    pe.wait_ge(m.exps, t)
                for h in range(MH):
                    last = nc.tensor.matmul(DF[h // 4][:, (h % 4) * P:(h % 4 + 1) * P], al[q][:, h, :], r.upto[:, :],
                                            start=True, stop=True)
                last.then_inc(m.diffs, 1)

            def second_half(i, c):
                t, q, cols = i * NT + c, c % 2, slice(c * P, (c + 1) * P)
                pe.wait_ge(m.weights, t + 1)
                if not early(t):
                    pe.wait_ge(m.y_used, t)
                for h in range(MH):
                    nc.tensor.matmul(Y[:, h * MP:(h + 1) * MP], mm[q][:, h, :], dx[q][:, h, :], start=True, stop=True)
                nc.tensor.matmul(Y[:, P:2 * P], cs[:, cols], st[:, :, :].rearrange("n h p -> n (h p)"),
                                 start=True, stop=True)
                nc.tensor.matmul(Y[0:MS, 2 * P:3 * P], bt[q][:, :], xd[q][:, :, :].rearrange("s h p -> s (h p)"),
                                 start=True, stop=True).then_inc(m.y_made, 1)

            def body(i, par, first, half):
                pe.wait_ge(xs_in[par], (half + 1) * 16)
                if not early(i):
                    pe.wait_ge(m.conv_in, i * 3)
                nc.tensor.matmul(PX[:, :], r.win[:, P:2 * P], xs[par][:, :], start=True, stop=True).then_inc(m.projected, 1)
                nc.tensor.matmul(PB[0:2 * SECOND, :], r.win[:, 2 * P:2 * P + 2 * SECOND], xs[par][:, :],
                                 start=True, stop=True).then_inc(m.projected, 1)
                for c in range(NT):
                    last = nc.tensor.matmul(PZ[:, c * P:(c + 1) * P], xs[par][:, c * P:(c + 1) * P], r.win[:, 0:P],
                                            start=True, stop=True)
                last.then_inc(m.projected, 1)
                first_half(i, 0)
                for c in range(NT):
                    if c + 1 < NT:
                        first_half(i, c + 1)
                    second_half(i, c)
                for c in range(NT):
                    t = i * NT + c
                    pe.wait_ge(m.scaled, t + 1)
                    if not early(t):
                        pe.wait_ge(m.out_added, t)
                    for e in range(2):
                        last = nc.tensor.transpose(O[:, e * P:(e + 1) * P], yn[:, c, e * P:(e + 1) * P], k.ident[:, :])
                    last.then_inc(m.yn_turned, 1)
                    pe.wait_ge(m.yt_kept, t + 1)
                    for e in range(2):
                        last = nc.tensor.matmul(O[:, 2 * P:3 * P], yt[:, e, :], r.wo[:, e, :], start=(e == 0), stop=(e == 1))
                    last.then_inc(m.out_made, 1)

            two_at_a_time(pe, B, body, with_half=True)

        @block.scalar
        def _(act):
            def decays(i, c):
                t, q = i * NT + c, c % 2
                act.wait_ge(m.diffs, t + 1)
                if not early(t - 1):
                    act.wait_ge(m.weights, t - 1)
                for e in range(2):
                    last = nc.scalar.activation(ex[q][:, 4 * e:4 * e + 4, :].rearrange("p h t -> p (h t)"), DF[e][:, :], ACT.Exp)
                last.then_inc(m.exps, 1)

            def body(i, par, first):
                act.wait_ge(m.projected, i * 3 + 1)
                act.wait_ge(m.conv_out, i * 2) if not early(i) else None
                nc.scalar.activation(xp[:, PAD:], PX[:, :], ACT.Copy).then_inc(m.conv_in, 1)
                act.wait_ge(m.projected, i * 3 + 2)
                nc.scalar.activation(bp[:, PAD:], PB[0:2 * SECOND, :], ACT.Copy).then_inc(m.conv_in, 1)
                act.wait_ge(m.projected, i * 3 + 3)
                if not early(i):
                    act.wait_ge(m.scaled, i * NT)
                nc.scalar.activation(yz[:, :, HALF_IN:], PZ[:, :].rearrange("p (c e) -> p c e", c=NT),
                                     ACT.Copy).then_inc(m.conv_in, 1)
                act.wait_ge(m.conv_out, i * 2 + 1)
                if not early(i):
                    act.wait_ge(m.silu, i * 3)
                nc.scalar.activation(tx[:, :], cx[1][:, :], ACT.Tanh, bias=r.cbx2[:, :], scale=0.5)
                nc.scalar.activation(hx[:, :], cx[1][:, :], ACT.Identity, bias=r.cbx2[:, :], scale=0.5).then_inc(m.squashed, 1)
                act.wait_ge(m.conv_out, i * 2 + 2)
                nc.scalar.activation(tb[:, :], cb[1][:, :], ACT.Tanh, bias=r.cbb2[:, :], scale=0.5)
                nc.scalar.activation(hb[:, :], cb[1][:, :], ACT.Identity, bias=r.cbb2[:, :], scale=0.5).then_inc(m.squashed, 1)
                for c in range(NT):
                    decays(i, c)
                for c in range(NT):
                    t = i * NT + c
                    act.wait_ge(m.yn_turned, t + 1)
                    if not early(t):
                        act.wait_ge(m.out_made, t)
                    for e in range(2):
                        last = nc.scalar.activation(yt[:, e, :], O[:, e * P:(e + 1) * P], ACT.Identity,
                                                    scale=r.lnw[:, e:e + 1], bias=r.lnb[:, e:e + 1])
                    last.then_inc(m.yt_kept, 1)

            two_at_a_time(act, B, body)

        @block.gpsimd
        def _(pool):
            def body(i, par, first):
                for c in range(NT):
                    t, q = i * NT + c, c % 2
                    if not early(t - 1):
                        pool.wait_ge(m.diffs, t - 1)
                    nc.gpsimd.tensor_tensor(al[q][:, :, :], bcast(r.after[:, :], [[0, MH], [1, P]]),
                                            b.a[:, bass.ds(t * MH, MH)].unsqueeze(2).to_broadcast([P, MH, P]),
                                            ALU.mult).then_inc(m.spread, 1)
                pool.wait_ge(m.var, i + 1)
                nc.gpsimd.tensor_tensor(w.rstd[:, :], w.vareps[:, :], w.mhalf[:, :], ALU.pow).then_inc(m.rstd, 1)

            two_at_a_time(pool, B, body)

        @block.vector
        def _(dve):
            nc.vector.memset(w.mhalf[:, :], -0.5)
            nc.vector.memset(xp[:, 0:PAD], 0.0)
            nc.vector.memset(bp[:, 0:PAD], 0.0).then_inc(m.padded, 1)
            dve.wait_ge(m.padded, 1)

            def body(i, par, first):
                links = [0]

                def link(ins):
                    links[0] += 1
                    ins.then_inc(m.link, 1)
                    return i * LINKS + links[0]

                dve.wait_ge(m.conv_in, i * 3 + 1)
                ax = link(nc.vector.tensor_scalar(cx[0][:, :], xp[:, 0:N], r.cwx[:, 0:1], None, ALU.mult))
                dve.wait_ge(m.conv_in, i * 3 + 2)
                ab = link(nc.vector.tensor_scalar(cb[0][:, :], bp[:, 0:N], r.cwb[:, 0:1], None, ALU.mult))
                for j in range(1, CONV):
                    dve.wait_ge(m.link, ax)
                    o = nc.vector.scalar_tensor_tensor(out=cx[j % 2][:, :], in0=xp[:, j:j + N], scalar=r.cwx[:, j:j + 1],
                                                       in1=cx[1 - j % 2][:, :], op0=ALU.mult, op1=ALU.add)
                    if j < CONV - 1:
                        ax = link(o)
                    else:
                        o.then_inc(m.conv_out, 1)
                    dve.wait_ge(m.link, ab)
                    o = nc.vector.scalar_tensor_tensor(out=cb[j % 2][:, :], in0=bp[:, j:j + N], scalar=r.cwb[:, j:j + 1],
                                                       in1=cb[1 - j % 2][:, :], op0=ALU.mult, op1=ALU.add)
                    if j < CONV - 1:
                        ab = link(o)
                    else:
                        o.then_inc(m.conv_out, 1)
                nc.vector.memset(st[:, :, :], 0.0)
                dve.wait_ge(m.squashed, i * 2 + 1)
                nc.vector.scalar_tensor_tensor(out=xc[:, :], in0=tx[:, :], scalar=1.0, in1=hx[:, :],
                                               op0=ALU.add, op1=ALU.mult).then_inc(m.silu, 1)
                dve.wait_ge(m.squashed, i * 2 + 2)
                nc.vector.scalar_tensor_tensor(out=bs[:, :], in0=tb[0:MS, :], scalar=1.0, in1=hb[0:MS, :],
                                               op0=ALU.add, op1=ALU.mult).then_inc(m.silu, 1)
                nc.vector.scalar_tensor_tensor(out=cs[:, :], in0=tb[SECOND:SECOND + MS, :], scalar=1.0,
                                               in1=hb[SECOND:SECOND + MS, :],
                                               op0=ALU.add, op1=ALU.mult).then_inc(m.silu, 1)

                def before(c):
                    t, q = i * NT + c, c % 2
                    dve.wait_ge(m.turned, t + 1)
                    xrows = T1[:, 0:P].rearrange("s (h p) -> s h p", h=MH)
                    nc.vector.tensor_copy(bt[q][:, :], T1[:, P:P + MS])
                    nc.vector.tensor_tensor(gm[q][:, :], T1[:, 2 * P:3 * P], r.upto[:, :], ALU.mult)
                    n1 = link(nc.vector.tensor_tensor(dx[q][:, :, :], xrows, heads(b.dt, i, c), ALU.mult))
                    nc.vector.tensor_tensor(yz[:, c, 0:HALF_IN].rearrange("p (h w) -> p h w", h=MH), xrows,
                                            r.dskip[:, :].unsqueeze(2).to_broadcast([P, MH, MP]),
                                            ALU.mult).then_inc(m.turned_used, 1)
                    dve.wait_ge(m.link, n1)
                    nc.vector.tensor_tensor(xd[q][:, :, :], dx[q][:, :, :], heads(b.to_end, i, c), ALU.mult)
                    dve.wait_ge(m.exps, t + 1)
                    for e in range(2):
                        last = nc.vector.tensor_tensor(mm[q][:, 4 * e:4 * e + 4, :], ex[q][:, 4 * e:4 * e + 4, :],
                                                       bcast(gm[q][:, :], [[0, 4], [1, P]]), ALU.mult)
                    last.then_inc(m.weights, 1)

                def behind(c):
                    t = i * NT + c
                    dve.wait_ge(m.y_made, t + 1)
                    nc.vector.tensor_tensor(yo[:, :, :], Y[:, P:2 * P].rearrange("p (h w) -> p h w", h=MH),
                                            heads(b.from_start, i, c), ALU.mult)
                    n1 = link(nc.vector.tensor_tensor(st2[:, :, :], st[:, :, :],
                                                      b.whole[0:MS, bass.ds(t * MH, MH)].unsqueeze(2)
                                                      .to_broadcast([MS, MH, MP]), ALU.mult))
                    dve.wait_ge(m.link, n1)
                    n2 = link(nc.vector.tensor_tensor(y1[:, :, :], Y[:, 0:P].rearrange("p (h w) -> p h w", h=MH),
                                                      yo[:, :, :], ALU.add))
                    nc.vector.tensor_tensor(st[:, :, :], Y[0:MS, 2 * P:3 * P].rearrange("n (h w) -> n h w", h=MH),
                                            st2[:, :, :], ALU.add).then_inc(m.y_used, 1)
                    dve.wait_ge(m.link, n2)
                    yc = yz[:, c, 0:HALF_IN]
                    n3 = link(nc.vector.tensor_tensor(yc, yc, y1[:, :, :].rearrange("p h w -> p (h w)"), ALU.add))
                    return n3

                before(0)
                for c in range(NT):
                    if c + 1 < NT:
                        before(c + 1)
                    n = behind(c)
                dve.wait_ge(m.link, n)
                dve.wait_ge(m.conv_in, i * 3 + 3)
                for c in range(NT):
                    last = nc.vector.bn_stats(stat[:, c, :], yz[:, c, :])
                n = link(last)
                dve.wait_ge(m.link, n)
                nc.vector.tensor_tensor(w.mean2[:, :], stat[:, :, 1], stat[:, :, 4], ALU.add)
                nc.vector.tensor_tensor(w.diff[:, :], stat[:, :, 1], stat[:, :, 4], ALU.subtract)
                n = link(nc.vector.tensor_tensor(w.var2[:, :], stat[:, :, 2], stat[:, :, 5], ALU.add))
                dve.wait_ge(m.link, n)
                nc.vector.tensor_tensor(w.diff2[:, :], w.diff[:, :], w.diff[:, :], ALU.mult)
                nc.vector.tensor_scalar(w.mean[:, :], w.mean2[:, :], 0.5, None, ALU.mult)
                n = link(nc.vector.tensor_scalar(w.var[:, :], w.var2[:, :], 0.5 / HALF_IN, EPS, ALU.mult, ALU.add))
                dve.wait_ge(m.link, n)
                nc.vector.scalar_tensor_tensor(out=w.vareps[:, :], in0=w.diff2[:, :], scalar=0.25, in1=w.var[:, :],
                                               op0=ALU.mult, op1=ALU.add).then_inc(m.var, 1)
                dve.wait_ge(m.rstd, i + 1)
                for c in range(NT):
                    nc.vector.tensor_scalar(yn[:, c, :], yz[:, c, :], w.mean[:, c:c + 1], w.rstd[:, c:c + 1],
                                            ALU.subtract, ALU.mult).then_inc(m.scaled, 1)
                for c in range(NT):
                    t = i * NT + c
                    dve.wait_ge(m.out_made, t + 1)
                    Xc = k.X[:, bass.ds(t * D, D)]
                    nc.vector.tensor_tensor(Xc, O[:, 2 * P:3 * P], Xc, ALU.add).then_inc(m.out_added, 1)
                if links[0] != LINKS:
                    raise ValueError(f"LINKS is {links[0]}")

            two_at_a_time(dve, B, body)


INPUTS = ("L0_attn_a_x", "L0_attn_a_Wqkv", "L0_attn_a_bqkv", "L0_attn_a_Wout", "L0_attn_a_bout",
          "L0_attn_a_rel_k_emb", "L0_attn_a_rel_v_emb", "L0_attn_a_alphas_raw", "L0_attn_b_W_in",
          "L0_attn_b_conv_w", "L0_attn_b_conv_b", "L0_attn_b_dt_bias", "L0_attn_b_A_log",
          "L0_attn_b_Dskip", "L0_attn_b_ln_w", "L0_attn_b_ln_b", "L0_attn_b_W_out", "L0_ffn_wg",
          "L0_ffn_W", "L0_ffn_b")


def norm(nc, sem, ctx_sb, ps, k, w, tag):
    s = norm_sems(sem, tag)
    with nc.Block() as block:
        @block.vector
        def _(dve):
            norm_vector(nc, dve, s, w, k.X)

        @block.gpsimd
        def _(pool):
            norm_gpsimd(nc, pool, s, w)

        @block.tensor
        def _(pe):
            norm_tensor(nc, pe, s, w, ps[0:2], k.ident)

        @block.scalar
        def _(act):
            norm_scalar(nc, act, s, ps[0:2], k.XNT)


def store_stream(nc, sem, k, out):
    done = sem("stream_stored")
    with nc.Block() as block:
        @block.sync
        def _(sp):
            sp.dma_start(out.rearrange("b (t p) d -> p (b t) d", p=P),
                         k.X[:, :].rearrange("p (t d) -> p t d", d=D)).then_inc(done, 16)
            sp.wait_ge(done, 16)


def program(nc, a, out, phases=4, start=1):
    with ExitStack() as outer:
        def sem(name):
            return outer.enter_context(nc.semaphore(name))

        def allocate(ctx):
            return lambda name, shape: ctx.enter_context(nc.sbuf_tensor(name, shape, F32))

        ps = [outer.enter_context(nc.psum_tensor(f"bank{q}", [P, 512], F32)) for q in range(8)]
        k = Namespace()
        keep = allocate(outer)
        k.X = keep("stream", [P, TILES * D])
        k.XNT = keep("stream_normed_t", [P, TILES * P])
        k.ident = keep("identity", [P, P])
        k.bout = keep("attention_out_bias", [P, D])
        k.zeros = keep("zeros", [P, 2 * P])
        w = norm_buffers(keep, "norm")
        with ExitStack() as ctx:
            sb = allocate(ctx)
            t = Namespace()
            t.TJf = sb("table_j", [P, PAIRS * J_COLS])
            t.TOf = sb("table_o", [P, PAIRS * O_COLS])
            t.TJ = t.TJf[:, :].rearrange("p (r c) -> p r c", r=PAIRS)
            t.TO = t.TOf[:, :].rearrange("p (r c) -> p r c", r=PAIRS)
            t.XNT = k.XNT
            t.prob = [sb(f"probs_of_tile{T}", [P, 2, PADDED]) for T in range(NT)]
            t.kz = [[sb(f"keys{q}_of_head{h}", [P, N]) for h in range(2)] for q in range(2)]
            t.relk = [sb(f"rel_keys_head{h}", [P, EXT]) for h in range(2)]
            t.relv = sb("rel_values", [P, DH])
            t.r_dram = [nc.dram_tensor(f"rel_scratch{q}", [P * 2 * EXT], F32, kind="Internal") for q in range(2)]
            t.p_dram = [nc.dram_tensor(f"probs_scratch{q}", [P + P * 2 * PITCH], F32, kind="Internal") for q in range(2)]
            with ExitStack() as ctx2:
                set_up(nc, sem, allocate(ctx2), ps, a, k, t)
            norm(nc, sem, keep, ps, k, w, "norm1")
            if start == 1:
                attention(nc, sem, sb, ps, k, t)
        if phases > 1:
            r = Namespace()
            r.we = keep("rest_we", [P, E * D])
            r.wg = keep("rest_wg", [P, E])
            r.eb = keep("rest_eb", [E, D])
            r.before = keep("rest_before", [P, P])
            r.upto = keep("rest_upto", [P, P])
            r.after = keep("rest_after", [P, P])
            r.ones = keep("rest_ones", [P, P])
            r.rank = keep("rest_rank", [P, E])
            r.win = keep("rest_win", [P, 2 * P + 2 * SECOND])
            r.wdt = keep("rest_wdt", [P, MH])
            r.wo = keep("rest_wo", [P, 2, P])
            r.cwx = keep("rest_cwx", [P, CONV])
            r.cwb = keep("rest_cwb", [2 * SECOND, CONV])
            r.cbx = keep("rest_cbx", [P, 1])
            r.cbb = keep("rest_cbb", [2 * SECOND, 1])
            r.cbx2 = keep("rest_cbx2", [P, 1])
            r.cbb2 = keep("rest_cbb2", [2 * SECOND, 1])
            r.dtb = keep("rest_dtb", [P, MH])
            r.A = keep("rest_A", [P, MH])
            r.dskip = keep("rest_dskip", [P, MH])
            r.lnw = keep("rest_lnw", [P, 2])
            r.lnb = keep("rest_lnb", [P, 2])
            with ExitStack() as ctx:
                set_up_rest(nc, sem, allocate(ctx), ps, a, k, r)
            norm(nc, sem, keep, ps, k, w, "norm2")
            if start <= 2:
                with ExitStack() as ctx:
                    experts(nc, sem, allocate(ctx), ps, k, r, "experts1")
            if phases > 2:
                if start < 3:
                    norm(nc, sem, keep, ps, k, w, "norm3")
                with ExitStack() as ctx:
                    mixer(nc, sem, allocate(ctx), ps, k, r)
            if phases > 3:
                norm(nc, sem, keep, ps, k, w, "norm4")
                with ExitStack() as ctx:
                    experts(nc, sem, allocate(ctx), ps, k, r, "experts2")
        store_stream(nc, sem, k, out)


def kernel(**inputs):
    import numpy as _np
    import concourse.bacc as _bacc
    from concourse import mybir as _mybir
    from concourse.bass_utils import run_bass_kernel_spmd as _run

    nc = _bacc.Bacc("TRN2", target_bir_lowering=False, num_devices=1)
    arrays, a = {}, {}
    for name in INPUTS:
        array = _np.ascontiguousarray(inputs[name])
        arrays[f"in_{name}"] = array
        short = name.replace("L0_attn_a_", "").replace("L0_attn_b_", "b_").replace("L0_ffn_", "f_")
        a[short] = nc.dram_tensor(f"in_{name}", array.shape, _mybir.dt.from_np(array.dtype), kind="ExternalInput").ap()
    out = nc.dram_tensor("out_stream", (B, N, D), F32, kind="ExternalOutput").ap()
    program(nc, a, out)
    r = _run(nc, [arrays], core_ids=[0])
    return r.results[0]["out_stream"]
```

```python
from contextlib import ExitStack

import concourse.bass as bass
import concourse.mybir as mybir
from concourse.alu_op_type import AluOpType as ALU

F32 = mybir.dt.float32
ACT = mybir.ActivationFunctionType
AX = mybir.AxisListType

P = 128
B, N, D = 8, 512, 128
NT = N // P
TILES = B * NT
EPS = 1e-5

H, DH, ORDER = 16, 64, 3
PAIRS = H // 2
ITS = B * PAIRS
MAXREL = 64
TOPK = N // 4 // 4
SCALE = DH ** -0.5
HALF = MAXREL
RECT = P + 2 * HALF
EXT = RECT + P - 1
BAND = P + 1
PADDED = N + 2 * HALF
NEG = -3.0e38

J_WQ, J_WK, J_WV, J_BV, J_BQ, J_BK = 0, 128, 256, 384, 512, 513
J_COLS = 514
O_W, O_AL = 0, 128
O_COLS = O_AL + 2 * ORDER


class Namespace:
    pass


def rect_of(T):
    lo, hi = max(0, P * T - HALF), min(N, P * T + P + HALF)
    return lo, hi, lo - (P * T - HALF)


def bcast(ap, dims):
    return bass.AP(ap.tensor, ap.offset, [list(ap.ap[0])] + [list(d) for d in dims])


def two_at_a_time(eng, count, body, with_half=False):
    for k in range(2):
        body(k, k, True, *([0] if with_half else []))
    with eng.Fori(1, count // 2) as g:
        for k in range(2):
            body(g * 2 + k, k, False, *([g] if with_half else []))


GROUPS = TILES // 4


def norm_sems(sem, tag):
    s = Namespace()
    s.before = 0
    s.stats, s.chain, s.var, s.rstd = (sem(f"{tag}_{n}") for n in ("stats", "chain", "var", "rstd"))
    s.scaled, s.transposed, s.stored = (sem(f"{tag}_{n}") for n in ("scaled", "transposed", "stored"))
    return s


def norm_buffers(sb, tag):
    w = Namespace()
    w.stats = sb(f"{tag}_stats", [P, TILES * 6])
    w.mean2 = sb(f"{tag}_mean2", [P, TILES])
    w.diff = sb(f"{tag}_diff", [P, TILES])
    w.diff2 = sb(f"{tag}_diff2", [P, TILES])
    w.var2 = sb(f"{tag}_var2", [P, TILES])
    w.mean = sb(f"{tag}_mean", [P, TILES])
    w.var = sb(f"{tag}_var", [P, TILES])
    w.vareps = sb(f"{tag}_vareps", [P, TILES])
    w.rstd = sb(f"{tag}_rstd", [P, TILES])
    w.mhalf = sb(f"{tag}_mhalf", [P, TILES])
    w.xn = sb(f"{tag}_xn", [P, 2, 4 * D])
    return w


NORM_PARTS = 2
PART = TILES // NORM_PARTS


def norm_vector(nc, dve, s, w, X):
    nc.vector.memset(w.mhalf[:, :], -0.5)
    st = w.stats[:, :].rearrange("p (t s) -> p t s", s=6)
    steps = PART // 8
    for part in range(NORM_PARTS):
        r = slice(part * PART, (part + 1) * PART)
        with dve.Fori(part * steps, (part + 1) * steps) as g:
            for k in range(8):
                last = nc.vector.bn_stats(w.stats[:, bass.ds(g * 48 + k * 6, 6)], X[:, bass.ds((g * 8 + k) * D, D)])
            last.then_inc(s.stats, 1)
        dve.wait_ge(s.stats, s.before * NORM_PARTS * steps + (part + 1) * steps)
        nc.vector.tensor_tensor(w.mean2[:, r], st[:, r, 1], st[:, r, 4], ALU.add)
        nc.vector.tensor_tensor(w.diff[:, r], st[:, r, 1], st[:, r, 4], ALU.subtract)
        nc.vector.tensor_tensor(w.var2[:, r], st[:, r, 2], st[:, r, 5], ALU.add).then_inc(s.chain, 1)
        dve.wait_ge(s.chain, 2 * (s.before * NORM_PARTS + part) + 1)
        nc.vector.tensor_tensor(w.diff2[:, r], w.diff[:, r], w.diff[:, r], ALU.mult)
        nc.vector.tensor_scalar(w.mean[:, r], w.mean2[:, r], 0.5, None, ALU.mult)
        nc.vector.tensor_scalar(w.var[:, r], w.var2[:, r], 1.0 / D, EPS, ALU.mult, ALU.add).then_inc(s.chain, 1)
        dve.wait_ge(s.chain, 2 * (s.before * NORM_PARTS + part) + 2)
        nc.vector.scalar_tensor_tensor(out=w.vareps[:, r], in0=w.diff2[:, r], scalar=0.25, in1=w.var[:, r],
                                       op0=ALU.mult, op1=ALU.add).then_inc(s.var, 1)

    def scale(i, par, first):
        if not first:
            dve.wait_ge(s.transposed, s.before * GROUPS + i - 1)
        for k in range(4):
            last = nc.vector.tensor_scalar(w.xn[:, par, k * D:(k + 1) * D],
                                           X[:, bass.ds((i * 4 + k) * D, D)],
                                           w.mean[:, bass.ds(i * 4 + k, 1)], w.rstd[:, bass.ds(i * 4 + k, 1)],
                                           ALU.subtract, ALU.mult)
        last.then_inc(s.scaled, 1)

    of_part = PART // 4
    dve.wait_ge(s.rstd, s.before * NORM_PARTS + 1)
    for i in range(of_part):
        scale(i, i % 2, i < 2)
    dve.wait_ge(s.rstd, (s.before + 1) * NORM_PARTS)
    with dve.Fori(of_part // 2, GROUPS // 2) as g:
        for k in range(2):
            scale(g * 2 + k, k, False)


def norm_gpsimd(nc, pool, s, w):
    for part in range(NORM_PARTS):
        r = slice(part * PART, (part + 1) * PART)
        pool.wait_ge(s.var, s.before * NORM_PARTS + part + 1)
        nc.gpsimd.tensor_tensor(w.rstd[:, r], w.vareps[:, r], w.mhalf[:, r], ALU.pow).then_inc(s.rstd, 1)


def norm_tensor(nc, pe, s, w, banks, ident):
    def transpose(i, par, first):
        pe.wait_ge(s.scaled, s.before * GROUPS + i + 1)
        if not first:
            pe.wait_ge(s.stored, s.before * GROUPS + i - 1)
        for k in range(4):
            last = nc.tensor.transpose(banks[par][:, k * P:(k + 1) * P], w.xn[:, par, k * D:(k + 1) * D],
                                       ident[:, :])
        last.then_inc(s.transposed, 1)

    two_at_a_time(pe, GROUPS, transpose)


def norm_scalar(nc, act, s, banks, XNT):
    def store(i, par, first):
        act.wait_ge(s.transposed, s.before * GROUPS + i + 1)
        nc.scalar.activation(XNT[:, bass.ds(i * 4 * P, 4 * P)], banks[par][:, :], ACT.Copy).then_inc(s.stored, 1)

    two_at_a_time(act, GROUPS, store)


def set_up(nc, sem, sb, ps, a, k, t, wr, r):
    x_in, w_in, consts, turned, kept, chain = (sem(f"setup_{n}") for n in
                                               ("x_in", "w_in", "consts", "turned", "kept", "chain"))
    wqkv = sb("wqkv_rows", [P, 24, D])
    wout = sb("wout_rows", [P, H * DH])
    relk = sb("relk_rows", [P, 2 * DH])
    relk0 = sb("relk0_col", [P, 1])
    relv = sb("relv_rows", [P, DH])
    relv0 = sb("relv0_all", [P, DH])
    bqk = sb("bqk_rows", [16, P])
    bv = sb("bv_all", [P, H * DH])
    al = sb("alphas_all", [P, ORDER * H])
    al1 = sb("alphas_e", [P, ORDER * H])
    al2 = sb("alphas_d", [P, ORDER * H])
    relv_turned = sb("relv_turned", [P, DH])
    anti = sb("anti_identity", [P, P])
    zeros = k.zeros
    LOADS = 12

    with nc.Block() as block:
        @block.sync
        def _(sp):
            xv = a["x"].rearrange("b (t p) d -> p (b t) d", p=P)
            Xv = k.X[:, :].rearrange("p (t d) -> p t d", d=D)
            for q in range(4):
                sp.dma_start(Xv[:, q * 8:(q + 1) * 8, :], xv[:, q * 8:(q + 1) * 8, :]).then_inc(x_in, 16)
            sp.wait_ge(consts, 1)
            for q in range(2):
                rows = bass.AP(t.p_dram[q], P + RECT, [[2 * PITCH, P], [PITCH, 2], [1, P]])
                sp.dma_start(rows, zeros[:, 0:2 * P].rearrange("p (h c) -> p h c", h=2)).then_inc(x_in, 16)
                sp.dma_start(bass.AP(t.p_dram[q], 0, [[P, 1], [1, P]]), zeros[0:1, 0:P]).then_inc(x_in, 16)
            sp.wait_ge(x_in, 16 * 8)

        @block.gpsimd
        def _(pool):
            nc.gpsimd.memset(zeros[:, :], 0.0).then_inc(consts, 1)
            nc.gpsimd.memset(k.ident[:, :], 0.0)
            nc.gpsimd.memset(anti[:, :], 0.0).then_inc(consts, 1)
            pool.wait_ge(consts, 2)
            nc.gpsimd.affine_select(out=k.ident[:, :], in_=k.ident[:, :], compare_op=ALU.not_equal, fill=1.0,
                                    base=0, pattern=[[-1, P]], channel_multiplier=1)
            nc.gpsimd.affine_select(out=anti[:, :], in_=anti[:, :], compare_op=ALU.not_equal, fill=1.0,
                                    base=-(P - 1), pattern=[[1, P]], channel_multiplier=1).then_inc(consts, 1)

        @block.scalar
        def _(act):
            act.dma_start(wqkv[:, :, :], a["Wqkv"].rearrange("(c p) d -> p c d", p=P)).then_inc(w_in, 16)
            act.dma_start(wout[:, :], a["Wout"]).then_inc(w_in, 16)
            for s in range(2):
                act.dma_start(relk[:, s * DH:(s + 1) * DH], a["rel_k_emb"][1:2 * MAXREL + 1, :]).then_inc(w_in, 16)
                with nc.allow_non_contiguous_dma(reason="64 values, once"):
                    act.dma_start(relk0[s * DH:(s + 1) * DH, :],
                                  a["rel_k_emb"][0:1, :].rearrange("o d -> d o")).then_inc(w_in, 16)
            act.dma_start(relv[:, :], a["rel_v_emb"][1:2 * MAXREL + 1, :]).then_inc(w_in, 16)
            act.dma_start(relv0[:, :], a["rel_v_emb"][0:1, :].to_broadcast([P, DH])).then_inc(w_in, 16)
            act.dma_start(bqk[:, :], a["bqkv"][0:2 * H * DH].rearrange("(c p) -> c p", p=P)).then_inc(w_in, 16)
            act.dma_start(bv[:, :], a["bqkv"][2 * H * DH:].rearrange("(o n) -> o n", o=1)
                          .to_broadcast([P, H * DH])).then_inc(w_in, 16)
            act.dma_start(al[:, :], a["alphas_raw"].rearrange("(o k) h -> o (k h)", o=1)
                          .to_broadcast([P, ORDER * H])).then_inc(w_in, 16)
            act.dma_start(k.bout[:, :], a["bout"].rearrange("(o n) -> o n", o=1)
                          .to_broadcast([P, D])).then_inc(w_in, 16)
            act.wait_ge(w_in, 16 * LOADS)
            nc.scalar.activation(al1[:, :], al[:, :], ACT.Exp, scale=-1.0).then_inc(chain, 1)
            for g in range(8):
                act.wait_ge(turned, g + 1)
                which, half = divmod(g, 2)
                if which < 3:
                    to = t.TJ[:, 4 * half:4 * half + 4, which * P:(which + 1) * P]
                else:
                    to = t.TO[:, 4 * half:4 * half + 4, 0:P]
                nc.scalar.activation(to, ps[g % 4][:, :].rearrange("p (c n) -> p c n", c=4), ACT.Copy).then_inc(kept, 1)

        @block.tensor
        def _(pe):
            pe.wait_ge(consts, 3)
            pe.wait_ge(w_in, 16 * LOADS)
            for g in range(8):
                if g >= 4:
                    pe.wait_ge(kept, g - 3)
                for c in range(4):
                    src = wqkv[:, g * 4 + c, :] if g < 6 else wout[:, ((g - 6) * 4 + c) * P:((g - 6) * 4 + c + 1) * P]
                    last = nc.tensor.transpose(ps[g % 4][:, c * P:(c + 1) * P], src, k.ident[:, :])
                last.then_inc(turned, 1)
            nc.tensor.transpose(ps[4][:, 0:16], bqk[:, :], k.ident[0:16, 0:16])
            nc.tensor.transpose(ps[5][:, 0:P], relk[:, :], anti[:, :])
            nc.tensor.matmul(ps[6][:, 0:DH], anti[:, :], relv[:, :], start=True, stop=True).then_inc(turned, 1)

        @block.vector
        def _(dve):
            nc.vector.memset(wr.bc[:, :], 0.0)
            nc.vector.memset(r.cwb[:, :], 0.0)
            nc.vector.memset(r.cbb[:, :], 0.0)
            for T in range(NT):
                nc.vector.memset(t.prob[T][:, :, 0:HALF], 0.0)
                nc.vector.memset(t.prob[T][:, :, HALF + N:PADDED], 0.0)
            for par in range(2):
                nc.vector.memset(t.kz[par][0][DH:P, :], 0.0)
                nc.vector.memset(t.kz[par][1][0:DH, :], 0.0)
            nc.vector.memset(t.relk[DH:P, 0, :], 0.0)
            nc.vector.memset(t.relk[0:DH, 1, :], 0.0)
            dve.wait_ge(w_in, 16 * LOADS)
            dve.wait_ge(chain, 1)
            nc.vector.tensor_scalar(al2[:, :], al1[:, :], 1.0, None, ALU.add).then_inc(chain, 1)
            dve.wait_ge(chain, 2)
            nc.vector.reciprocal(al[:, :], al2[:, :]).then_inc(chain, 1)
            dve.wait_ge(chain, 3)
            nc.vector.tensor_copy(t.TO[:, :, O_AL:O_AL + 2 * ORDER].rearrange("p r (k s) -> p r k s", k=ORDER),
                                  al[:, :].rearrange("p (k r s) -> p r k s", k=ORDER, s=2))
            nc.vector.tensor_tensor(t.TJ[:, :, J_BV:J_BV + P].rearrange("p r (s d) -> p r s d", s=2),
                                    bv[:, :].rearrange("p (r s d) -> p r s d", s=2, d=DH),
                                    bcast(relv0[:, :], [[0, PAIRS], [0, 2], [1, DH]]), ALU.add)
            dve.wait_ge(turned, 9)
            nc.vector.tensor_copy(t.TJ[:, :, J_BQ:J_BQ + 1].rearrange("p r o -> p (r o)"), ps[4][:, 0:PAIRS])
            nc.vector.tensor_scalar(t.TJ[:, :, J_BK:J_BK + 1].rearrange("p r o -> p (r o)"), ps[4][:, PAIRS:2 * PAIRS],
                                    SCALE, None, ALU.mult)
            for s in range(2):
                half = slice(s * DH, (s + 1) * DH)
                nc.vector.tensor_copy(t.relk[half, s, 0:P], ps[5][half, 0:P])
                nc.vector.tensor_copy(t.relk[half, s, P:BAND], relk0[half, 0:1])
            nc.vector.tensor_copy(relv_turned[:, :], ps[6][:, 0:DH]).then_inc(chain, 1)
            dve.wait_ge(chain, 4)
            nc.vector.tensor_tensor(t.relv[:, :], relv_turned[:, :], relv0[:, :], ALU.subtract)


PITCH = RECT + P


class Slots:

    def __init__(self, g, par, T):
        self.g, self.par, self.i, self.T = g, par, g * 2 + par, T

    def half(self, d):
        return self.g + (self.par + d) // 2

    def back(self, slots):
        q, T = divmod(self.T - slots, NT)
        it = self.i + q
        if isinstance(it, int) and not 0 <= it < ITS:
            return None
        return it, T, it * NT + T

    def iteration(self, d):
        it = self.i + d
        if isinstance(it, int) and not 0 <= it < ITS:
            return None
        return it


def early(value):
    return isinstance(value, int) and value <= 0


def known(eng, *values):
    for value in values:
        if not isinstance(value, int):
            eng.compute_val(value)
    return values


def run_iterations(eng, body):
    first, last = 4, ITS - 2
    for i in range(-1, first):
        for T in range(NT):
            body(Slots(i // 2, i % 2, T), i % 2)
    with eng.Fori(first // 2, last // 2) as g:
        for par in range(2):
            for T in range(NT):
                body(Slots(g, par, T), par)
    for i in range(last, ITS + 3):
        for T in range(NT):
            body(Slots(i // 2, i % 2, T), i % 2)


def attention(nc, sem, sb, ps, k, t):
    s = Namespace()
    s.q_made = sem("att_q_made")
    s.k_made = sem("att_k_made")
    s.v_made = sem("att_v_made")
    s.q_kept = sem("att_q_kept")
    s.k_kept = sem("att_k_kept")
    s.v_kept = sem("att_v_kept")
    s.v_ready = sem("att_v_ready")
    s.rel_made = sem("att_rel_made")
    s.rel_kept = sem("att_rel_kept")
    s.scores_made = sem("att_scores_made")
    s.scores_kept = sem("att_scores_kept")
    s.tops = sem("att_tops")
    s.maxes = sem("att_maxes")
    s.exps = sem("att_exps")
    s.probs = [sem(f"att_probs_of_head{h}") for h in range(2)]
    s.at_least = sem("att_at_least")
    s.row_sums = sem("att_row_sums")
    s.probs_turned = sem("att_probs_turned")
    s.probs_kept = sem("att_probs_kept")
    s.sums = sem("att_sums")
    s.band_closed = sem("att_band_closed")
    s.band_turned = sem("att_band_turned")
    s.band_kept = sem("att_band_kept")
    s.mixed = sem("att_mixed")
    s.mixed_kept = sem("att_mixed_kept")
    s.mixed_turned = sem("att_mixed_turned")
    s.raw_kept = sem("att_raw_kept")
    s.inverse = sem("att_inverse")
    s.values_next = sem("att_values_next")
    s.res_chain = sem("att_res_chain")
    s.res_turned = sem("att_res_turned")
    s.res_kept = sem("att_res_kept")
    s.out_made = sem("att_out_made")
    s.out_added = sem("att_out_added")
    s.next_tops = sem("att_next_tops")
    s.shortened = sem("att_shortened")
    s.bias_added = sem("att_bias_added")
    s.pj_in = [sem(f"att_pj_in{q}") for q in range(2)]
    s.po_in = [sem(f"att_po_in{q}") for q in range(2)]
    s.rel_stored = [sem(f"att_rel_stored{q}") for q in range(2)]
    s.rel_in = [sem(f"att_rel_in{q}") for q in range(2)]
    s.probs_stored = [sem(f"att_probs_stored{q}") for q in range(2)]
    s.band_in = [sem(f"att_band_in{q}") for q in range(2)]

    def two(name, shape):
        return [sb(f"{name}{q}", shape) for q in range(2)]

    pj = two("pair_j", [P, J_COLS])
    po = two("pair_o", [P, O_COLS])
    xt = two("xt", [P, N])
    qt = two("qt", [P, N])
    v = two("v", [P, NT, P])
    vraw = sb("vraw", [P, NT, P])
    rel = two("rel", [P, 2, EXT])
    relj = two("relj", [P, 2, RECT])
    sc = two("scores", [P, 2, N])
    work = sb("work", [P, 2, N])
    top = two("top", [P, 2, TOPK])
    nmax = two("nmax", [P, 2])
    ex = two("exps", [P, 2, N])
    kept = sb("kept", [P, N])
    rs = two("row_sums", [P, 2 * NT])
    inv = two("inverse", [P, 2 * NT])
    band = two("band", [P, 2, RECT])
    la = two("left_a", [P, 2])
    lb = two("left_b", [P, 2])
    pt = two("probs_t", [P, 2, NT, N])
    bt = two("band_t", [P, 2, N])
    mixed = sb("mixed", [P, N])
    raw = sb("raw", [P, NT, 2, DH])
    u = sb("u", [P, NT, 2, DH])
    tmp = sb("tmp", [P, NT, 2, DH])
    res = sb("res", [P, NT, 2, DH])
    rest = sb("rest", [P, N])
    SC, RL, PT, U, MISC = ps[0:2], ps[2:4], ps[4:6], ps[6], ps[7]

    with nc.Block() as block:
        @block.sync
        def _(sp):
            def body(z, par):
                T, q = z.T, z.T % 2
                if T == 0 and (it := z.iteration(1)) is not None:
                    at_pair, at_batch = known(sp, (it % PAIRS) * J_COLS, (it // PAIRS) * N)
                    c0 = known(sp, it - 1)[0]
                    if not early(c0):
                        sp.wait_ge(s.v_ready, c0)
                    sp.dma_start(pj[1 - par][:, :], t.TJf[:, bass.ds(at_pair, J_COLS)]).then_inc(s.pj_in[1 - par], 16)
                    sp.dma_start(xt[1 - par][:, :], t.XNT[:, bass.ds(at_batch, N)]).then_inc(s.pj_in[1 - par], 16)
                if T == 2 and (it := z.iteration(-1)) is not None:
                    at_out, = known(sp, (it % PAIRS) * O_COLS)
                    c0 = known(sp, it - 1)[0]
                    if not early(c0):
                        sp.wait_ge(s.out_made, c0)
                    sp.dma_start(po[1 - par][:, :], t.TOf[:, bass.ds(at_out, O_COLS)]).then_inc(s.po_in[1 - par], 16)
                d, a = z.back(4), z.back(0)
                if d:
                    it, Td, n = d
                    qd = Td % 2
                    c0, c1 = known(sp, n + 1, 16 * (it * 2 + Td // 2))
                    for h in range(2):
                        sp.wait_ge(s.probs[h], c0)
                    if not early(c1):
                        sp.wait_ge(s.band_in[qd], c1)
                    sp.dma_start(bass.AP(t.p_dram[qd], P, [[2 * PITCH, P], [PITCH, 2], [1, RECT]]),
                                 t.prob[Td][:, :, P * Td:P * Td + RECT]).then_inc(s.probs_stored[qd], 16)
                if a:
                    it, Ta, n = a
                    c0, c1 = known(sp, n + 1, 16 * (it * 2 + Ta // 2))
                    sp.wait_ge(s.rel_kept, c0)
                    if not early(c1):
                        sp.wait_ge(s.rel_in[q], c1)
                    sp.dma_start(bass.AP(t.r_dram[q], 0, [[2 * EXT, P], [EXT, 2], [1, EXT]]),
                                 rel[q][:, :, :]).then_inc(s.rel_stored[q], 16)
                if d:
                    it, Td, n = d
                    qd = Td % 2
                    c0, c1 = known(sp, 16 * (it * 2 + Td // 2 + 1), n - 1)
                    sp.wait_ge(s.probs_stored[qd], c0)
                    if not early(c1):
                        sp.wait_ge(s.band_turned, c1)
                    sp.dma_start(band[qd][:, :, :],
                                 bass.AP(t.p_dram[qd], 0, [[2 * PITCH + 1, P], [PITCH, 2], [1, RECT]]))\
                        .then_inc(s.band_in[qd], 16)
                if a:
                    it, Ta, n = a
                    c0, c1 = known(sp, 16 * (it * 2 + Ta // 2 + 1), 2 * n - 2)
                    sp.wait_ge(s.rel_stored[q], c0)
                    if not early(c1):
                        sp.wait_ge(s.scores_made, c1)
                    sp.dma_start(relj[q][:, :, :],
                                 bass.AP(t.r_dram[q], P - 1, [[2 * EXT - 1, P], [EXT, 2], [1, RECT]]))\
                        .then_inc(s.rel_in[q], 16)

            run_iterations(sp, body)
            for q in range(2):
                sp.wait_ge(s.rel_stored[q], 16 * ITS * 2)
                sp.wait_ge(s.probs_stored[q], 16 * ITS * 2)

        @block.tensor
        def _(pe):
            def body(z, par):
                T = z.T
                old, av, cur, nxt = z.iteration(-3), z.iteration(-2), z.iteration(0), z.iteration(1)
                def mix(it, values):
                    if not early(it * ORDER + T):
                        pe.wait_ge(s.mixed_kept, it * ORDER + T)
                    for jt in range(NT):
                        for h in range(2):
                            lhs = values[:, jt, h * DH:(h + 1) * DH] if T == 0 else values[:, jt, h, :]
                            last = nc.tensor.matmul(U[h * DH:(h + 1) * DH, :], lhs, pt[par][:, h, jt, :],
                                                    start=(jt == 0), stop=(jt == NT - 1 and T > 0))
                    return last

                b = z.back(2)
                if b:
                    it, Tb, n = b
                    q = Tb % 2
                    bpar = par if T >= 2 else 1 - par
                    lo, hi, at = rect_of(Tb)
                    pe.wait_ge(s.k_kept, it + 1)
                    for h in range(2):
                        if not early(2 * n + h - 1):
                            pe.wait_ge(s.scores_kept, 2 * n + h - 1)
                        nc.tensor.matmul(SC[h][:, :], qt[bpar][:, Tb * P:(Tb + 1) * P], t.kz[bpar][h][:, :],
                                         start=True, stop=False)
                        if h == 0:
                            pe.wait_ge(s.rel_in[q], 16 * (it * 2 + Tb // 2 + 1))
                        nc.tensor.matmul(SC[h][:, lo:hi], k.ident[:, :], relj[q][:, h, at:at + hi - lo],
                                         start=False, stop=True).then_inc(s.scores_made, 1)
                a = z.back(0)
                if a:
                    it, Ta, n = a
                    pe.wait_ge(s.q_kept, it + 1)
                    if not early(n - 1):
                        pe.wait_ge(s.rel_kept, n - 1)
                    nc.tensor.matmul(RL[T % 2][:, 0:2 * BAND], qt[par][:, Ta * P:(Ta + 1) * P],
                                     t.relk[:, :, :].rearrange("p h c -> p (h c)"),
                                     start=True, stop=True).then_inc(s.rel_made, 1)
                if old is not None and T == 0:
                    pe.wait_ge(s.res_chain, old * 5 + 5)
                    if cur is not None:
                        pe.wait_ge(s.k_kept, cur + 1)
                    for jt in range(NT):
                        last = nc.tensor.transpose(MISC[:, jt * P:(jt + 1) * P],
                                                   res[:, jt, :, :].rearrange("p h d -> p (h d)"), k.ident[:, :])
                    last.then_inc(s.res_turned, 1)
                if av is not None and T > 0:
                    pe.wait_ge(s.mixed_kept, av * ORDER + T)
                    if T == 1 and not early(av):
                        pe.wait_ge(s.out_added, av)
                    if T == 1 and cur is not None:
                        pe.wait_ge(s.k_kept, cur + 1)
                    if T == 2:
                        if cur is not None:
                            pe.wait_ge(s.v_kept, cur + 1)
                        else:
                            pe.wait_ge(s.raw_kept, av * ORDER + 1)
                    if T == 3:
                        if nxt is not None:
                            pe.wait_ge(s.q_kept, nxt + 1)
                        else:
                            pe.wait_ge(s.raw_kept, av * ORDER + 2)
                    for jt in range(NT):
                        last = nc.tensor.transpose(MISC[:, jt * P:(jt + 1) * P], mixed[:, jt * P:(jt + 1) * P],
                                                   k.ident[:, :])
                    last.then_inc(s.mixed_turned, 1)
                if av is not None and T == 0:
                    pe.wait_ge(s.probs_kept, (av + 1) * 2 * NT)
                    pe.wait_ge(s.v_ready, av + 1)
                    mix(av, v[par])
                d = z.back(4)
                if d:
                    it, Td, n = d
                    for h in range(2):
                        pe.wait_ge(s.probs[h], n + 1)
                        if h == 0 and not early(n - 1):
                            pe.wait_ge(s.band_kept, n - 1)
                        elif h == 0 and n > 0:
                            pe.wait_ge(s.probs_kept, 2 * n - 1)
                        if h == 1 and not early(2 * n):
                            pe.wait_ge(s.probs_kept, 2 * n)
                        for jt in range(NT):
                            last = nc.tensor.transpose(PT[h][:, jt * P:(jt + 1) * P],
                                                       t.prob[Td][:, h, HALF + jt * P:HALF + (jt + 1) * P],
                                                       k.ident[:, :])
                        last.then_inc(s.probs_turned, 1)
                if old is not None and T == 0:
                    pe.wait_ge(s.res_kept, old + 1)
                    pe.wait_ge(s.po_in[1 - par], 16 * (z.half(-3) + 1))
                    for jt in range(NT):
                        last = nc.tensor.matmul(MISC[:, jt * P:(jt + 1) * P], rest[:, jt * P:(jt + 1) * P],
                                                po[1 - par][:, O_W:O_W + P], start=True, stop=True)
                    last.then_inc(s.out_made, 1)
                if T == 1 and cur is not None:
                    pe.wait_ge(s.k_kept, cur + 1)
                    if av is not None:
                        pe.wait_ge(s.raw_kept, av * ORDER + 1)
                    for jt in range(NT):
                        last = nc.tensor.matmul(MISC[:, jt * P:(jt + 1) * P], xt[par][:, jt * P:(jt + 1) * P],
                                                pj[par][:, J_WV:J_WV + P], start=True, stop=True)
                    last.then_inc(s.v_made, 1)
                if T == 2 and nxt is not None:
                    pe.wait_ge(s.pj_in[1 - par], 32 * (z.half(1) + 1))
                    if av is not None:
                        pe.wait_ge(s.raw_kept, av * ORDER + 2)
                    elif cur is not None:
                        pe.wait_ge(s.v_kept, cur + 1)
                    nc.tensor.matmul(MISC[:, :], pj[1 - par][:, J_WQ:J_WQ + P], xt[1 - par][:, :],
                                     start=True, stop=True).then_inc(s.q_made, 1)
                if T == 3 and nxt is not None:
                    pe.wait_ge(s.q_kept, nxt + 1)
                    if av is not None:
                        pe.wait_ge(s.raw_kept, av * ORDER + 3)
                    nc.tensor.matmul(MISC[:, :], pj[1 - par][:, J_WK:J_WK + P], xt[1 - par][:, :],
                                     start=True, stop=True).then_inc(s.k_made, 1)
                e = z.back(5)
                if e:
                    it, Te, n = e
                    q = Te % 2
                    pe.wait_ge(s.band_closed, n + 1)
                    if d:
                        pe.wait_ge(s.probs_kept, 2 * (n + 1) + 1)
                    elif not early(n):
                        pe.wait_ge(s.band_kept, n)
                    for h in range(2):
                        last = nc.tensor.transpose(PT[0][:, h * P:(h + 1) * P], band[q][:, h, P:2 * P], k.ident[:, :])
                    last.then_inc(s.band_turned, 1)
                if av is not None and T in (1, 2):
                    pe.wait_ge(s.values_next, av * ORDER + T)
                    last = mix(av, u)
                    last.then_inc(s.mixed, 1)
                if av is not None and T == 0:
                    pe.wait_ge(s.band_kept, (av + 1) * NT)
                    for h in range(2):
                        last = nc.tensor.matmul(U[h * DH:(h + 1) * DH, :], t.relv[:, :], bt[par][:, h, :],
                                                start=False, stop=True)
                    last.then_inc(s.mixed, 1)

            run_iterations(pe, body)

        @block.scalar
        def _(act):
            def body(z, par):
                T, sp2 = z.T, z.T % 2
                old, av, cur, nxt = z.iteration(-3), z.iteration(-2), z.iteration(0), z.iteration(1)
                if av is not None and T > 0:
                    act.wait_ge(s.mixed, av * ORDER + T)
                    if not early(av * ORDER + T - 1):
                        act.wait_ge(s.mixed_turned, av * ORDER + T - 1)
                    nc.scalar.activation(mixed[:, :], U[:, :], ACT.Copy).then_inc(s.mixed_kept, 1)
                e = z.back(5)
                if e:
                    it, Te, n = e
                    q = Te % 2
                    act.wait_ge(s.band_in[q], 16 * (it * 2 + Te // 2 + 1))
                    act.wait_ge(s.row_sums, n + 1)
                    for h in range(2):
                        last = nc.scalar.activation(band[q][:, h, 0:P + 1], band[q][:, h, 0:P + 1], ACT.Copy,
                                                    accum_out=la[q][:, h:h + 1])
                        if Te > 0:
                            far = t.prob[Te][:, h, HALF:P * Te]
                            last = nc.scalar.activation(far, far, ACT.Copy, accum_out=lb[q][:, h:h + 1])
                    last.then_inc(s.sums, 1)
                    act.wait_ge(s.sums, n + 1)
                    for h in range(2):
                        if Te > 0:
                            last = nc.scalar.activation(band[q][:, h, P:P + 1], la[q][:, h:h + 1], ACT.Identity,
                                                        bias=lb[q][:, h:h + 1])
                        else:
                            last = nc.scalar.activation(band[q][:, h, P:P + 1], la[q][:, h:h + 1], ACT.Copy)
                    last.then_inc(s.band_closed, 1)
                b = z.back(2)
                if b:
                    it, Tb, n = b
                    q = Tb % 2
                    lo, hi, _ = rect_of(Tb)
                    act.wait_ge(s.rel_kept, n + 1)
                    for h in range(2):
                        act.wait_ge(s.scores_made, 2 * n + h + 1)
                        if not early(n - 1):
                            act.wait_ge(s.probs[h], n - 1)
                        last = nc.scalar.activation(sc[q][:, h, lo:hi], SC[h][:, lo:hi], ACT.Copy)
                        if lo > 0:
                            last = nc.scalar.activation(sc[q][:, h, 0:lo], SC[h][:, 0:lo], ACT.Identity,
                                                        bias=rel[q][:, h, 0:1])
                        if hi < N:
                            last = nc.scalar.activation(sc[q][:, h, hi:N], SC[h][:, hi:N], ACT.Identity,
                                                        bias=rel[q][:, h, EXT - 1:EXT])
                        last.then_inc(s.scores_kept, 1)
                if old is not None and T == 0:
                    act.wait_ge(s.res_turned, old + 1)
                    if not early(old):
                        act.wait_ge(s.out_made, old)
                    nc.scalar.activation(rest[:, :], MISC[:, :], ACT.Copy).then_inc(s.res_kept, 1)
                if av is not None and T > 0:
                    act.wait_ge(s.mixed_turned, av * ORDER + T)
                    if not early(av * ORDER + T - 1):
                        act.wait_ge(s.values_next, av * ORDER + T - 1)
                    nc.scalar.activation(raw[:, :, :, :].rearrange("p j h d -> p (j h d)"), MISC[:, :],
                                         ACT.Copy).then_inc(s.raw_kept, 1)
                d = z.back(4)
                if d:
                    it, Td, n = d
                    dpar = 1 - par
                    if Td == 0 and not early((it - 1) * ORDER):
                        act.wait_ge(s.mixed, (it - 1) * ORDER)
                    for h in range(2):
                        act.wait_ge(s.probs_turned, 2 * n + h + 1)
                        nc.scalar.activation(pt[dpar][:, h, :, Td * P:(Td + 1) * P],
                                             PT[h][:, :].rearrange("p (j i) -> p j i", j=NT),
                                             ACT.Copy).then_inc(s.probs_kept, 1)
                a = z.back(0)
                if a:
                    it, Ta, n = a
                    if not early(it * 2 + Ta // 2):
                        act.wait_ge(s.rel_stored[sp2], 16 * (it * 2 + Ta // 2))
                    if not early(2 * n - 2):
                        act.wait_ge(s.scores_kept, 2 * n - 2)
                    act.wait_ge(s.rel_made, n + 1)
                    made = RL[sp2][:, :]
                    nc.scalar.activation(rel[sp2][:, :, P - 1:2 * P], bcast(made, [[BAND, 2], [1, BAND]]), ACT.Copy)
                    nc.scalar.activation(rel[sp2][:, :, 0:P - 1], bcast(made, [[BAND, 2], [0, P - 1]]), ACT.Copy)
                    nc.scalar.activation(rel[sp2][:, :, 2 * P:EXT],
                                         bcast(RL[sp2][:, P:P + 1], [[BAND, 2], [0, EXT - 2 * P]]),
                                         ACT.Copy).then_inc(s.rel_kept, 1)
                c = z.back(3)
                if c:
                    it, Tc, n = c
                    q = Tc % 2
                    act.wait_ge(s.tops, 2 * n + 2)
                    nc.scalar.activation(nmax[q][:, :], top[q][:, :, 0], ACT.Copy, scale=-1.0).then_inc(s.maxes, 1)
                    act.wait_ge(s.maxes, n + 1)
                    for h in range(2):
                        if not early(n - 1):
                            act.wait_ge(s.probs[h], n - 1)
                        if h == 1 and not early(n - 1):
                            act.wait_ge(s.row_sums, n - 1)
                        nc.scalar.activation(ex[q][:, h, :], sc[q][:, h, :], ACT.Exp,
                                             bias=nmax[q][:, h:h + 1]).then_inc(s.exps, 1)
                if e:
                    it, Te, n = e
                    epar = 1 - par if T > 0 else par
                    if Te == 0 and not early((it - 1) * ORDER):
                        act.wait_ge(s.mixed, (it - 1) * ORDER)
                    act.wait_ge(s.band_turned, n + 1)
                    nc.scalar.activation(bt[epar][:, :, Te * P:(Te + 1) * P],
                                         PT[0][:, 0:2 * P].rearrange("p (h i) -> p h i", h=2),
                                         ACT.Copy).then_inc(s.band_kept, 1)
                if T == 1 and cur is not None:
                    act.wait_ge(s.v_made, cur + 1)
                    if not early(cur):
                        act.wait_ge(s.v_ready, cur)
                    nc.scalar.activation(vraw[:, :, :].rearrange("p j n -> p (j n)"), MISC[:, :],
                                         ACT.Copy).then_inc(s.v_kept, 1)
                if T == 2 and nxt is not None:
                    act.wait_ge(s.q_made, nxt + 1)
                    nc.scalar.activation(qt[1 - par][:, :], MISC[:, :], ACT.Identity,
                                         bias=pj[1 - par][:, J_BQ:J_BQ + 1]).then_inc(s.q_kept, 1)
                if T == 3 and nxt is not None:
                    act.wait_ge(s.k_made, nxt + 1)
                    for h in range(2):
                        r = slice(h * DH, (h + 1) * DH)
                        last = nc.scalar.activation(t.kz[1 - par][h][r, :], MISC[r, :], ACT.Identity, scale=SCALE,
                                                    bias=pj[1 - par][r, J_BK:J_BK + 1])
                    last.then_inc(s.k_kept, 1)
                if d:
                    it, Td, n = d
                    dpar = 1 - par
                    if Td == 0 and not early(it - 1):
                        act.wait_ge(s.inverse, it - 1)
                    act.wait_ge(s.probs[1], n + 1)
                    nc.scalar.activation(ex[Td % 2][:, 1, :], t.prob[Td][:, 1, HALF:HALF + N], ACT.Copy,
                                         accum_out=rs[dpar][:, 2 * Td + 1:2 * Td + 2]).then_inc(s.row_sums, 1)

            run_iterations(act, body)

        @block.vector
        def _(dve):
            def met():
                dve.wait_ge(s.bias_added, B)

            def body(z, par):
                T = z.T
                old = z.iteration(-3)
                c = z.back(3)
                if c:
                    it, Tc, n = c
                    q = Tc % 2
                    cpar = par if T >= 3 else 1 - par
                    for r in range(4):
                        for h in range(2):
                            kept, shortened = known(dve, 2 * n + h + 1, 6 * n + (r - 1) * 2 + h + 1)
                            met()
                            if r == 0:
                                dve.wait_ge(s.scores_kept, kept)
                                nc.vector.max(top[q][:, h, 0:8], sc[q][:, h, :]).then_inc(s.tops, 1)
                            else:
                                dve.wait_ge(s.shortened, shortened)
                                nc.vector.max(top[q][:, h, 8 * r:8 * r + 8], work[:, h, :]).then_inc(s.next_tops, 1)
                        if r == 3:
                            continue
                        for h in range(2):
                            first_found, found = known(dve, 2 * n + h + 1, 6 * n + (r - 1) * 2 + h + 1)
                            met()
                            if r == 0:
                                dve.wait_ge(s.tops, first_found)
                            else:
                                dve.wait_ge(s.next_tops, found)
                            nc.vector.match_replace(out=work[:, h, :], in_to_replace=top[q][:, h, 8 * r:8 * r + 8],
                                                    in_values=sc[q][:, h, :] if r == 0 else work[:, h, :],
                                                    imm_value=NEG).then_inc(s.shortened, 1)
                    if Tc == 0 and not early((it - 1)):
                        dve.wait_ge(s.inverse, it - 1)
                    dve.wait_ge(s.next_tops, 6 * n + 5)
                    dve.wait_ge(s.exps, 2 * n + 1)
                    if not early(n - 3):
                        dve.wait_ge(s.band_closed, n - 3)
                    nc.vector.scalar_tensor_tensor(out=t.prob[Tc][:, 0, HALF:HALF + N], in0=sc[q][:, 0, :],
                                                   scalar=top[q][:, 0, TOPK - 1:TOPK], in1=ex[q][:, 0, :],
                                                   op0=ALU.is_ge, op1=ALU.mult,
                                                   accum_out=rs[cpar][:, 2 * Tc:2 * Tc + 1]).then_inc(s.probs[0], 1)
                if T == 0 and (it := z.iteration(-2)) is not None:
                    dve.wait_ge(s.probs[0], (it + 1) * NT)
                    dve.wait_ge(s.row_sums, (it + 1) * NT)
                    if not early((it - 1) * ORDER):
                        dve.wait_ge(s.values_next, (it - 1) * ORDER)
                    nc.vector.reciprocal(inv[par][:, :], rs[par][:, :]).then_inc(s.inverse, 1)
                if old is not None and T == 0:
                    dve.wait_ge(s.out_made, old + 1)
                    if not early(old):
                        dve.wait_ge(s.out_added, old)
                    Xb = k.X[:, bass.ds((old // PAIRS) * N, N)]
                    nc.vector.tensor_tensor(Xb, MISC[:, :], Xb, ALU.add).then_inc(s.out_added, 1)

            with dve.Fori(0, B) as b:
                Xb = k.X[:, bass.ds(b * N, N)].rearrange("p (t d) -> p t d", d=D)
                nc.vector.tensor_tensor(Xb, Xb, bcast(k.bout[:, :], [[0, NT], [1, D]]), ALU.add)\
                    .then_inc(s.bias_added, 1)
            dve.wait_ge(s.bias_added, B)
            run_iterations(dve, body)

        @block.gpsimd
        def _(pool):
            def body(z, par):
                T = z.T
                av, cur = z.iteration(-2), z.iteration(0)
                if av is not None and T > 0:
                    pool.wait_ge(s.raw_kept, av * ORDER + T)
                    if T == 1:
                        pool.wait_ge(s.inverse, av + 1)
                        if not early(av):
                            pool.wait_ge(s.res_chain, av * 5)
                    else:
                        pool.wait_ge(s.res_chain, av * 5 + 2 * T - 3)
                    nc.gpsimd.tensor_tensor(u[:, :, :, :], raw[:, :, :, :],
                                            bcast(inv[par][:, :], [[2, NT], [1, 2], [0, DH]]),
                                            ALU.mult).then_inc(s.values_next, 1)
                    alpha = bcast(po[par][:, O_AL + 2 * T - 2:O_AL + 2 * T], [[0, NT], [1, 2], [0, DH]])
                    pool.wait_ge(s.values_next, av * ORDER + T)
                    if T == 1:
                        pool.wait_ge(s.po_in[par], 16 * (z.half(-2) + 1))
                        if not early(av):
                            pool.wait_ge(s.res_turned, av)
                        nc.gpsimd.tensor_tensor(res[:, :, :, :], u[:, :, :, :], alpha,
                                                ALU.mult).then_inc(s.res_chain, 1)
                    else:
                        nc.gpsimd.tensor_tensor(tmp[:, :, :, :], u[:, :, :, :], alpha,
                                                ALU.mult).then_inc(s.res_chain, 1)
                        pool.wait_ge(s.res_chain, av * 5 + 2 * T - 2)
                        nc.gpsimd.tensor_tensor(res[:, :, :, :], res[:, :, :, :], tmp[:, :, :, :],
                                                ALU.add).then_inc(s.res_chain, 1)
                if T == 1 and cur is not None:
                    pool.wait_ge(s.v_kept, cur + 1)
                    if not early((cur - 2) * ORDER + 1):
                        pool.wait_ge(s.mixed, (cur - 2) * ORDER + 1)
                    nc.gpsimd.tensor_tensor(v[par][:, :, :], vraw[:, :, :],
                                            bcast(pj[par][:, J_BV:J_BV + P], [[0, NT], [1, P]]),
                                            ALU.add).then_inc(s.v_ready, 1)

                if c := z.back(3):
                    it, Tc, n = c
                    q = Tc % 2
                    found, used = known(pool, 6 * n + 6, n)
                    pool.wait_ge(s.bias_added, B)
                    pool.wait_ge(s.next_tops, found)
                    if not early(used):
                        pool.wait_ge(s.probs[1], used)
                    nc.gpsimd.tensor_scalar(kept[:, :], sc[q][:, 1, :], top[q][:, 1, TOPK - 1:TOPK], None,
                                            ALU.is_ge).then_inc(s.at_least, 1)
                    pool.wait_ge(s.at_least, n + 1)
                    pool.wait_ge(s.exps, 2 * n + 2)
                    if not early(n - 3):
                        pool.wait_ge(s.band_closed, n - 3)
                    nc.gpsimd.tensor_tensor(t.prob[Tc][:, 1, HALF:HALF + N], kept[:, :], ex[q][:, 1, :],
                                            ALU.mult).then_inc(s.probs[1], 1)

            run_iterations(pool, body)


E, CAP = 8, TILES * P // 8
HALF_IN = 128
MH, MP, MS = 8, 16, 16
CONV = 4
SECOND = 32


def rest_rows(sb):
    w = Namespace()
    w.expert = sb("expert_rows", [P, E, D])
    w.inn = sb("w_in_rows", [P, 2, D])
    w.bc = sb("w_bc_rows", [2 * SECOND, D])
    w.dt = sb("w_dt_rows", [MH, D])
    w.out = sb("w_out_rows", [P, 2 * HALF_IN])
    w.alog = sb("a_log_all", [P, MH])
    return w


REST_LOADS = 19


def load_rest(nc, sp, loaded, a, w, r):
    few = nc.allow_non_contiguous_dma
    w_in = a["b_W_in"]
    x0 = HALF_IN
    b0 = x0 + HALF_IN
    c0 = b0 + MS
    d0 = c0 + MS
    sp.dma_start(w.expert[:, :, :], a["f_W"].rearrange("e f h -> f e h")).then_inc(loaded, 16)
    sp.dma_start(w.inn[:, :, :], w_in[0:b0, :].rearrange("(c p) d -> p c d", p=P)).then_inc(loaded, 16)
    sp.dma_start(w.bc[0:MS, :], w_in[b0:c0, :]).then_inc(loaded, 16)
    sp.dma_start(w.bc[SECOND:SECOND + MS, :], w_in[c0:d0, :]).then_inc(loaded, 16)
    sp.dma_start(w.dt[:, :], w_in[d0:d0 + MH, :]).then_inc(loaded, 16)
    sp.dma_start(w.out[:, :], a["b_W_out"]).then_inc(loaded, 16)
    sp.dma_start(r.wg[:, :], a["f_wg"]).then_inc(loaded, 16)
    sp.dma_start(r.eb[:, :], a["f_b"]).then_inc(loaded, 16)
    cw = a["b_conv_w"].rearrange("c o k -> c (o k)")
    cb = a["b_conv_b"].rearrange("(c o) -> c o", o=1)
    sp.dma_start(r.cwx[:, :], cw[0:P, :]).then_inc(loaded, 16)
    sp.dma_start(r.cwb[0:MS, :], cw[P:P + MS, :]).then_inc(loaded, 16)
    sp.dma_start(r.cwb[SECOND:SECOND + MS, :], cw[P + MS:P + 2 * MS, :]).then_inc(loaded, 16)
    sp.dma_start(r.cbx[:, :], cb[0:P, :]).then_inc(loaded, 16)
    sp.dma_start(r.cbb[0:MS, :], cb[P:P + MS, :]).then_inc(loaded, 16)
    sp.dma_start(r.cbb[SECOND:SECOND + MS, :], cb[P + MS:P + 2 * MS, :]).then_inc(loaded, 16)

    def everywhere(to, of):
        sp.dma_start(to, of.rearrange("(o n) -> o n", o=1).to_broadcast([P, MH])).then_inc(loaded, 16)

    everywhere(r.dtb[:, :], a["b_dt_bias"])
    everywhere(w.alog[:, :], a["b_A_log"])
    everywhere(r.dskip[:, :], a["b_Dskip"])
    with few(reason="256 values each, once"):
        sp.dma_start(r.lnw[:, :], a["b_ln_w"].rearrange("(c p) -> p c", p=P)).then_inc(loaded, 16)
        sp.dma_start(r.lnb[:, :], a["b_ln_b"].rearrange("(c p) -> p c", p=P)).then_inc(loaded, 16)


def set_up_rest(nc, sem, sb, ps, k, w, r, loaded):
    turned, chain, kept = (sem(f"rest_{n}") for n in ("turned", "chain", "kept"))
    alog_e = sb("a_log_exp", [P, MH])

    with nc.Block() as block:
        @block.gpsimd
        def _(pool):
            pool.wait_ge(chain, 1)
            for m, base in ((r.before, 0), (r.upto, 1)):
                nc.gpsimd.affine_select(out=m[:, :], in_=m[:, :], compare_op=ALU.is_gt, fill=0.0,
                                        base=base, pattern=[[1, P]], channel_multiplier=-1)
            nc.gpsimd.affine_select(out=r.after[:, :], in_=r.after[:, :], compare_op=ALU.is_gt, fill=0.0,
                                    base=0, pattern=[[-1, P]], channel_multiplier=1)

        @block.vector
        def _(dve):
            for m in (r.before, r.upto, r.after):
                nc.vector.memset(m[:, :], 1.0)
            nc.vector.memset(r.ones[:, :], 1.0)
            nc.vector.memset(r.rank[:, 0:1], float(E))
            for e in range(1, E):
                last = nc.vector.memset(r.rank[:, e:e + 1], float(E - e))
            last.then_inc(chain, 1)
            dve.wait_ge(loaded, 16 * REST_LOADS)
            dve.wait_ge(turned, 1)
            nc.vector.tensor_copy(r.win[:, 0:2 * P], ps[2][:, 0:2 * P])
            nc.vector.tensor_copy(r.win[:, 2 * P:2 * P + 2 * SECOND], ps[3][:, 0:2 * SECOND])
            nc.vector.tensor_copy(r.wdt[:, :], ps[4][:, 0:MH])
            nc.vector.tensor_copy(r.wo[:, :, :].rearrange("p c d -> p (c d)"), ps[5][:, 0:2 * P])
            nc.vector.tensor_scalar(r.cbx2[:, :], r.cbx[:, :], 0.5, None, ALU.mult)
            nc.vector.tensor_scalar(r.cbb2[:, :], r.cbb[:, :], 0.5, None, ALU.mult)
            dve.wait_ge(kept, 1)
            nc.vector.tensor_scalar(r.A[:, :], alog_e[:, :], -1.0, None, ALU.mult).then_inc(chain, 1)
            dve.wait_ge(chain, 2)

        @block.tensor
        def _(pe):
            pe.wait_ge(loaded, 16 * REST_LOADS)
            for e in range(E):
                nc.tensor.transpose(ps[e // 4][:, (e % 4) * P:(e % 4 + 1) * P], w.expert[:, e, :], k.ident[:, :])
            for c in range(2):
                nc.tensor.transpose(ps[2][:, c * P:(c + 1) * P], w.inn[:, c, :], k.ident[:, :])
                nc.tensor.transpose(ps[5][:, c * P:(c + 1) * P], w.out[:, c * P:(c + 1) * P], k.ident[:, :])
            nc.tensor.transpose(ps[3][:, 0:2 * SECOND], w.bc[:, :], k.ident[0:2 * SECOND, 0:2 * SECOND])
            nc.tensor.transpose(ps[4][:, 0:MH], w.dt[:, :], k.ident[0:MH, 0:MH]).then_inc(turned, 1)

        @block.scalar
        def _(act):
            act.wait_ge(loaded, 16 * REST_LOADS)
            nc.scalar.activation(alog_e[:, :], w.alog[:, :], ACT.Exp).then_inc(kept, 1)
            act.wait_ge(turned, 1)
            for q in range(2):
                last = nc.scalar.activation(r.we[:, q * 512:(q + 1) * 512], ps[q][:, :], ACT.Copy)
            last.then_inc(kept, 1)


def eight_sems(sem, tag):
    s = Namespace()
    s.made, s.stored = (sem(f"{tag}_{n}") for n in ("made", "stored"))
    return s


def eight_tensor(nc, pe, s, W, XNT, bank):
    for t in range(TILES):
        last = nc.tensor.matmul(bank[:, t * 8:(t + 1) * 8], XNT[:, t * P:(t + 1) * P], W, start=True, stop=True)
    last.then_inc(s.made, 1)


def eight_vector(nc, dve, s, OUT, bank):
    dve.wait_ge(s.made, 1)
    nc.vector.tensor_copy(OUT[:, :], bank[:, 0:TILES * 8]).then_inc(s.stored, 1)


def experts(nc, sem, sb, ps, k, r, tag):
    def S(n):
        return sem(f"{tag}_{n}")

    g = eight_sems(sem, f"{tag}_logits")
    step, ex_done, counted, gates = S("step"), S("exp"), S("counted"), S("gates")
    xs_in = [S(f"xs_in{q}") for q in range(2)]
    gs_in = [S(f"gs_in{q}") for q in range(2)]
    g_turned, g_kept, bias_made, bias_added = (S(n) for n in ("g_turned", "g_kept", "bias_made", "bias_added"))
    near_made, y_made, near_scaled, far_scaled = (S(n) for n in ("near_made", "y_made", "near_scaled", "far_scaled"))
    summed, tree, stream_added = (S(n) for n in ("summed", "tree", "stream_added"))
    n8 = TILES * E
    b = Namespace()
    b.logit = sb(f"{tag}_logit", [P, n8])
    b.diff = sb(f"{tag}_diff", [P, n8])
    b.exp = sb(f"{tag}_exp", [P, n8])
    b.same = sb(f"{tag}_same", [P, n8])
    b.score = sb(f"{tag}_score", [P, n8])
    b.mask = sb(f"{tag}_mask", [P, n8])
    b.loc = sb(f"{tag}_loc", [P, n8])
    b.keep = sb(f"{tag}_keep", [P, n8])
    b.gate8 = sb(f"{tag}_gate8", [P, n8])
    b.prev = sb(f"{tag}_prev", [P, n8])
    b.sum_a = sb(f"{tag}_sum_a", [P, n8])
    b.sum_b = sb(f"{tag}_sum_b", [P, n8])
    b.top = sb(f"{tag}_top", [P, TILES])
    b.total = sb(f"{tag}_total", [P, TILES])
    b.prob = sb(f"{tag}_prob", [P, TILES])
    b.best = sb(f"{tag}_best", [P, TILES])
    xs = [sb(f"{tag}_xs{q}", [P, 512]) for q in range(2)]
    gs = [sb(f"{tag}_gs{q}", [P, 4 * E]) for q in range(2)]
    gt = [sb(f"{tag}_gt{q}", [E, 512]) for q in range(2)]
    near = [sb(f"{tag}_near{q}", [P, 512]) for q in range(2)]
    far = [sb(f"{tag}_far{q}", [P, 512]) for q in range(2)]
    sums = [sb(f"{tag}_sums{q}", [P, 4, 512]) for q in range(2)]
    two_sums = sb(f"{tag}_two_sums", [P, 4, 2, P])
    one_sum = sb(f"{tag}_one_sum", [P, 4, P])

    def v3(x):
        return x[:, :].rearrange("p (t e) -> p t e", e=E)

    def over(x):
        return bcast(x[:, :], [[1, TILES], [0, E]])

    with nc.Block() as block:
        @block.tensor
        def _(pe):
            eight_tensor(nc, pe, g, r.wg[:, :], k.XNT, ps[0])
            pe.wait_ge(step, 1)
            nc.tensor.matmul(ps[4][:, 0:n8], r.before[:, :], b.mask[:, :], start=True, stop=True)
            nc.tensor.matmul(ps[5][:, 0:n8], r.ones[:, :], b.mask[:, :], start=True, stop=True).then_inc(counted, 1)

        @block.scalar
        def _(act):
            act.wait_ge(ex_done, 1)
            nc.scalar.activation(b.exp[:, :], b.diff[:, :], ACT.Exp).then_inc(ex_done, 1)

        @block.vector
        def _(dve):
            chain = [0]

            def link(ins):
                chain[0] += 1
                ins.then_inc(gates, 1)
                dve.wait_ge(gates, chain[0])

            eight_vector(nc, dve, g, b.logit, ps[0])
            dve.wait_ge(g.stored, 1)
            link(nc.vector.tensor_reduce(out=b.top[:, :], in_=v3(b.logit), axis=AX.X, op=ALU.max))
            nc.vector.tensor_tensor(v3(b.diff), v3(b.logit), over(b.top), ALU.subtract).then_inc(ex_done, 1)
            link(nc.vector.tensor_tensor(v3(b.same), v3(b.logit), over(b.top), ALU.is_equal))
            link(nc.vector.tensor_tensor(v3(b.score), v3(b.same), bcast(r.rank[:, :], [[0, TILES], [1, E]]), ALU.mult))
            link(nc.vector.tensor_reduce(out=b.best[:, :], in_=v3(b.score), axis=AX.X, op=ALU.max))
            nc.vector.tensor_tensor(v3(b.mask), v3(b.score), over(b.best), ALU.is_equal).then_inc(step, 1)
            dve.wait_ge(ex_done, 2)
            link(nc.vector.tensor_reduce(out=b.total[:, :], in_=v3(b.exp), axis=AX.X, op=ALU.add))
            link(nc.vector.reciprocal(b.prob[:, :], b.total[:, :]))
            dve.wait_ge(counted, 1)
            nc.vector.memset(b.sum_a[:, 0:E], 0.0)
            link(nc.vector.tensor_copy(b.sum_a[:, E:n8], ps[5][:, 0:n8 - E]))
            src, dst, stride = b.sum_a, b.sum_b, E
            while stride < n8:
                nc.vector.tensor_copy(dst[:, 0:stride], src[:, 0:stride])
                link(nc.vector.tensor_tensor(dst[:, stride:n8], src[:, stride:n8], src[:, 0:n8 - stride], ALU.add))
                src, dst, stride = dst, src, stride * 2
            link(nc.vector.tensor_tensor(b.loc[:, :], ps[4][:, 0:n8], src[:, :], ALU.add))
            link(nc.vector.scalar_tensor_tensor(out=b.keep[:, :], in0=b.loc[:, :], scalar=float(CAP), in1=b.mask[:, :],
                                                op0=ALU.is_lt, op1=ALU.mult))
            link(nc.vector.tensor_tensor(v3(b.gate8), v3(b.keep), over(b.prob), ALU.mult))

    with nc.Block() as block:
        @block.sync
        def _(sp):
            def body(i, par, first):
                at, gates_at, free, turned = known(sp, i * 512, i * 4 * E, (i - 1) * 4, i - 1)
                if not first:
                    sp.wait_ge(y_made, free)
                sp.dma_start(xs[par][:, :], k.XNT[:, bass.ds(at, 512)]).then_inc(xs_in[par], 16)
                if not first:
                    sp.wait_ge(g_turned, turned)
                sp.dma_start(gs[par][:, :], b.gate8[:, bass.ds(gates_at, 4 * E)]).then_inc(gs_in[par], 16)

            two_at_a_time(sp, GROUPS, body)

        @block.tensor
        def _(pe):
            def body(i, par, first, half=0):
                pe.wait_ge(gs_in[par], (half + 1) * 16)
                if not first:
                    pe.wait_ge(g_kept, i - 1)
                for c in range(4):
                    last = nc.tensor.transpose(ps[4 + par][0:E, c * P:(c + 1) * P], gs[par][:, c * E:(c + 1) * E],
                                               k.ident[:, :])
                last.then_inc(g_turned, 1)
                pe.wait_ge(xs_in[par], (half + 1) * 16)
                for c in range(4):
                    for q in range(2):
                        bank = ps[2 * (c % 2) + q]
                        if not (first and par == 0 and c < 2):
                            pe.wait_ge((near_scaled, far_scaled)[q], i * 4 + c - 1)
                        nc.tensor.matmul(bank[:, :], xs[par][:, c * P:(c + 1) * P],
                                         r.we[:, q * 512:(q + 1) * 512], start=True, stop=True)\
                            .then_inc((near_made, y_made)[q], 1)
                    if c == 0:
                        pe.wait_ge(g_kept, i + 1)
                        if not first:
                            pe.wait_ge(bias_added, i - 1)
                        for cc in range(4):
                            last = nc.tensor.matmul(ps[6 + par][:, cc * P:(cc + 1) * P],
                                                    gt[par][:, cc * P:(cc + 1) * P], r.eb[:, :], start=True, stop=True)
                        last.then_inc(bias_made, 1)

            two_at_a_time(pe, GROUPS, body, with_half=True)

        @block.scalar
        def _(act):
            def body(i, par, first):
                act.wait_ge(g_turned, i + 1)
                if not first:
                    act.wait_ge(bias_made, i - 1)
                nc.scalar.activation(gt[par][:, :], ps[4 + par][0:E, :], ACT.Copy).then_inc(g_kept, 1)
                for c in range(4):
                    act.wait_ge(y_made, i * 4 + c + 1)
                    if not (first and par == 0 and c < 2):
                        act.wait_ge(summed, i * 4 + c - 1)
                    for e in range(4):
                        last = nc.scalar.activation(far[c % 2][:, e * P:(e + 1) * P],
                                                    ps[2 * (c % 2) + 1][:, e * P:(e + 1) * P],
                                                    ACT.Copy, scale=b.gate8[:, bass.ds((i * 4 + c) * E + 4 + e, 1)])
                    last.then_inc(far_scaled, 1)

            two_at_a_time(act, GROUPS, body)

        @block.vector
        def _(dve):
            def body(i, par, first):
                def add(c):
                    t = i * 4 + c
                    dve.wait_ge(near_scaled, t + 1)
                    dve.wait_ge(far_scaled, t + 1)
                    if c == 0 and not first:
                        dve.wait_ge(stream_added, i - 1)
                    nc.vector.tensor_tensor(sums[par][:, c, :], near[c % 2][:, :], far[c % 2][:, :],
                                            ALU.add).then_inc(summed, 1)

                for c in range(4):
                    t = i * 4 + c
                    dve.wait_ge(near_made, t + 1)
                    if not (first and par == 0 and c < 2):
                        dve.wait_ge(summed, t - 1)
                    nc.vector.tensor_tensor(near[c % 2][:, :].rearrange("p (e f) -> p e f", e=4),
                                            ps[2 * (c % 2)][:, :].rearrange("p (e f) -> p e f", e=4),
                                            b.gate8[:, bass.ds(t * E, 4)].unsqueeze(2).to_broadcast([P, 4, P]),
                                            ALU.mult).then_inc(near_scaled, 1)
                    if c > 0:
                        add(c - 1)
                    else:
                        X4 = k.X[:, bass.ds(i * 512, 512)]
                        dve.wait_ge(bias_made, i + 1)
                        nc.vector.tensor_tensor(X4, ps[6 + par][:, :], X4, ALU.add).then_inc(bias_added, 1)
                add(3)

            two_at_a_time(dve, GROUPS, body)

        @block.gpsimd
        def _(pool):
            def body(i, par, first):
                four = sums[par][:, :, :].rearrange("p t (e f) -> p t e f", e=4)
                pool.wait_ge(summed, i * 4 + 4)
                if not early(i):
                    pool.wait_ge(stream_added, i)
                nc.gpsimd.tensor_tensor(two_sums[:, :, :, :], four[:, :, 0:2, :], four[:, :, 2:4, :],
                                        ALU.add).then_inc(tree, 1)
                pool.wait_ge(tree, i * 2 + 1)
                nc.gpsimd.tensor_tensor(one_sum[:, :, :], two_sums[:, :, 0, :], two_sums[:, :, 1, :],
                                        ALU.add).then_inc(tree, 1)
                pool.wait_ge(tree, i * 2 + 2)
                pool.wait_ge(bias_added, i + 1)
                X4 = k.X[:, bass.ds(i * 512, 512)].rearrange("p (t f) -> p t f", t=4)
                nc.gpsimd.tensor_tensor(X4, one_sum[:, :, :], X4, ALU.add).then_inc(stream_added, 1)

            two_at_a_time(pool, GROUPS, body)


def mixer(nc, sem, sb, ps, k, r):
    def S(n):
        return sem(f"mixer_{n}")

    g = eight_sems(sem, "mixer_dt")
    step, e_done, sums, dt_chain = S("step"), S("exp"), S("sums"), S("dt_chain")
    n8 = TILES * MH
    b = Namespace()
    b.raw = sb("mixer_raw", [P, n8])
    b.v = sb("mixer_v", [P, n8])
    b.neg = sb("mixer_neg", [P, n8])
    b.e = sb("mixer_e", [P, n8])
    b.log = sb("mixer_log", [P, n8])
    b.dt = sb("mixer_dt", [P, n8])
    b.a = sb("mixer_a", [P, n8])
    b.to_end = sb("mixer_to_end", [P, n8])
    b.from_start = sb("mixer_from_start", [P, n8])
    b.whole = sb("mixer_whole", [P, n8])

    with nc.Block() as block:
        @block.tensor
        def _(pe):
            eight_tensor(nc, pe, g, r.wdt[:, :], k.XNT, ps[0])
            pe.wait_ge(step, 2)
            nc.tensor.matmul(ps[4][:, 0:n8], r.after[:, :], b.a[:, :], start=True, stop=True)
            nc.tensor.matmul(ps[5][:, 0:n8], r.upto[:, :], b.a[:, :], start=True, stop=True)
            nc.tensor.matmul(ps[6][:, 0:n8], r.ones[:, :], b.a[:, :], start=True, stop=True).then_inc(sums, 1)

        @block.scalar
        def _(act):
            act.wait_ge(step, 1)
            nc.scalar.activation(b.e[:, :], b.neg[:, :], ACT.Exp).then_inc(e_done, 1)
            act.wait_ge(e_done, 1)
            nc.scalar.activation(b.log[:, :], b.e[:, :], ACT.Ln, bias=1.0).then_inc(e_done, 1)
            act.wait_ge(sums, 1)
            for bank, to in ((ps[4], b.to_end), (ps[5], b.from_start), (ps[6], b.whole)):
                nc.scalar.activation(to[:, :], bank[:, 0:n8], ACT.Exp).then_inc(e_done, 1)

        @block.vector
        def _(dve):
            eight_vector(nc, dve, g, b.raw, ps[0])
            dve.wait_ge(g.stored, 1)
            v3, raw3 = (x[:, :].rearrange("p (t e) -> p t e", e=MH) for x in (b.v, b.raw))
            nc.vector.tensor_tensor(v3, raw3, bcast(r.dtb[:, :], [[0, TILES], [1, MH]]), ALU.add).then_inc(dt_chain, 1)
            dve.wait_ge(dt_chain, 1)
            nc.vector.scalar_tensor_tensor(out=b.neg[:, :], in0=b.v[:, :], scalar=-1.0, in1=b.v[:, :],
                                           op0=ALU.mult, op1=ALU.min).then_inc(step, 1)
            dve.wait_ge(e_done, 2)
            nc.vector.scalar_tensor_tensor(out=b.dt[:, :], in0=b.v[:, :], scalar=0.0, in1=b.log[:, :],
                                           op0=ALU.max, op1=ALU.add).then_inc(dt_chain, 1)
            dve.wait_ge(dt_chain, 2)
            nc.vector.tensor_tensor(b.a[:, :].rearrange("p (t e) -> p t e", e=MH),
                                    b.dt[:, :].rearrange("p (t e) -> p t e", e=MH),
                                    bcast(r.A[:, :], [[0, TILES], [1, MH]]), ALU.mult).then_inc(step, 1)

    xs_in = [S(f"xs_in{q}") for q in range(2)]
    m = Namespace()
    m.projected = S("projected")
    m.conv_in = S("conv_in")
    m.conv_out = S("conv_out")
    m.squashed = S("squashed")
    m.silu = S("silu")
    m.turned = S("turned")
    m.turned_used = S("turned_used")
    m.spread = S("spread")
    m.diffs = S("diffs")
    m.exps = S("exps")
    m.weights = S("weights")
    m.y_made = S("y_made")
    m.padded = S("padded")
    m.y_used = S("y_used")
    m.var = S("var")
    m.rstd = S("rstd")
    m.scaled = S("scaled")
    m.yn_turned = S("yn_turned")
    m.yt_kept = S("yt_kept")
    m.out_made = S("out_made")
    m.out_added = S("out_added")
    m.link = S("link")
    m.conv_link = S("conv_link")
    xs = [sb(f"mixer_xs{q}", [P, N]) for q in range(2)]
    PAD = CONV - 1
    xp = sb("mixer_conv_x", [P, PAD + N])
    bp = sb("mixer_conv_bc", [2 * SECOND, PAD + N])
    cx = [sb(f"mixer_sum_x{q}", [P, N]) for q in range(2)]
    cb = [sb(f"mixer_sum_bc{q}", [2 * SECOND, N]) for q in range(2)]
    tx, hx = sb("mixer_tanh_x", [P, N]), sb("mixer_half_x", [P, N])
    tb, hb = sb("mixer_tanh_bc", [2 * SECOND, N]), sb("mixer_half_bc", [2 * SECOND, N])
    xc = [sb(f"mixer_x{q}", [P, N]) for q in range(2)]
    bs = [sb(f"mixer_b{q}", [MS, N]) for q in range(2)]
    cs = [sb(f"mixer_c{q}", [MS, N]) for q in range(2)]
    yz = [sb(f"mixer_yz{q}", [P, NT, 2 * HALF_IN]) for q in range(2)]
    yn = sb("mixer_yn", [P, NT, 2 * HALF_IN])
    yt = sb("mixer_yt", [P, 2, P])
    al = [sb(f"mixer_a_spread{q}", [P, MH, P]) for q in range(2)]
    ex = [sb(f"mixer_decay{q}", [P, MH, P]) for q in range(2)]
    mm = [sb(f"mixer_weights{q}", [P, MH, P]) for q in range(2)]
    gm = [sb(f"mixer_cb{q}", [P, P]) for q in range(2)]
    dx = [sb(f"mixer_dtx{q}", [P, MH, MP]) for q in range(2)]
    xd = [sb(f"mixer_dtx_end{q}", [P, MH, MP]) for q in range(2)]
    bt = [sb(f"mixer_b_rows{q}", [P, MS]) for q in range(2)]
    st, st2 = sb("mixer_state", [MS, MH, MP]), sb("mixer_state_decayed", [MS, MH, MP])
    yo, y1 = sb("mixer_y_off", [P, MH, MP]), sb("mixer_y_sum", [P, MH, MP])
    stat = sb("mixer_stats", [P, NT, 6])
    w = Namespace()
    w.mean2 = sb("mixer_n_mean2", [P, NT])
    w.mean = sb("mixer_n_mean", [P, NT])
    w.diff = sb("mixer_n_diff", [P, NT])
    w.diff2 = sb("mixer_n_diff2", [P, NT])
    w.var2 = sb("mixer_n_var2", [P, NT])
    w.var = sb("mixer_n_var", [P, NT])
    w.vareps = sb("mixer_n_vareps", [P, NT])
    w.rstd = sb("mixer_n_rstd", [P, NT])
    w.mhalf = sb("mixer_n_mhalf", [P, NT])
    T1, DF, Y, O = ps[3], ps[4:6], ps[6], ps[7]
    PX, PB, PZ = ps[0], ps[1], ps[2]
    CONV_LINKS, CHUNK_LINKS = 2 * (CONV - 1), 4 * NT + 3

    def heads(x, t):
        return x[:, bass.ds(t * MH, MH)].unsqueeze(2).to_broadcast([P, MH, MP])

    def run_steps(eng, body):
        for i in range(-1, 3):
            body(i, i % 2, (i + 1) // 2)
        with eng.Fori(1, B // 2 - 1) as g:
            body(g * 2 + 1, 1, g + 1)
            body(g * 2 + 2, 0, g + 1)
        for i in range(B - 1, B + 1):
            body(i, i % 2, (i + 1) // 2)

    def stages(i):
        if not isinstance(i, int):
            return i + 1, i, i - 1
        return tuple(x if 0 <= x < B else None for x in (i + 1, i, i - 1))

    with nc.Block() as block:
        @block.sync
        def _(sp):
            def body(i, par, first):
                at, used = known(sp, i * N, (i - 1) * 3)
                if not first:
                    sp.wait_ge(m.projected, used)
                sp.dma_start(xs[par][:, :], k.XNT[:, bass.ds(at, N)]).then_inc(xs_in[par], 16)

            two_at_a_time(sp, B, body)

        @block.tensor
        def _(pe):
            def first_half(j, par, c):
                t, q, cols = j * NT + c, c % 2, slice(c * P, (c + 1) * P)
                pe.wait_ge(m.spread, t + 1)
                if not early(t):
                    pe.wait_ge(m.exps, t)
                for h in range(MH):
                    last = nc.tensor.matmul(DF[h // 4][:, (h % 4) * P:(h % 4 + 1) * P], al[q][:, h, :], r.upto[:, :],
                                            start=True, stop=True)
                last.then_inc(m.diffs, 1)
                if c == 0:
                    pe.wait_ge(m.silu, j * 3 + 3)
                if not early(t):
                    pe.wait_ge(m.turned_used, t)
                nc.tensor.transpose(T1[:, 0:P], xc[par][:, cols], k.ident[:, :])
                nc.tensor.transpose(T1[:, P:P + MS], bs[par][:, cols], k.ident[0:MS, 0:MS])
                nc.tensor.matmul(T1[:, 2 * P:3 * P], bs[par][:, cols], cs[par][:, cols],
                                 start=True, stop=True).then_inc(m.turned, 1)

            def second_half(j, par, c):
                t, q, cols = j * NT + c, c % 2, slice(c * P, (c + 1) * P)
                pe.wait_ge(m.weights, t + 1)
                if not early(t):
                    pe.wait_ge(m.y_used, t)
                for h in range(MH):
                    nc.tensor.matmul(Y[:, h * MP:(h + 1) * MP], mm[q][:, h, :], dx[q][:, h, :], start=True, stop=True)
                nc.tensor.matmul(Y[:, P:2 * P], cs[par][:, cols], st[:, :, :].rearrange("n h p -> n (h p)"),
                                 start=True, stop=True)
                nc.tensor.matmul(Y[0:MS, 2 * P:3 * P], bt[q][:, :], xd[q][:, :, :].rearrange("s h p -> s (h p)"),
                                 start=True, stop=True).then_inc(m.y_made, 1)

            def projections(j, par, pairs):
                pe.wait_ge(xs_in[par], (pairs + 1) * 16)
                if not early(j):
                    pe.wait_ge(m.conv_in, j * 3)
                nc.tensor.matmul(PX[:, :], r.win[:, P:2 * P], xs[par][:, :],
                                 start=True, stop=True).then_inc(m.projected, 1)
                nc.tensor.matmul(PB[0:2 * SECOND, :], r.win[:, 2 * P:2 * P + 2 * SECOND], xs[par][:, :],
                                 start=True, stop=True).then_inc(m.projected, 1)
                for c in range(NT):
                    last = nc.tensor.matmul(PZ[:, c * P:(c + 1) * P], xs[par][:, c * P:(c + 1) * P], r.win[:, 0:P],
                                            start=True, stop=True)
                last.then_inc(m.projected, 1)

            def turn_normed(j, c):
                t = j * NT + c
                pe.wait_ge(m.scaled, t + 1)
                if not early(t):
                    pe.wait_ge(m.out_added, t)
                for e in range(2):
                    last = nc.tensor.transpose(O[:, e * P:(e + 1) * P], yn[:, c, e * P:(e + 1) * P], k.ident[:, :])
                last.then_inc(m.yn_turned, 1)

            def output(j, c):
                pe.wait_ge(m.yt_kept, j * NT + c + 1)
                for e in range(2):
                    last = nc.tensor.matmul(O[:, 2 * P:3 * P], yt[:, e, :], r.wo[:, e, :],
                                            start=(e == 0), stop=(e == 1))
                last.then_inc(m.out_made, 1)

            def body(i, par, pairs):
                front, cur, back = stages(i)
                if cur is not None:
                    first_half(cur, par, 0)
                    first_half(cur, par, 1)
                if front is not None:
                    projections(front, 1 - par, pairs)
                for c in range(NT):
                    if cur is not None:
                        second_half(cur, par, c)
                    if back is not None:
                        turn_normed(back, c)
                    if cur is not None and c + 2 < NT:
                        first_half(cur, par, c + 2)
                    if back is not None:
                        output(back, c)

            run_steps(pe, body)

        @block.scalar
        def _(act):
            def decays(j, c):
                t, q = j * NT + c, c % 2
                act.wait_ge(m.diffs, t + 1)
                if not early(t - 1):
                    act.wait_ge(m.weights, t - 1)
                for e in range(2):
                    last = nc.scalar.activation(ex[q][:, 4 * e:4 * e + 4, :].rearrange("p h t -> p (h t)"),
                                                DF[e][:, :], ACT.Exp)
                last.then_inc(m.exps, 1)

            def projected(j, par):
                act.wait_ge(m.projected, j * 3 + 1)
                if not early(j):
                    act.wait_ge(m.conv_out, j * 2)
                nc.scalar.activation(xp[:, PAD:], PX[:, :], ACT.Copy).then_inc(m.conv_in, 1)
                act.wait_ge(m.projected, j * 3 + 2)
                nc.scalar.activation(bp[:, PAD:], PB[0:2 * SECOND, :], ACT.Copy).then_inc(m.conv_in, 1)
                act.wait_ge(m.projected, j * 3 + 3)
                if not early(j - 1):
                    act.wait_ge(m.scaled, (j - 1) * NT)
                nc.scalar.activation(yz[par][:, :, HALF_IN:], PZ[:, :].rearrange("p (c e) -> p c e", c=NT),
                                     ACT.Copy).then_inc(m.conv_in, 1)

            def squash(j):
                for of, to, half, bias, n in ((cx, tx, hx, r.cbx2, 1), (cb, tb, hb, r.cbb2, 2)):
                    act.wait_ge(m.conv_out, j * 2 + n)
                    if not early(j):
                        act.wait_ge(m.silu, j * 3)
                    nc.scalar.activation(to[:, :], of[1][:, :], ACT.Tanh, bias=bias[:, :], scale=0.5)
                    nc.scalar.activation(half[:, :], of[1][:, :], ACT.Identity, bias=bias[:, :],
                                         scale=0.5).then_inc(m.squashed, 1)

            def keep_turned(j, c):
                t = j * NT + c
                act.wait_ge(m.yn_turned, t + 1)
                if not early(t):
                    act.wait_ge(m.out_made, t)
                for e in range(2):
                    last = nc.scalar.activation(yt[:, e, :], O[:, e * P:(e + 1) * P], ACT.Identity,
                                                scale=r.lnw[:, e:e + 1], bias=r.lnb[:, e:e + 1])
                last.then_inc(m.yt_kept, 1)

            def body(i, par, pairs):
                front, cur, back = stages(i)
                if cur is not None:
                    decays(cur, 0)
                    decays(cur, 1)
                if front is not None:
                    projected(front, 1 - par)
                for c in range(2):
                    if back is not None:
                        keep_turned(back, c)
                    if cur is not None:
                        decays(cur, c + 2)
                if front is not None:
                    squash(front)
                for c in range(2, NT):
                    if back is not None:
                        keep_turned(back, c)

            run_steps(act, body)

        @block.gpsimd
        def _(pool):
            def spread(j, c):
                t, q = j * NT + c, c % 2
                if not early(t - 1):
                    pool.wait_ge(m.diffs, t - 1)
                nc.gpsimd.tensor_tensor(al[q][:, :, :], bcast(r.after[:, :], [[0, MH], [1, P]]),
                                        b.a[:, bass.ds(t * MH, MH)].unsqueeze(2).to_broadcast([P, MH, P]),
                                        ALU.mult).then_inc(m.spread, 1)

            def body(i, par, pairs):
                front, cur, back = stages(i)
                if cur is not None:
                    spread(cur, 2)
                    spread(cur, 3)
                if front is not None:
                    spread(front, 0)
                    spread(front, 1)
                if cur is not None:
                    pool.wait_ge(m.var, cur + 1)
                    nc.gpsimd.tensor_tensor(w.rstd[:, :], w.vareps[:, :], w.mhalf[:, :], ALU.pow).then_inc(m.rstd, 1)

            run_steps(pool, body)

        @block.vector
        def _(dve):
            nc.vector.memset(w.mhalf[:, :], -0.5)
            nc.vector.memset(xp[:, 0:PAD], 0.0)
            nc.vector.memset(bp[:, 0:PAD], 0.0).then_inc(m.padded, 1)
            dve.wait_ge(m.padded, 1)

            def convolution(j):
                at = {}
                count = 0
                for tap in range(CONV):
                    for which, src, acc, weight in (("x", xp, cx, r.cwx), ("bc", bp, cb, r.cwb)):
                        if tap == 0:
                            dve.wait_ge(m.conv_in, j * 3 + (1 if which == "x" else 2))
                            done = nc.vector.tensor_scalar(acc[0][:, :], src[:, 0:N], weight[:, 0:1], None, ALU.mult)
                        else:
                            dve.wait_ge(m.conv_link, j * CONV_LINKS + at[which])
                            done = nc.vector.scalar_tensor_tensor(
                                out=acc[tap % 2][:, :], in0=src[:, tap:tap + N], scalar=weight[:, tap:tap + 1],
                                in1=acc[1 - tap % 2][:, :], op0=ALU.mult, op1=ALU.add)
                        if tap < CONV - 1:
                            count += 1
                            at[which] = count
                            done.then_inc(m.conv_link, 1)
                        else:
                            done.then_inc(m.conv_out, 1)

            def silu(j, par):
                dve.wait_ge(m.squashed, j * 2 + 1)
                nc.vector.scalar_tensor_tensor(out=xc[par][:, :], in0=tx[:, :], scalar=1.0, in1=hx[:, :],
                                               op0=ALU.add, op1=ALU.mult).then_inc(m.silu, 1)
                dve.wait_ge(m.squashed, j * 2 + 2)
                nc.vector.scalar_tensor_tensor(out=bs[par][:, :], in0=tb[0:MS, :], scalar=1.0, in1=hb[0:MS, :],
                                               op0=ALU.add, op1=ALU.mult).then_inc(m.silu, 1)
                nc.vector.scalar_tensor_tensor(out=cs[par][:, :], in0=tb[SECOND:SECOND + MS, :], scalar=1.0,
                                               in1=hb[SECOND:SECOND + MS, :],
                                               op0=ALU.add, op1=ALU.mult).then_inc(m.silu, 1)

            def body(i, par, pairs):
                front, cur, back = stages(i)
                links = [0]

                def link(ins):
                    links[0] += 1
                    ins.then_inc(m.link, 1)
                    return cur * CHUNK_LINKS + links[0]

                def before(c):
                    t, q = cur * NT + c, c % 2
                    dve.wait_ge(m.turned, t + 1)
                    xrows = T1[:, 0:P].rearrange("s (h p) -> s h p", h=MH)
                    nc.vector.tensor_copy(bt[q][:, :], T1[:, P:P + MS])
                    nc.vector.tensor_tensor(gm[q][:, :], T1[:, 2 * P:3 * P], r.upto[:, :], ALU.mult)
                    n1 = link(nc.vector.tensor_tensor(dx[q][:, :, :], xrows, heads(b.dt, t), ALU.mult))
                    nc.vector.tensor_tensor(yz[par][:, c, 0:HALF_IN].rearrange("p (h w) -> p h w", h=MH), xrows,
                                            r.dskip[:, :].unsqueeze(2).to_broadcast([P, MH, MP]),
                                            ALU.mult).then_inc(m.turned_used, 1)
                    dve.wait_ge(m.link, n1)
                    nc.vector.tensor_tensor(xd[q][:, :, :], dx[q][:, :, :], heads(b.to_end, t), ALU.mult)
                    dve.wait_ge(m.exps, t + 1)
                    for e in range(2):
                        last = nc.vector.tensor_tensor(mm[q][:, 4 * e:4 * e + 4, :], ex[q][:, 4 * e:4 * e + 4, :],
                                                       bcast(gm[q][:, :], [[0, 4], [1, P]]), ALU.mult)
                    last.then_inc(m.weights, 1)

                def behind(c):
                    t = cur * NT + c
                    dve.wait_ge(m.y_made, t + 1)
                    nc.vector.tensor_tensor(yo[:, :, :], Y[:, P:2 * P].rearrange("p (h w) -> p h w", h=MH),
                                            heads(b.from_start, t), ALU.mult)
                    n1 = link(nc.vector.tensor_tensor(st2[:, :, :], st[:, :, :],
                                                      b.whole[0:MS, bass.ds(t * MH, MH)].unsqueeze(2)
                                                      .to_broadcast([MS, MH, MP]), ALU.mult))
                    dve.wait_ge(m.link, n1)
                    n2 = link(nc.vector.tensor_tensor(y1[:, :, :], Y[:, 0:P].rearrange("p (h w) -> p h w", h=MH),
                                                      yo[:, :, :], ALU.add))
                    nc.vector.tensor_tensor(st[:, :, :], Y[0:MS, 2 * P:3 * P].rearrange("n (h w) -> n h w", h=MH),
                                            st2[:, :, :], ALU.add).then_inc(m.y_used, 1)
                    dve.wait_ge(m.link, n2)
                    yc = yz[par][:, c, 0:HALF_IN]
                    return link(nc.vector.tensor_tensor(yc, yc, y1[:, :, :].rearrange("p h w -> p (h w)"), ALU.add))

                def into_stream(c):
                    t = back * NT + c
                    dve.wait_ge(m.out_made, t + 1)
                    Xc = k.X[:, bass.ds(t * D, D)]
                    nc.vector.tensor_tensor(Xc, O[:, 2 * P:3 * P], Xc, ALU.add).then_inc(m.out_added, 1)

                if cur is not None:
                    nc.vector.memset(st[:, :, :], 0.0)
                    before(0)
                    before(1)
                if front is not None:
                    convolution(front)
                for c in range(NT):
                    if cur is not None:
                        n = behind(c)
                        if c + 2 < NT:
                            before(c + 2)
                    if back is not None and c + 1 < NT:
                        into_stream(c)
                if cur is not None:
                    dve.wait_ge(m.link, n)
                    dve.wait_ge(m.conv_in, cur * 3 + 3)
                    for c in range(NT):
                        last = nc.vector.bn_stats(stat[:, c, :], yz[par][:, c, :])
                    n = link(last)
                    dve.wait_ge(m.link, n)
                    nc.vector.tensor_tensor(w.mean2[:, :], stat[:, :, 1], stat[:, :, 4], ALU.add)
                    nc.vector.tensor_tensor(w.diff[:, :], stat[:, :, 1], stat[:, :, 4], ALU.subtract)
                    n = link(nc.vector.tensor_tensor(w.var2[:, :], stat[:, :, 2], stat[:, :, 5], ALU.add))
                    dve.wait_ge(m.link, n)
                    nc.vector.tensor_tensor(w.diff2[:, :], w.diff[:, :], w.diff[:, :], ALU.mult)
                    nc.vector.tensor_scalar(w.mean[:, :], w.mean2[:, :], 0.5, None, ALU.mult)
                    n = link(nc.vector.tensor_scalar(w.var[:, :], w.var2[:, :], 0.5 / HALF_IN, EPS, ALU.mult, ALU.add))
                    dve.wait_ge(m.link, n)
                    nc.vector.scalar_tensor_tensor(out=w.vareps[:, :], in0=w.diff2[:, :], scalar=0.25, in1=w.var[:, :],
                                                   op0=ALU.mult, op1=ALU.add).then_inc(m.var, 1)
                    if links[0] != CHUNK_LINKS:
                        raise ValueError(f"CHUNK_LINKS is {links[0]}")
                if back is not None:
                    into_stream(NT - 1)
                if front is not None:
                    silu(front, 1 - par)
                if cur is not None:
                    dve.wait_ge(m.rstd, cur + 1)
                    if not early(cur):
                        dve.wait_ge(m.yn_turned, cur * NT)
                    for c in range(NT):
                        nc.vector.tensor_scalar(yn[:, c, :], yz[par][:, c, :], w.mean[:, c:c + 1], w.rstd[:, c:c + 1],
                                                ALU.subtract, ALU.mult).then_inc(m.scaled, 1)

            run_steps(dve, body)


INPUTS = ("L0_attn_a_x", "L0_attn_a_Wqkv", "L0_attn_a_bqkv", "L0_attn_a_Wout", "L0_attn_a_bout",
          "L0_attn_a_rel_k_emb", "L0_attn_a_rel_v_emb", "L0_attn_a_alphas_raw", "L0_attn_b_W_in",
          "L0_attn_b_conv_w", "L0_attn_b_conv_b", "L0_attn_b_dt_bias", "L0_attn_b_A_log",
          "L0_attn_b_Dskip", "L0_attn_b_ln_w", "L0_attn_b_ln_b", "L0_attn_b_W_out", "L0_ffn_wg",
          "L0_ffn_W", "L0_ffn_b")


def norm(nc, s, ps, k, w, load=None):
    with nc.Block() as block:
        if load:
            block.sync(load)

        @block.vector
        def _(dve):
            norm_vector(nc, dve, s, w, k.X)

        @block.gpsimd
        def _(pool):
            norm_gpsimd(nc, pool, s, w)

        @block.tensor
        def _(pe):
            norm_tensor(nc, pe, s, w, ps[0:2], k.ident)

        @block.scalar
        def _(act):
            norm_scalar(nc, act, s, ps[0:2], k.XNT)

    s.before += 1


def store_stream(nc, sem, k, out):
    done = sem("stream_stored")
    with nc.Block() as block:
        @block.sync
        def _(sp):
            sp.dma_start(out.rearrange("b (t p) d -> p (b t) d", p=P),
                         k.X[:, :].rearrange("p (t d) -> p t d", d=D)).then_inc(done, 16)
            sp.wait_ge(done, 16)


def program(nc, a, out):
    with ExitStack() as outer:
        def sem(name):
            return outer.enter_context(nc.semaphore(name))

        def allocate(ctx):
            return lambda name, shape: ctx.enter_context(nc.sbuf_tensor(name, shape, F32))

        ps = [outer.enter_context(nc.psum_tensor(f"bank{q}", [P, 512], F32)) for q in range(8)]
        k = Namespace()
        keep = allocate(outer)
        k.X = keep("stream", [P, TILES * D])
        k.XNT = keep("stream_normed_t", [P, TILES * P])
        k.ident = keep("identity", [P, P])
        k.bout = keep("attention_out_bias", [P, D])
        k.zeros = keep("zeros", [P, 2 * P])
        w = norm_buffers(keep, "norm")
        norms = norm_sems(sem, "norm")
        r = Namespace()
        r.wg = keep("rest_wg", [P, E])
        r.eb = keep("rest_eb", [E, D])
        r.cwx = keep("rest_cwx", [P, CONV])
        r.cwb = keep("rest_cwb", [2 * SECOND, CONV])
        r.cbx = keep("rest_cbx", [P, 1])
        r.cbb = keep("rest_cbb", [2 * SECOND, 1])
        r.dtb = keep("rest_dtb", [P, MH])
        r.dskip = keep("rest_dskip", [P, MH])
        r.lnw = keep("rest_lnw", [P, 2])
        r.lnb = keep("rest_lnb", [P, 2])
        wr = rest_rows(keep)
        rest_loaded = sem("rest_loaded")

        def load(sp):
            load_rest(nc, sp, rest_loaded, a, wr, r)

        with ExitStack() as ctx:
            sb = allocate(ctx)
            t = Namespace()
            t.TJf = sb("table_j", [P, PAIRS * J_COLS])
            t.TOf = sb("table_o", [P, PAIRS * O_COLS])
            t.TJ = t.TJf[:, :].rearrange("p (r c) -> p r c", r=PAIRS)
            t.TO = t.TOf[:, :].rearrange("p (r c) -> p r c", r=PAIRS)
            t.XNT = k.XNT
            t.prob = [sb(f"probs_of_tile{T}", [P, 2, PADDED]) for T in range(NT)]
            t.kz = [[sb(f"keys{q}_of_head{h}", [P, N]) for h in range(2)] for q in range(2)]
            t.relk = sb("rel_keys", [P, 2, BAND])
            t.relv = sb("rel_values", [P, DH])
            t.r_dram = [nc.dram_tensor(f"rel_scratch{q}", [P * 2 * EXT], F32, kind="Internal") for q in range(2)]
            t.p_dram = [nc.dram_tensor(f"probs_scratch{q}", [P + P * 2 * PITCH], F32, kind="Internal")
                        for q in range(2)]
            with ExitStack() as ctx2:
                set_up(nc, sem, allocate(ctx2), ps, a, k, t, wr, r)
            norm(nc, norms, ps, k, w, load)
            attention(nc, sem, sb, ps, k, t)

        r.we = keep("rest_we", [P, E * D])
        r.before = keep("rest_before", [P, P])
        r.upto = keep("rest_upto", [P, P])
        r.after = keep("rest_after", [P, P])
        r.ones = keep("rest_ones", [P, P])
        r.rank = keep("rest_rank", [P, E])
        r.win = keep("rest_win", [P, 2 * P + 2 * SECOND])
        r.wdt = keep("rest_wdt", [P, MH])
        r.wo = keep("rest_wo", [P, 2, P])
        r.cbx2 = keep("rest_cbx2", [P, 1])
        r.cbb2 = keep("rest_cbb2", [2 * SECOND, 1])
        r.A = keep("rest_A", [P, MH])
        with ExitStack() as ctx:
            set_up_rest(nc, sem, allocate(ctx), ps, k, wr, r, rest_loaded)
        norm(nc, norms, ps, k, w)
        with ExitStack() as ctx:
            experts(nc, sem, allocate(ctx), ps, k, r, "experts1")
        norm(nc, norms, ps, k, w)
        with ExitStack() as ctx:
            mixer(nc, sem, allocate(ctx), ps, k, r)
        norm(nc, norms, ps, k, w)
        with ExitStack() as ctx:
            experts(nc, sem, allocate(ctx), ps, k, r, "experts2")
        store_stream(nc, sem, k, out)


def kernel(**inputs):
    import numpy as _np
    import concourse.bacc as _bacc
    from concourse import mybir as _mybir
    from concourse.bass_utils import run_bass_kernel_spmd as _run

    nc = _bacc.Bacc("TRN2", target_bir_lowering=False, num_devices=1)
    arrays, a = {}, {}
    for name in INPUTS:
        array = _np.ascontiguousarray(inputs[name])
        arrays[f"in_{name}"] = array
        short = name.replace("L0_attn_a_", "").replace("L0_attn_b_", "b_").replace("L0_ffn_", "f_")
        a[short] = nc.dram_tensor(f"in_{name}", array.shape, _mybir.dt.from_np(array.dtype), kind="ExternalInput").ap()
    out = nc.dram_tensor("out_stream", (B, N, D), F32, kind="ExternalOutput").ap()
    program(nc, a, out)
    r = _run(nc, [arrays], core_ids=[0])
    return r.results[0]["out_stream"]
```
